# Optimizing a Trainium2 kernel written in Bass

```python
import numpy as np
import jax
import jax.numpy as jnp

def _softmax(x, axis=-1):
    return jax.nn.softmax(x, axis=axis)

def _gelu(x):
    return jax.nn.gelu(x, approximate=True)

def _silu(x):
    return jax.nn.silu(x)

def _sigmoid(x):
    return jax.nn.sigmoid(x)

def _layernorm(x, axis=-1, eps=1e-05):
    m = jnp.mean(x, axis=axis, keepdims=True)
    v = jnp.var(x, axis=axis, keepdims=True)
    return (x - m) / jnp.sqrt(v + eps)

def _scatter_add(tgt, idx, src, axis=0):
    return tgt.at[idx].add(src)

def _segment_sum(src, seg, n):
    return jax.ops.segment_sum(src, seg, n)
kernel_name = 'mk_gnn_resnorm_d4_gnn_r32_e391ce'

def setup_inputs(seed: int=0):
    np.random.seed(seed)
    _w = jnp.asarray

    def _rec_inputs():
        import jax
        import jax.numpy as jnp
        _gk = jax.random.key(seed)
        x = -0.0002117 + 1 * jax.random.normal(jax.random.fold_in(_gk, 1), (3125, 256), jnp.float32)
        _s = jax.random.randint(jax.random.fold_in(_gk, 2), (25000,), 0, 3125, jnp.int32)
        _d = jax.random.randint(jax.random.fold_in(_gk, 3), (25000,), 0, 3125, jnp.int32)
        _loop = jnp.arange(3125, dtype=jnp.int32)
        src = jnp.concatenate([_s, _d, _loop])
        dst = jnp.concatenate([_d, _s, _loop])
        _o = jnp.argsort(dst, stable=True)
        src = src[_o]
        dst = dst[_o]
        edge_type_8 = jax.random.randint(jax.random.fold_in(_gk, 13), (53125,), 0, 8, jnp.int32)
        edge_weight = jax.random.uniform(jax.random.fold_in(_gk, 14), (53125,), jnp.float32, 0.0, 1)
        return (x, src, dst, edge_type_8, edge_weight)
    x, src, dst, edge_type_8, edge_weight = _rec_inputs()

    def _L0_gnn_setup():
        import jax, jax.numpy as jnp
        import numpy as np
        N = 3125
        E = 50000
        C_IN = 256
        H = 2
        D = 128
        ALPHA = 0.2
        key = jax.random.key(seed)
        ks = jax.random.split(key, 5)
        x = jax.random.normal(ks[0], (N, C_IN), dtype=jnp.float32)
        edge_index = jax.random.randint(ks[1], (2, E), 0, N, dtype=jnp.int64)
        W = jax.random.normal(ks[2], (H, D, C_IN), dtype=jnp.float32) * 0.05
        b = jax.random.normal(ks[3], (H, D), dtype=jnp.float32) * 0.05
        a = jax.random.normal(ks[4], (H, 2 * D), dtype=jnp.float32) * 0.05
        return {'x': x, 'edge_index': edge_index, 'W': W, 'b': b, 'a': a, 'n': N}
    _L0_gnn_all = _L0_gnn_setup()
    _L0_gnn_in = {k: v for k, v in _L0_gnn_all.items() if k in ('W', 'b', 'a')}
    del _L0_gnn_all

    def _L1_gnn_setup():
        import jax, jax.numpy as jnp
        import numpy as np
        N, E, D, H, C = (50000, 50000, 256, 8, 32)
        key = jax.random.key(seed)
        ks = jax.random.split(key, 7)
        feat = jax.random.normal(ks[0], (N, D), dtype=jnp.float32)
        edge_weight = jax.random.uniform(ks[1], (E,), dtype=jnp.float32)
        W_lin = jax.random.normal(ks[2], (D, H * C), dtype=jnp.float32) * (1.0 / np.sqrt(D))
        att_l = jax.random.normal(ks[3], (1, H, C), dtype=jnp.float32) * (1.0 / np.sqrt(H))
        att_r = jax.random.normal(ks[4], (1, H, C), dtype=jnp.float32) * (1.0 / np.sqrt(H))
        W_res = jax.random.normal(ks[5], (D, H * C), dtype=jnp.float32) * (1.0 / np.sqrt(D))
        edge_index = jax.random.randint(ks[6], (2, E), 0, N, dtype=jnp.int32)
        return {'feat': feat, 'edge_weight': edge_weight, 'W_lin': W_lin, 'att_l': att_l, 'att_r': att_r, 'W_res': W_res, 'edge_index': edge_index}
    _L1_gnn_all = _L1_gnn_setup()
    _L1_gnn_in = {k: v for k, v in _L1_gnn_all.items() if k in ('W_lin', 'att_l', 'att_r', 'W_res')}
    del _L1_gnn_all

    def _L2_gnn_setup():
        import jax, jax.numpy as jnp
        import numpy as np
        import math
        N = 1024
        E = N * 16
        D = 256
        H = 8
        DH = 32
        TD = H * DH
        FFN = 1024
        L = 2
        EPS = 1e-05

        def _layernorm(x, g, b):
            mu = jnp.mean(x, axis=-1, keepdims=True)
            var = jnp.mean(jnp.square(x - mu), axis=-1, keepdims=True)
            return (x - mu) * jax.lax.rsqrt(var + EPS) * g + b
        key = jax.random.key(seed)
        ks = jax.random.split(key, 16)
        w = lambda k, *s: jax.random.normal(k, s, dtype=jnp.float32) * 0.02
        return {'x': jax.random.normal(ks[0], (N, D), dtype=jnp.float32), 'edge_index': jax.random.randint(ks[1], (2, E), 0, N, dtype=jnp.int64).astype(jnp.int32), 'w_in': w(ks[2], D, D), 'b_in': jnp.zeros((D,), jnp.float32), 'ln1_g': jnp.ones((L, D), jnp.float32), 'ln1_b': jnp.zeros((L, D), jnp.float32), 'ln2_g': jnp.ones((L, D), jnp.float32), 'ln2_b': jnp.zeros((L, D), jnp.float32), 'wq': w(ks[3], L, D, TD), 'bq': jnp.zeros((L, TD), jnp.float32), 'wk': w(ks[4], L, D, TD), 'bk': jnp.zeros((L, TD), jnp.float32), 'wv': w(ks[5], L, D, TD), 'bv': jnp.zeros((L, TD), jnp.float32), 'wo': w(ks[6], L, TD, D), 'bo': jnp.zeros((L, D), jnp.float32), 'w1': w(ks[7], L, D, FFN), 'b1': jnp.zeros((L, FFN), jnp.float32), 'w2': w(ks[8], L, FFN, D), 'b2': jnp.zeros((L, D), jnp.float32)}
    _L2_gnn_all = _L2_gnn_setup()
    _L2_gnn_in = {k: v for k, v in _L2_gnn_all.items() if k in ('w_in', 'b_in', 'ln1_g', 'ln1_b', 'ln2_g', 'ln2_b', 'wq', 'bq', 'wk', 'bk', 'wv', 'bv', 'wo', 'bo', 'w1', 'b1', 'w2', 'b2')}
    del _L2_gnn_all

    def _L3_gnn_setup():
        import jax, jax.numpy as jnp
        import numpy as np
        N_NODES = 625
        N_EDGES = 10000
        NUM_RELS = 8
        DIM = 256
        BN_EPS = 1e-05
        key = jax.random.key(seed)
        k1, k2, k3, k4, k5 = jax.random.split(key, 5)
        h = jax.random.normal(k1, (N_NODES, DIM), dtype=jnp.float32)
        weight = jax.random.normal(k2, (NUM_RELS, DIM, DIM), dtype=jnp.float32) * 0.05
        gamma = jnp.ones((DIM,), dtype=jnp.float32)
        beta = jnp.zeros((DIM,), dtype=jnp.float32)
        src = jax.random.randint(k3, (N_EDGES,), 0, N_NODES, dtype=jnp.int32)
        dst = jax.random.randint(k4, (N_EDGES,), 0, N_NODES, dtype=jnp.int32)
        rel = jax.random.randint(k5, (N_EDGES,), 0, NUM_RELS, dtype=jnp.int32)
        return {'h': h, 'weight': weight, 'gamma': gamma, 'beta': beta, 'src': src, 'dst': dst, 'rel': rel}
    _L3_gnn_all = _L3_gnn_setup()
    _L3_gnn_in = {k: v for k, v in _L3_gnn_all.items() if k in ('weight', 'gamma', 'beta')}
    del _L3_gnn_all
    return {'x': x, 'src': src, 'dst': dst, 'edge_type_8': edge_type_8, 'edge_weight': edge_weight, 'L0_gnn_W': _L0_gnn_in['W'], 'L0_gnn_b': _L0_gnn_in['b'], 'L0_gnn_a': _L0_gnn_in['a'], 'L1_gnn_W_lin': _L1_gnn_in['W_lin'], 'L1_gnn_att_l': _L1_gnn_in['att_l'], 'L1_gnn_att_r': _L1_gnn_in['att_r'], 'L1_gnn_W_res': _L1_gnn_in['W_res'], 'L2_gnn_w_in': _L2_gnn_in['w_in'], 'L2_gnn_b_in': _L2_gnn_in['b_in'], 'L2_gnn_ln1_g': _L2_gnn_in['ln1_g'], 'L2_gnn_ln1_b': _L2_gnn_in['ln1_b'], 'L2_gnn_ln2_g': _L2_gnn_in['ln2_g'], 'L2_gnn_ln2_b': _L2_gnn_in['ln2_b'], 'L2_gnn_wq': _L2_gnn_in['wq'], 'L2_gnn_bq': _L2_gnn_in['bq'], 'L2_gnn_wk': _L2_gnn_in['wk'], 'L2_gnn_bk': _L2_gnn_in['bk'], 'L2_gnn_wv': _L2_gnn_in['wv'], 'L2_gnn_bv': _L2_gnn_in['bv'], 'L2_gnn_wo': _L2_gnn_in['wo'], 'L2_gnn_bo': _L2_gnn_in['bo'], 'L2_gnn_w1': _L2_gnn_in['w1'], 'L2_gnn_b1': _L2_gnn_in['b1'], 'L2_gnn_w2': _L2_gnn_in['w2'], 'L2_gnn_b2': _L2_gnn_in['b2'], 'L3_gnn_weight': _L3_gnn_in['weight'], 'L3_gnn_gamma': _L3_gnn_in['gamma'], 'L3_gnn_beta': _L3_gnn_in['beta']}

def reference(x, src, dst, edge_type_8, edge_weight, L0_gnn_W, L0_gnn_b, L0_gnn_a, L1_gnn_W_lin, L1_gnn_att_l, L1_gnn_att_r, L1_gnn_W_res, L2_gnn_w_in, L2_gnn_b_in, L2_gnn_ln1_g, L2_gnn_ln1_b, L2_gnn_ln2_g, L2_gnn_ln2_b, L2_gnn_wq, L2_gnn_bq, L2_gnn_wk, L2_gnn_bk, L2_gnn_wv, L2_gnn_bv, L2_gnn_wo, L2_gnn_bo, L2_gnn_w1, L2_gnn_b1, L2_gnn_w2, L2_gnn_b2, L3_gnn_weight, L3_gnn_gamma, L3_gnn_beta):
    import jax
    import jax.numpy as jnp

    def _L0_gnn_ref(x, edge_index, W, b, a, n):
        import jax, jax.numpy as jnp
        import numpy as np
        N = 3125
        E = 50000
        C_IN = 256
        H = 2
        D = 128
        ALPHA = 0.2
        src = edge_index[0]
        dst = edge_index[1]

        def head(Wh, bh, ah):
            h = x @ Wh.T + bh
            s_src = h @ ah[:D]
            s_dst = h @ ah[D:]
            score = s_src[src] + s_dst[dst]
            lrelu = jnp.where(score > 0, score, ALPHA * score)
            e = jnp.exp(-lrelu)
            row_sum = jax.ops.segment_sum(e, src, num_segments=n)
            num = jax.ops.segment_sum(e[:, None] * h[dst], src, num_segments=n)
            h_prime = num / row_sum[:, None]
            return jax.nn.elu(h_prime)
        outs = jax.vmap(head)(W, b, a)
        return jnp.moveaxis(outs, 0, 1).reshape(x.shape[0], H * D)

    def _L1_gnn_ref(feat, edge_weight, W_lin, att_l, att_r, W_res, edge_index):
        import jax, jax.numpy as jnp
        import numpy as np
        N, E, D, H, C = (50000, 50000, 256, 8, 32)
        n_nodes = feat.shape[0]
        h, c = (att_l.shape[1], att_l.shape[2])
        src, dst = (edge_index[0], edge_index[1])
        x = (feat @ W_lin).reshape(n_nodes, h, c)
        alpha_l = (x * att_l).sum(-1)
        alpha_r = (x * att_r).sum(-1)
        alpha = alpha_l[src] + alpha_r[dst]
        alpha = edge_weight[:, None] * alpha
        alpha = jnp.where(alpha > 0, alpha, 0.2 * alpha)
        amax = jax.lax.stop_gradient(jax.ops.segment_max(alpha, dst, num_segments=n_nodes))
        ex = jnp.exp(alpha - amax[dst])
        denom = jax.ops.segment_sum(ex, dst, num_segments=n_nodes)
        coeff = ex / (denom[dst] + 1e-16)
        msg = x[src] * coeff[:, :, None]
        agg = jax.ops.segment_sum(msg, dst, num_segments=n_nodes)
        out = jax.nn.elu(agg).reshape(n_nodes, h * c)
        out = out + feat @ W_res
        return out

    def _L2_gnn_ref(x, edge_index, w_in, b_in, ln1_g, ln1_b, ln2_g, ln2_b, wq, bq, wk, bk, wv, bv, wo, bo, w1, b1, w2, b2):
        import jax, jax.numpy as jnp
        import numpy as np
        import math
        N = 1024
        E = N * 16
        D = 256
        H = 8
        DH = 32
        TD = H * DH
        FFN = 1024
        L = 2
        EPS = 1e-05

        def _layernorm(x, g, b):
            mu = jnp.mean(x, axis=-1, keepdims=True)
            var = jnp.mean(jnp.square(x - mu), axis=-1, keepdims=True)
            return (x - mu) * jax.lax.rsqrt(var + EPS) * g + b
        n = x.shape[0]
        src0, dst0 = (edge_index[0], edge_index[1])
        deg = jax.ops.segment_sum(jnp.ones_like(src0, jnp.float32), dst0, num_segments=n)
        ar = jnp.arange(n, dtype=src0.dtype)
        src = jnp.concatenate([src0, ar])
        dst = jnp.concatenate([dst0, ar])
        h = x @ w_in + b_in
        scale = 1.0 / math.sqrt(DH)
        for l in range(L):
            xn = _layernorm(h, ln1_g[l], ln1_b[l])
            q = (xn @ wq[l] + bq[l]).reshape(n, H, DH)
            k = (xn @ wk[l] + bk[l]).reshape(n, H, DH)
            v = (xn @ wv[l] + bv[l]).reshape(n, H, DH)
            scores = jnp.einsum('ehd,ehd->eh', q[dst], k[src]) * scale
            m = jax.ops.segment_max(scores, dst, num_segments=n)
            ex = jnp.exp(scores - m[dst])
            z = jax.ops.segment_sum(ex, dst, num_segments=n)
            attn = ex / z[dst]
            agg = jax.ops.segment_sum(attn[:, :, None] * v[src], dst, num_segments=n)
            agg = jnp.where((deg > 0)[:, None, None], agg, 0.0)
            h = h + agg.reshape(n, TD) @ wo[l] + bo[l] * jnp.where(deg > 0, 1.0, 1.0)[:, None] * 0 + agg.reshape(n, TD) @ wo[l] * 0
            h = h - agg.reshape(n, TD) @ wo[l]
            h = h + (agg.reshape(n, TD) @ wo[l] + bo[l]) - bo[l] * 0
            xn2 = _layernorm(h, ln2_g[l], ln2_b[l])
            ffn = jax.nn.gelu(xn2 @ w1[l] + b1[l], approximate=False) @ w2[l] + b2[l]
            h = h + ffn
        return h

    def _L3_gnn_ref(h, weight, gamma, beta, src, dst, rel):
        import jax, jax.numpy as jnp
        import numpy as np
        N_NODES = 625
        N_EDGES = 10000
        NUM_RELS = 8
        DIM = 256
        BN_EPS = 1e-05
        all_h = jnp.einsum('ni,rio->nro', h, weight)
        msg = all_h[src, rel]
        agg = jax.ops.segment_sum(msg, dst, num_segments=h.shape[0])
        mean = jnp.mean(agg, axis=0)
        var = jnp.mean(jnp.square(agg - mean), axis=0)
        out = (agg - mean) * jax.lax.rsqrt(var + BN_EPS) * gamma + beta
        return out
    edge_index = jnp.stack([src, dst])
    x = _layernorm(x + _L0_gnn_ref(x, edge_index, L0_gnn_W, L0_gnn_b, L0_gnn_a, 3125), axis=-1)
    x = _layernorm(x + _L1_gnn_ref(x, edge_weight, L1_gnn_W_lin, L1_gnn_att_l, L1_gnn_att_r, L1_gnn_W_res, edge_index), axis=-1)
    x = _layernorm(x + _L2_gnn_ref(x, edge_index, L2_gnn_w_in, L2_gnn_b_in, L2_gnn_ln1_g, L2_gnn_ln1_b, L2_gnn_ln2_g, L2_gnn_ln2_b, L2_gnn_wq, L2_gnn_bq, L2_gnn_wk, L2_gnn_bk, L2_gnn_wv, L2_gnn_bv, L2_gnn_wo, L2_gnn_bo, L2_gnn_w1, L2_gnn_b1, L2_gnn_w2, L2_gnn_b2), axis=-1)
    x = _layernorm(x + _L3_gnn_ref(x, L3_gnn_weight, L3_gnn_gamma, L3_gnn_beta, src, dst, edge_type_8), axis=-1)
    return x

_drawn_inputs = setup_inputs


def setup_inputs(seed=0):
    import zlib

    import numpy as np

    out = dict(_drawn_inputs(seed))
    spreads = {'L2_gnn_b_in': (0.0, 0.1),
     'L2_gnn_ln1_g': (1.0, 0.6),
     'L2_gnn_ln1_b': (0.0, 0.601),
     'L2_gnn_ln2_g': (1.0, 0.2),
     'L2_gnn_ln2_b': (0.0, 0.493),
     'L2_gnn_bq': (0.0, 0.8),
     'L2_gnn_bk': (0.0, 0.8),
     'L2_gnn_bv': (0.0, 0.1),
     'L2_gnn_bo': (0.0, 0.1),
     'L2_gnn_b1': (0.0, 0.1),
     'L2_gnn_b2': (0.0, 0.1),
     'L3_gnn_gamma': (1.0, 0.2),
     'L3_gnn_beta': (0.0, 0.1)}
    factors = {'L2_gnn_wq': 8.0, 'L2_gnn_wk': 8.0}
    for name, (base, spread) in spreads.items():
        noise = np.random.default_rng([zlib.crc32(name.encode()), seed]).standard_normal(out[name].shape)
        drawn = base * np.exp(spread * noise) if base else spread * noise
        out[name] = jnp.asarray(drawn.astype(out[name].dtype))
    for name, factor in factors.items():
        out[name] = (out[name] * factor).astype(out[name].dtype)
    return out
```

```python
from contextlib import ExitStack

import concourse.bass as bass
from concourse import mybir

fp32, bf16, i32 = mybir.dt.float32, mybir.dt.bfloat16, mybir.dt.int32
ALU = mybir.AluOpType
ACT = mybir.ActivationFunctionType
AX = mybir.AxisListType

P = 128
N = 3125
E = 53125
C = 256
NT = -(-N // P)
NL = N - (NT - 1) * P
NP = NT * P
EP = 125
ET = E // EP
U = 4
NB = 4
ST = 448
SR = ST // (U * NB)
assert (E + NT * (P - 1)) // P <= ST and ET * EP == E and SR * U * NB == ST
STP = ST + U
NOKEY = 4095
BIG = 1e38
EPS = 1e-5
HIST = 17
LOOK = 5
SLOTS = 5
ROUNDS = NT // SLOTS


def after(eng, sem, value):
    if isinstance(value, int) and value <= 0:
        return
    eng.wait_ge(sem, value)


def rounds(eng, n, body):
    body(0)
    with eng.Fori(1, n) as i:
        body(i)


class Chain:

    def __init__(self, eng, sem, base=0):
        self.eng, self.sem, self.n = eng, sem, base

    def __call__(self, ins):
        self.n = self.n + 1
        ins.then_inc(self.sem, 1)
        self.eng.wait_ge(self.sem, self.n)


class Phase:
    used = []

    def __init__(self, nc, tag):
        self.nc, self.tag, self.ctx, self.sems = nc, tag, ExitStack(), []

    def __enter__(self):
        self.ctx.__enter__()
        return self

    def __exit__(self, *a):
        done = self.ctx.__exit__(*a)
        Phase.used += self.sems
        if len(Phase.used) > 120:
            Phase.clear(self.nc)
        return done

    @staticmethod
    def clear(nc):
        nc.clear_and_free_semaphores(Phase.used)
        nc.all_engine_barrier()
        Phase.used = []

    def sb(self, name, shape, dt=fp32):
        return self.ctx.enter_context(self.nc.sbuf_tensor(f"{self.tag}_{name}", shape, dt))

    def ps(self, name, shape, dt=fp32):
        return self.ctx.enter_context(self.nc.psum_tensor(f"{self.tag}_{name}", shape, dt))

    def sem(self, name):
        self.sems.append(self.nc.alloc_semaphore(f"{self.tag}_{name}"))
        return self.sems[-1]

    def block(self):
        return self.ctx.enter_context(self.nc.Block())


class Constants:
    pass


def make_constants(nc, hold):
    k = Constants()
    k.ident = hold.sb("ident", [P, P])
    k.ramp = hold.sb("ramp", [P, P])
    k.ramp_b = hold.sb("ramp_b", [P, P], bf16)
    k.row = hold.sb("row", [P, 1])
    k.ones = hold.sb("ones", [P, P])
    k.before = hold.sb("before", [P, P])
    k.above = hold.sb("above", [P, P])
    k.upto = hold.sb("upto", [P, P])
    k.slots = hold.sb("slots", [P, ST])
    k.spread = hold.sb("spread", [8, 16, P])
    with Phase(nc, "const") as ph:
        diff = ph.sb("diff", [P, P], i32)
        ramp_i = ph.sb("ramp_i", [P, ST], i32)
        row_i = ph.sb("row_i", [P, 1], i32)
        spread_i = ph.sb("spread_i", [8, 16, P], i32)
        made = ph.sem("made")
        block = ph.block()

        @block.gpsimd
        def _(pool):
            nc.gpsimd.iota(diff[:, :], pattern=[[1, P]], base=0, channel_multiplier=-1)
            nc.gpsimd.iota(ramp_i[:, :], pattern=[[1, ST]], base=0, channel_multiplier=0)
            nc.gpsimd.iota(row_i[:, :], pattern=[[1, 1]], base=0, channel_multiplier=1)
            nc.gpsimd.iota(spread_i[:, :, :], pattern=[[-8, 16], [1, P]], base=0,
                           channel_multiplier=-1).then_inc(made, 1)
            nc.gpsimd.memset(k.ones[:, :], 1.0)

        @block.vector
        def _(dve):
            dve.wait_ge(made, 1)
            nc.vector.tensor_scalar(k.ident[:, :], diff[:, :], 0.0, None, ALU.is_equal)
            nc.vector.tensor_scalar(k.above[:, :], diff[:, :], 0.0, None, ALU.is_gt)
            nc.vector.tensor_scalar(k.upto[:, :], diff[:, :], 0.0, None, ALU.is_ge)
            nc.vector.tensor_scalar(k.before[:, :], diff[:, :], 0.0, None, ALU.is_lt)
            nc.vector.tensor_copy(k.ramp[:, :], ramp_i[:, 0:P])
            nc.vector.tensor_copy(k.ramp_b[:, :], ramp_i[:, 0:P])
            nc.vector.tensor_copy(k.slots[:, :], ramp_i[:, :])
            nc.vector.tensor_copy(k.row[:, :], row_i[:, :])
            nc.vector.tensor_scalar(k.spread[:, :, :], spread_i[:, :, :], 0.0, None, ALU.is_equal)
    return k


def sort_edges(nc, k, tag, key, other, etype, weight, table, tile_of, tile_row):
    arrays = [key, other] + ([etype, weight] if weight is not None else [])
    with ExitStack() as outer:
        def keep(name, shape, dt=fp32):
            return outer.enter_context(nc.sbuf_tensor(f"{tag}_{name}", shape, dt))

        stage_all = keep("stage_all", [EP, ET + LOOK, 5], i32)
        key_c = keep("key_c", [EP, ET])
        count = keep("count", [P, ET + 1, NT])
        hi_hot = keep("hi_hot", [EP, ET, NT], bf16)

        with Phase(nc, tag + "_in") as ph:
            rows = [ph.sb(f"rows{n}", [P, 4, EP], i32) for n in range(len(arrays))]
            rows_f = [ph.sb(f"rows_f{n}", [P, 4, EP]) for n in range(len(arrays))]
            cols = [key_c] + [ph.sb(f"cols{n}", [EP, ET]) for n in range(1, len(arrays))]
            key_i = ph.sb("key_i", [EP, ET], i32)
            part_i = ph.sb("part_i", [EP, ET], i32)
            part_f = ph.sb("part_f", [EP, ET], bf16)
            relation = ph.sb("relation", [EP, ET])
            empty = ph.sb("empty", [P, ST, 4], i32)
            turned = [ph.ps(f"turned{n}", [EP, 512]) for n in range(len(arrays))]
            loaded, cast, turn, own, blank, wiped = (
                ph.sem(n) for n in ("loaded", "cast", "turn", "own", "blank", "wiped"))
            block = ph.block()
            full = ET // P * P

            @block.sync
            def _(sp):
                for n, a in enumerate(arrays):
                    src = a if a.dtype != fp32 else a.bitcast(i32)
                    sp.dma_start(rows[n][:, 0:3, :],
                                 src[0:full * EP].rearrange("(b p e) -> p b e", p=P, e=EP)).then_inc(loaded, 16)
                    sp.dma_start(rows[n][0:ET - full, 3, :],
                                 src[full * EP:E].rearrange("(p e) -> p e", e=EP)).then_inc(loaded, 16)
                sp.wait_ge(blank, 3)
                sp.dma_start(table.rearrange("(p t) w -> p t w", p=P), empty[:, :, :]).then_inc(wiped, 16)
                sp.wait_ge(wiped, 16)

            @block.gpsimd
            def _(pool):
                nc.gpsimd.memset(empty[:, :, :], 0).then_inc(blank, 1)
                pool.wait_ge(blank, 1)
                nc.gpsimd.memset(empty[:, :, 2:3], NOKEY).then_inc(blank, 2)

            @block.vector
            def _(dve):
                dve.wait_ge(loaded, 32 * len(arrays))
                for n in range(len(arrays)):
                    for r, m in ((slice(0, 3), P), (slice(3, 4), ET - full)):
                        out, src = rows_f[n][0:m, r, :], rows[n][0:m, r, :]
                        if n == 3:
                            src = src.bitcast(fp32)
                        ins = nc.vector.tensor_copy(out, src)
                        ins.then_inc(cast, 1)
                step = Chain(dve, own)
                for n in range(len(arrays)):
                    dve.wait_ge(turn, n + 1)
                    step(nc.vector.tensor_copy(cols[n][:, :], turned[n][:, 0:ET]))
                step(nc.vector.tensor_copy(key_i[:, :], key_c[:, :]))
                step(nc.vector.tensor_scalar(part_i[:, :], key_i[:, :], 7, None, ALU.arith_shift_right))
                step(nc.vector.tensor_copy(part_f[:, :], part_i[:, :]))
                nc.vector.tensor_tensor(hi_hot[:, :, :], part_f[:, :].unsqueeze(2).to_broadcast([EP, ET, NT]),
                                        k.ramp_b[0:EP, 0:NT].unsqueeze(1).to_broadcast([EP, ET, NT]), ALU.is_equal)
                step(nc.vector.memset(stage_all[:, :, :], 0))
                nc.vector.tensor_copy(stage_all[:, 0:ET, 1], cols[1][:, :])
                nc.vector.tensor_copy(stage_all[:, 0:ET, 3], key_c[:, :])
                if weight is not None:
                    step(nc.vector.scalar_tensor_tensor(relation[:, :], cols[1][:, :], 8.0, cols[2][:, :],
                                                        ALU.mult, ALU.add))
                    nc.vector.tensor_copy(stage_all[:, 0:ET, 2], relation[:, :])
                    nc.vector.tensor_copy(stage_all[:, 0:ET, 4].bitcast(fp32), cols[3][:, :])

            @block.tensor
            def _(pe):
                for n in range(len(arrays)):
                    pe.wait_ge(cast, 2 * n + 2)
                    for b in range(4):
                        m = min(P, ET - b * P)
                        last = nc.tensor.transpose(turned[n][:, b * P:b * P + m], rows_f[n][0:m, b, :],
                                                   k.ident[0:m, 0:m])
                    last.then_inc(turn, 1)

        with Phase(nc, tag + "_hist") as ph:
            lo_hot = [ph.sb(f"lo_hot{u}", [EP, HIST, P], bf16) for u in range(SLOTS)]
            key_i = ph.sb("key_i", [EP, ET], i32)
            low_i = ph.sb("low_i", [EP, ET], i32)
            low = ph.sb("low", [EP, ET], bf16)
            sums = [ph.ps(f"sums{u}", [P, 512]) for u in range(SLOTS)]
            own, hot, summed, counted = (ph.sem(n) for n in ("own", "hot", "summed", "counted"))
            block = ph.block()
            assert ET // HIST == NT

            @block.vector
            def _(dve):
                step = Chain(dve, own)
                step(nc.vector.tensor_copy(key_i[:, :], key_c[:, :]))
                step(nc.vector.tensor_scalar(low_i[:, :], key_i[:, :], P - 1, None, ALU.bitwise_and))
                step(nc.vector.tensor_copy(low[:, :], low_i[:, :]))
                nc.vector.memset(count[:, 0:1, :], 0.0).then_inc(counted, 1)

                def accumulate(g, u):
                    dve.wait_ge(summed, g + 1)
                    dve.wait_ge(counted, g + 1)
                    nc.vector.tensor_tensor(
                        count[:, bass.ds(g * HIST + 1, HIST), :],
                        sums[u][:, 0:HIST * NT].rearrange("p (t h) -> p t h", h=NT),
                        count[:, bass.ds(g * HIST, 1), :].to_broadcast([P, HIST, NT]), ALU.add).then_inc(counted, 1)

                def body(i):
                    for u in range(SLOTS):
                        g = i * SLOTS + u
                        after(dve, summed, g - SLOTS + 1)
                        nc.vector.tensor_tensor(
                            lo_hot[u][:, :, :], low[:, bass.ds(g * HIST, HIST)].unsqueeze(2).to_broadcast([EP, HIST, P]),
                            k.ramp_b[0:EP, :].unsqueeze(1).to_broadcast([EP, HIST, P]), ALU.is_equal).then_inc(hot, 1)
                        if not (isinstance(g, int) and g == 0):
                            accumulate(g - 1, (u - 1) % SLOTS)

                rounds(dve, ET // HIST // SLOTS, body)
                accumulate(ET // HIST - 1, SLOTS - 1)

            @block.tensor
            def _(pe):
                def body(i):
                    for u in range(SLOTS):
                        g = i * SLOTS + u
                        pe.wait_ge(hot, g + 1)
                        after(pe, counted, g - SLOTS + 2)
                        for j in range(HIST):
                            n = HIST - j
                            last = nc.tensor.matmul(
                                sums[u][:, j * NT:HIST * NT].rearrange("p (t h) -> p t h", h=NT), lo_hot[u][:, j, :],
                                hi_hot[:, bass.ds(g * HIST + j, 1), :].to_broadcast([EP, n, NT]),
                                start=(j == 0), stop=(j == HIST - 1))
                        last.then_inc(summed, 1)

                rounds(pe, ET // HIST // SLOTS, body)

        with Phase(nc, tag + "_base") as ph:
            base = ph.sb("base", [P, NT])
            tiles_i = ph.sb("tiles_i", [P, NT], i32)
            tiles = ph.sb("tiles", [P, NT])
            ends = ph.sb("ends", [P, NT])
            col_i = ph.sb("col_i", [NT, 1], i32)
            col = ph.sb("col", [NT, 1])
            end_c = ph.sb("end_c", [NT, 1])
            past = ph.sb("past", [NT, ST])
            lows = ph.ps("lows", [P, 512])
            totals = ph.ps("totals", [P, 512])
            total_c = ph.ps("total_c", [NT, 512])
            end_p = ph.ps("end_p", [NT, 512])
            which = ph.ps("which", [P, 512])
            own, made, summed = (ph.sem(n) for n in ("own", "made", "summed"))
            block = ph.block()
            final = count[:, ET, :]

            @block.tensor
            def _(pe):
                nc.tensor.matmul(lows[:, 0:NT], k.above[:, :], final, start=True, stop=True)
                nc.tensor.matmul(totals[:, 0:NT], k.ones[:, :], final, start=True, stop=True)
                nc.tensor.matmul(total_c[:, 0:1], final, k.ones[:, 0:1], start=True, stop=True).then_inc(summed, 1)
                pe.wait_ge(made, 1)
                nc.tensor.matmul(end_p[:, 0:1], k.upto[0:NT, 0:NT], col[:, :], start=True, stop=True).then_inc(summed, 1)
                pe.wait_ge(made, 2)
                nc.tensor.matmul(which[:, 0:ST], k.ones[0:NT, :], past[:, :], start=True, stop=True).then_inc(summed, 1)

            @block.vector
            def _(dve):
                step = Chain(dve, own)
                dve.wait_ge(summed, 1)
                for total, whole, out in ((total_c[:, 0:1], col_i[:, :], col[:, :]),
                                          (totals[:, 0:NT], tiles_i[:, :], tiles[:, :])):
                    step(nc.vector.tensor_scalar(whole, total, float(P - 1), None, ALU.add))
                    step(nc.vector.tensor_scalar(whole, whole, 7, None, ALU.arith_shift_right))
                    step(nc.vector.tensor_copy(out, whole))
                nc.vector.memset(base[:, :], 0.0).then_inc(made, 1)
                step(nc.vector.tensor_tensor_scan(ends[:, :], k.ones[:, 0:NT], tiles[:, :], 0.0, ALU.mult, ALU.add))
                dve.wait_ge(summed, 2)
                step(nc.vector.tensor_copy(end_c[:, :], end_p[:, 0:1]))
                nc.vector.tensor_scalar(past[:, :], k.slots[0:NT, :], end_c[:, 0:1], None, ALU.is_ge).then_inc(made, 1)
                step(nc.vector.tensor_tensor(base[:, :], ends[:, :], tiles[:, :], ALU.subtract))
                step(nc.vector.scalar_tensor_tensor(base[:, :], base[:, :], float(P), lows[:, 0:NT], ALU.mult, ALU.add))
                nc.vector.tensor_tensor(count[:, 0:ET, :], count[:, 0:ET, :],
                                        base[:, :].unsqueeze(1).to_broadcast([P, ET, NT]), ALU.add)
                step(nc.vector.memset(tile_row[:, :], NT - 1))
                step(nc.vector.memset(tile_of[:, :], float(NT - 1)))
                dve.wait_ge(summed, 3)
                step(nc.vector.tensor_scalar(tile_of[:, 0:ST], which[:, 0:ST], float(NT - 1), None, ALU.min))
                nc.vector.tensor_copy(tile_row[:, 0:ST], tile_of[0:1, 0:ST])

        with Phase(nc, tag + "_rank") as ph:
            W = LOOK * EP
            keys = [ph.sb(f"keys{u}", [P, W], i32) for u in range(SLOTS)]
            low_i = [ph.sb(f"low_i{u}", [P, W], i32) for u in range(2)]
            low_hot = [ph.sb(f"low_hot{u}", [P, W]) for u in range(SLOTS)]
            same = ph.sb("same", [EP, LOOK, EP])
            picked = ph.sb("picked", [EP, LOOK, NT])
            rank = ph.sb("rank", [EP, ET])
            slot = ph.sb("slot", [EP, ET])
            slot_i = ph.sb("slot_i", [EP, ET], i32)
            in_tile = ph.sb("in_tile", [EP, ET], i32)
            found = [ph.ps(f"found{u}", [EP, 512]) for u in range(SLOTS)]
            loaded = [ph.sem(f"loaded{u}") for u in range(SLOTS)]
            masked, hot, looked, ranked, took, got, own = (
                ph.sem(n) for n in ("masked", "hot", "looked", "ranked", "took", "got", "own"))
            block = ph.block()
            groups = ET // LOOK

            @block.sync
            def _(sp):
                def body(i):
                    for u in range(SLOTS):
                        g = i * SLOTS + u
                        after(sp, ranked, g - SLOTS + 1)
                        sp.dma_start(keys[u][:, :], key[bass.ds(g * W, W)].partition_broadcast(P)).then_inc(loaded[u], 16)

                rounds(sp, groups // SLOTS, body)

            @block.vector
            def _(dve):
                def take(g, u):
                    dve.wait_ge(looked, g + 1)
                    after(dve, got, g)
                    nc.vector.tensor_tensor(
                        picked[:, :, :], found[u][:, 0:LOOK * NT].rearrange("p (t h) -> p t h", h=NT),
                        hi_hot[:, bass.ds(g * LOOK, LOOK), :], ALU.mult).then_inc(took, 1)
                    dve.wait_ge(took, g + 1)
                    nc.vector.tensor_reduce(slot[:, bass.ds(g * LOOK, LOOK)], picked[:, :, :], AX.X,
                                            ALU.add).then_inc(got, 1)

                def body(i):
                    for u in range(SLOTS):
                        g = i * SLOTS + u
                        dve.wait_ge(loaded[u], i * 16 + 16)
                        after(dve, hot, g - 1)
                        nc.vector.tensor_scalar(low_i[u % 2][:, :], keys[u][:, :], P - 1, None,
                                                ALU.bitwise_and).then_inc(masked, 1)
                        dve.wait_ge(masked, g + 1)
                        after(dve, looked, g - SLOTS + 1)
                        nc.vector.tensor_scalar(low_hot[u][:, :], low_i[u % 2][:, :], k.row[:, 0:1], None,
                                                ALU.is_equal).then_inc(hot, 1)
                        after(dve, ranked, g)
                        for j in range(LOOK):
                            t = g * LOOK + j
                            last = nc.vector.scalar_tensor_tensor(
                                same[:, j, :], keys[u][0:EP, j * EP:(j + 1) * EP], key_c[:, bass.ds(t, 1)],
                                k.before[0:EP, 0:EP], ALU.is_equal, ALU.mult, accum_out=rank[:, bass.ds(t, 1)])
                        last.then_inc(ranked, 1)
                        if not (isinstance(g, int) and g == 0):
                            take(g - 1, (u - 1) % SLOTS)

                rounds(dve, groups // SLOTS, body)
                take(groups - 1, SLOTS - 1)
                step = Chain(dve, own)
                dve.wait_ge(got, groups)
                dve.wait_ge(ranked, groups)
                step(nc.vector.tensor_tensor(slot[:, :], slot[:, :], rank[:, :], ALU.add))
                step(nc.vector.tensor_copy(slot_i[:, :], slot[:, :]))
                step(nc.vector.tensor_scalar(in_tile[:, :], slot_i[:, :], P - 1, None, ALU.bitwise_and))
                step(nc.vector.tensor_scalar(slot_i[:, :], slot_i[:, :], 7, None, ALU.arith_shift_right))
                nc.vector.scalar_tensor_tensor(stage_all[:, 0:ET, 0], in_tile[:, :], float(ST), slot_i[:, :],
                                               ALU.mult, ALU.add)

            @block.tensor
            def _(pe):
                def body(i):
                    for u in range(SLOTS):
                        g = i * SLOTS + u
                        pe.wait_ge(hot, g + 1)
                        after(pe, took, g - SLOTS + 1)
                        for j in range(LOOK):
                            last = nc.tensor.matmul(found[u][:, j * NT:(j + 1) * NT], low_hot[u][:, j * EP:(j + 1) * EP],
                                                    count[:, bass.ds(g * LOOK + j, 1), :].rearrange("p t h -> p (t h)"),
                                                    start=True, stop=True)
                        last.then_inc(looked, 1)

                rounds(pe, groups // SLOTS, body)

        with Phase(nc, tag + "_put") as ph:
            stage = ph.sb("stage", [EP, SLOTS, LOOK, 5], i32)
            staged = ph.sem("staged")
            put = [ph.sem(f"put{u}") for u in range(SLOTS)]
            block = ph.block()
            groups = ET // LOOK

            @block.gpsimd
            def _(pool):
                nc.gpsimd.tensor_copy(stage[:, 0, :, :], stage_all[:, 0:LOOK, :]).then_inc(staged, 1)

                def body(i):
                    for u in range(SLOTS):
                        g, v = i * SLOTS + u, (u + 1) % SLOTS
                        after(pool, put[v], (i + (1 if v == 0 else 0)) * 16 * LOOK)
                        pool.wait_ge(staged, g + 1)
                        nc.gpsimd.tensor_copy(stage[:, v, :, :],
                                              stage_all[:, bass.ds((g + 1) * LOOK, LOOK), :]).then_inc(staged, 1)
                        for j in range(LOOK):
                            pool.indirect_dma_start(
                                out=table[:, :], out_offset=bass.IndirectOffsetOnAxis(ap=stage[:, u, j, 0:1], axis=0),
                                in_=stage[:, u, j, 1:5], in_offset=None).then_inc(put[u], 16)

                rounds(pool, groups // SLOTS, body)
                for u in range(SLOTS):
                    pool.wait_ge(put[u], groups // SLOTS * 16 * LOOK)



def load_order(nc, k, tag, table, tile_of, index, local, more=None):
    with Phase(nc, tag) as ph:
        raw = ph.sb("raw", [P, ST, 4], i32)
        key_f = ph.sb("key_f", [P, ST])
        loaded, own = ph.sem("loaded"), ph.sem("own")
        rows = table.rearrange("(p t) w -> p t w", p=P)
        if more is not None:
            edges, edge_f = [ph.sb(f"edge{n}", [P, ST, 4], i32) for n in range(2)], [ph.sb(f"edge_f{n}", [P, ST]) for n in range(2)]
            wide = [ph.sb(f"wide{n}", [P, ST, 8]) for n in range(2)]
            turned = [ph.ps(f"turned{n}", [P, 512]) for n in range(6)]
            has = [ph.ps(f"has{n}", [8, 512]) for n in range(2)]
            cleared, marked, turn, moved = (ph.sem(n) for n in ("cleared", "marked", "turn", "moved"))
        block = ph.block()

        @block.sync
        def _(sp):
            sp.dma_start(raw[:, :, :], rows).then_inc(loaded, 16)
            if more is not None:
                sp.wait_ge(cleared, 2)
                sp.dma_start(edges[0][1:P, :, :], rows[0:P - 1]).then_inc(loaded, 16)
                sp.dma_start(edges[0][0:1, 1:ST, :], rows[P - 1:P, 0:ST - 1]).then_inc(loaded, 16)
                sp.dma_start(edges[1][0:P - 1, :, :], rows[1:P]).then_inc(loaded, 16)
                sp.dma_start(edges[1][P - 1:P, 0:ST - 1, :], rows[0:1, 1:ST]).then_inc(loaded, 16)

        @block.vector
        def _(dve):
            step = Chain(dve, own)
            if more is not None:
                for n in range(2):
                    nc.vector.memset(edges[n][:, :, :], -1).then_inc(cleared, 1)
            step(nc.vector.memset(index[0][:, :], 0))
            if more is not None:
                step(nc.vector.memset(index[1][:, :], 0))
            step(nc.vector.memset(local[:, :], float(NOKEY)))
            dve.wait_ge(loaded, 80 if more is not None else 16)
            nc.vector.tensor_copy(index[0][:, 0:ST], raw[:, :, 0])
            step(nc.vector.tensor_copy(key_f[:, :], raw[:, :, 2]))
            nc.vector.scalar_tensor_tensor(local[:, 0:ST], tile_of[:, 0:ST], -float(P), key_f[:, :], ALU.mult, ALU.add)
            if more is None:
                return
            nc.vector.tensor_copy(index[1][:, 0:ST], raw[:, :, 1])
            nc.vector.tensor_copy(more.weight[:, :], raw[:, :, 3].bitcast(fp32))
            last_mark = ph.sb("last_mark", [P, ST])
            for n, mark in enumerate((more.first, last_mark)):
                step(nc.vector.tensor_copy(edge_f[n][:, :], edges[n][:, :, 2]))
                step(nc.vector.tensor_tensor(mark[:, :], key_f[:, :], edge_f[n][:, :], ALU.not_equal))
                nc.vector.tensor_copy(wide[n][:, :, :], mark[:, :].unsqueeze(2).to_broadcast([P, ST, 8])).then_inc(marked, 1)
            more.last_mark = last_mark
            for n, (neg, edge) in enumerate(((more.not_first, 0), (more.not_last, P - 1))):
                for g in range(7):
                    dve.wait_ge(turn, 7 * n + g + 1)
                    nc.vector.tensor_scalar(neg[:, 4 * g:4 * g + 4, :],
                                            turned[(7 * n + g) % 6][:, :].rearrange("p (b e) -> p b e", e=P),
                                            -BIG, None, ALU.mult).then_inc(moved, 1)
                dve.wait_ge(moved, 7 * n + 7)
                step(nc.vector.tensor_copy(more.at_edge[n][:, :], neg[:, :, edge]))
                step(nc.vector.memset(neg[:, :, edge], -BIG))
            dve.wait_ge(turn, 15)
            for n in range(2):
                nc.vector.tensor_scalar(more.tile_cut[n][:, :], has[n][:, 0:ST], 1.0, -BIG, ALU.min, ALU.mult)

        if more is not None:
            @block.tensor
            def _(pe):
                for n in range(2):
                    pe.wait_ge(marked, n + 1)
                    for g in range(7):
                        after(pe, moved, 7 * n + g - 6 + 1)
                        for b in range(4):
                            last = nc.tensor.transpose(turned[(7 * n + g) % 6][:, b * P:(b + 1) * P],
                                                       wide[n][:, (4 * g + b) * 16:(4 * g + b + 1) * 16, :]
                                                       .rearrange("p t h -> p (t h)"), k.ident[:, :])
                        last.then_inc(turn, 1)
                for n, mark in enumerate((more.first, more.last_mark)):
                    last = nc.tensor.matmul(has[n][:, 0:ST], k.ones[:, 0:8], mark[:, :], start=True, stop=True)
                last.then_inc(turn, 1)


def gather_loop(nc, pool, stage, staged, arrived, index, source, dest, used, per_batch=1):
    nc.gpsimd.tensor_copy(stage[:, 0:U], index[:, 0:U]).then_inc(staged, 1)

    def body(i):
        for h in range(NB):
            j, v = i * NB + h, (h + 1) % NB
            pool.wait_ge(staged, j + 1)
            after(pool, used, (j - 2) * per_batch)
            nc.gpsimd.tensor_copy(stage[:, v * U:(v + 1) * U], index[:, bass.ds((j + 1) * U, U)]).then_inc(staged, 1)
            for b in range(U):
                pool.indirect_dma_start(
                    out=dest[:, h * U + b, :], out_offset=None, in_=source[:, :],
                    in_offset=bass.IndirectOffsetOnAxis(ap=stage[:, h * U + b:h * U + b + 1], axis=0)).then_inc(arrived[h], 16)

    rounds(pool, SR, body)


class EdgeBuffers:

    def __init__(self, ph, k, local, tile_row, index, source, width):
        self.k, self.local, self.tile_row, self.index, self.source = k, local, tile_row, index, source
        self.rows = ph.sb("rows", [P, NB * U, width])
        self.stage = ph.sb("stage", [P, NB * U], i32)
        self.hot = [ph.sb(f"hot{h}", [P, U, P]) for h in range(NB)]
        self.staged, self.hotted = ph.sem("staged"), ph.sem("hotted")
        self.arrived = [ph.sem(f"arrived{h}") for h in range(NB)]

    def turn_buffers(self, ph):
        self.turned = [ph.ps(f"turned{h}", [P, 512]) for h in range(2)]
        self.hot_t = [ph.sb(f"hot_t{h}", [P, U, P]) for h in range(2)]
        self.turn, self.moved = ph.sem("turn"), ph.sem("moved")

    def one_hot(self, nc, dve, j, h):
        nc.vector.tensor_tensor(self.hot[h][:, :, :], self.local[:, bass.ds(j * U, U)].unsqueeze(2).to_broadcast([P, U, P]),
                                self.k.ramp[:, :].unsqueeze(1).to_broadcast([P, U, P]), ALU.is_equal).then_inc(self.hotted, 1)

    def turn_hot(self, nc, pe, j, h):
        pe.wait_ge(self.hotted, j + 1)
        after(pe, self.moved, j - 1)
        for b in range(U):
            last = nc.tensor.transpose(self.turned[h % 2][:, b * P:(b + 1) * P], self.hot[h][:, b, :], self.k.ident[:, :])
        last.then_inc(self.turn, 1)

    def move_hot(self, nc, act, j, h, expanded, per_batch):
        act.wait_ge(self.turn, j + 1)
        after(act, expanded, (j - 1) * per_batch)
        nc.scalar.activation(self.hot_t[h % 2][:, :, :].rearrange("p b e -> p (b e)"), self.turned[h % 2][:, :],
                             ACT.Copy).then_inc(self.moved, 1)

    def node_tile(self, eng, tile):
        return eng.value_load(self.tile_row[0:1, bass.ds(tile, 1)], min_val=0, max_val=NT - 1)


def alpha_pass(nc, k, tag, buf_args, key_rows, alpha):
    with Phase(nc, tag) as ph:
        e = EdgeBuffers(ph, k, *buf_args, 8)
        e.turn_buffers(ph)
        own_rows = [ph.ps(f"own_rows{h}", [P, 512]) for h in range(2)]
        expanded, added = ph.sem("expanded"), ph.sem("added")
        block = ph.block()

        @block.gpsimd
        def _(pool):
            gather_loop(nc, pool, e.stage, e.staged, e.arrived, e.index, e.source, e.rows, added)

        @block.vector
        def _(dve):
            e.one_hot(nc, dve, 0, 0)

            def body(i):
                for h in range(NB):
                    j = i * NB + h
                    after(dve, expanded, j - 2)
                    e.one_hot(nc, dve, j + 1, (h + 1) % NB)
                    dve.wait_ge(e.arrived[h], (i + 1) * 16 * U)
                    dve.wait_ge(expanded, j + 1)
                    nc.vector.tensor_tensor(alpha[:, bass.ds(j * U, U), :],
                                            own_rows[h % 2][:, 0:U * 8].rearrange("p (b c) -> p b c", c=8),
                                            e.rows[:, h * U:(h + 1) * U, :], ALU.add).then_inc(added, 1)

            rounds(dve, SR, body)

        @block.tensor
        def _(pe):
            e.turn_hot(nc, pe, 0, 0)

            def body(i):
                for h in range(NB):
                    j = i * NB + h
                    e.turn_hot(nc, pe, j + 1, (h + 1) % NB)
                    after(pe, added, j - 1)
                    pe.wait_ge(e.moved, j + 1)
                    for b in range(U):
                        n = e.node_tile(pe, j * U + b)
                        last = nc.tensor.matmul(own_rows[h % 2][:, b * 8:(b + 1) * 8], e.hot_t[h % 2][:, b, :],
                                                key_rows[:, bass.ds(n, 1), :].rearrange("p t c -> p (t c)"),
                                                start=True, stop=True)
                    last.then_inc(expanded, 1)

            rounds(pe, SR, body)

        @block.scalar
        def _(act):
            e.move_hot(nc, act, 0, 0, expanded, 1)

            def body(i):
                for h in range(NB):
                    e.move_hot(nc, act, i * NB + h + 1, (h + 1) % NB, expanded, 1)

            rounds(act, SR, body)


def score_pass(nc, k, tag, buf_args, q_rows, score, self_score):
    with Phase(nc, tag) as ph:
        e = EdgeBuffers(ph, k, *buf_args, C)
        e.turn_buffers(ph)
        own_rows = [ph.ps(f"own_rows{f}", [P, 2, 512]) for f in range(2)]
        prod = ph.sb("prod", [P, U, C])
        expanded, multiplied, copied, used = (ph.sem(n) for n in ("expanded", "multiplied", "copied", "used"))
        block = ph.block()

        @block.gpsimd
        def _(pool):
            gather_loop(nc, pool, e.stage, e.staged, e.arrived, e.index, e.source, e.rows, used)

        @block.vector
        def _(dve):
            e.one_hot(nc, dve, 0, 0)

            def body(i):
                for h in range(NB):
                    j = i * NB + h
                    after(dve, expanded, (j - 2) * 2)
                    e.one_hot(nc, dve, j + 1, (h + 1) % NB)
                    dve.wait_ge(e.arrived[h], (i + 1) * 16 * U)
                    after(dve, used, j)
                    for f in range(2):
                        dve.wait_ge(expanded, j * 2 + f + 1)
                        nc.vector.tensor_tensor(prod[:, 2 * f:2 * f + 2, :], own_rows[f][:, :, 0:C],
                                                e.rows[:, h * U + 2 * f:h * U + 2 * f + 2, :], ALU.mult).then_inc(multiplied, 1)
                    dve.wait_ge(multiplied, j * 2 + 2)
                    nc.vector.tensor_reduce(score[:, bass.ds(j * U, U), :], prod[:, :, :].rearrange("p b (h d) -> p b h d", h=8),
                                            AX.X, ALU.add).then_inc(used, 1)

            rounds(dve, SR, body)

        @block.tensor
        def _(pe):
            e.turn_hot(nc, pe, 0, 0)

            def body(i):
                for h in range(NB):
                    j = i * NB + h
                    e.turn_hot(nc, pe, j + 1, (h + 1) % NB)
                    pe.wait_ge(e.moved, j + 1)
                    for f in range(2):
                        after(pe, copied, (j - 1) * 2 + f + 1)
                        for b in range(2):
                            n = e.node_tile(pe, j * U + 2 * f + b)
                            last = nc.tensor.matmul(own_rows[f][:, b, 0:C + 8], e.hot_t[h % 2][:, 2 * f + b, :],
                                                    q_rows[:, bass.ds(n, 1), :].rearrange("p t c -> p (t c)"),
                                                    start=True, stop=True)
                        last.then_inc(expanded, 1)

            rounds(pe, SR, body)

        @block.scalar
        def _(act):
            e.move_hot(nc, act, 0, 0, expanded, 2)

            def body(i):
                for h in range(NB):
                    j = i * NB + h
                    e.move_hot(nc, act, j + 1, (h + 1) % NB, expanded, 2)
                    for f in range(2):
                        act.wait_ge(multiplied, j * 2 + f + 1)
                        nc.scalar.activation(self_score[:, bass.ds(j * U + 2 * f, 2), :], own_rows[f][:, :, C:C + 8],
                                             ACT.Copy).then_inc(copied, 1)

            rounds(act, SR, body)


def add_to_nodes(nc, dve, e, sums, acc, width, summed, stored, j):
    for b in range(U):
        n = e.node_tile(dve, j * U + b)
        dve.wait_ge(summed, j * U + b + 1)
        dve.wait_ge(stored, j * U + b + 1)
        into = acc[:, bass.ds(n, 1), :].rearrange("p t c -> p (t c)")
        nc.vector.tensor_tensor(into, into, sums[b][:, 0:width], ALU.add).then_inc(stored, 1)


def sum_pass(nc, k, tag, buf_args, acc, coef=None, heads=0, extra=0):
    width = C + heads + extra
    with Phase(nc, tag) as ph:
        e = EdgeBuffers(ph, k, *buf_args, C)
        sums = [ph.ps(f"sums{b}", [P, 512]) for b in range(U)]
        if heads:
            msg = [ph.sb(f"msg{f}", [P, U, width]) for f in range(2)]
        weighed, copied, summed, stored, used = (ph.sem(n) for n in ("weighed", "copied", "summed", "stored", "used"))
        block = ph.block()

        @block.gpsimd
        def _(pool):
            gather_loop(nc, pool, e.stage, e.staged, e.arrived, e.index, e.source, e.rows, *((used, 1) if heads else (summed, U)))

        @block.vector
        def _(dve):
            nc.vector.memset(acc[:, :, :], 0.0).then_inc(stored, 1)
            e.one_hot(nc, dve, 0, 0)

            def body(i):
                for h in range(NB):
                    j = i * NB + h
                    after(dve, summed, (j - 2) * U)
                    e.one_hot(nc, dve, j + 1, (h + 1) % NB)
                    if heads:
                        dve.wait_ge(e.arrived[h], (i + 1) * 16 * U)
                        after(dve, summed, (j - 1) * U)
                        nc.vector.tensor_tensor(
                            msg[h % 2][:, :, 0:C].rearrange("p b (h d) -> p b h d", h=heads),
                            e.rows[:, h * U:(h + 1) * U, :].rearrange("p b (h d) -> p b h d", h=heads),
                            coef[:, bass.ds(j * U, U), 0:heads].unsqueeze(3).to_broadcast([P, U, heads, C // heads]),
                            ALU.mult).then_inc(used, 1)
                    if not (isinstance(j, int) and j == 0):
                        add_to_nodes(nc, dve, e, sums, acc, width, summed, stored, j - 1)

            rounds(dve, SR, body)
            add_to_nodes(nc, dve, e, sums, acc, width, summed, stored, SR * NB - 1)

        @block.tensor
        def _(pe):
            def body(i):
                for h in range(NB):
                    j = i * NB + h
                    pe.wait_ge(e.hotted, j + 1)
                    if heads:
                        pe.wait_ge(used, j + 1)
                        pe.wait_ge(copied, j + 1)
                    else:
                        pe.wait_ge(e.arrived[h], (i + 1) * 16 * U)
                    for b in range(U):
                        after(pe, stored, (j - 1) * U + b + 2)
                        rhs = msg[h % 2][:, b, :] if heads else e.rows[:, h * U + b, :]
                        last = nc.tensor.matmul(sums[b][:, 0:width], e.hot[h][:, b, :], rhs, start=True, stop=True)
                        last.then_inc(summed, 1)

            rounds(pe, SR, body)

        if heads:
            @block.scalar
            def _(act):
                def body(i):
                    for h in range(NB):
                        j = i * NB + h
                        after(act, summed, (j - 1) * U)
                        nc.scalar.activation(msg[h % 2][:, :, C:width], coef[:, bass.ds(j * U, U), 0:heads + extra],
                                             ACT.Copy).then_inc(copied, 1)

                rounds(act, SR, body)


def by_source_pass(nc, k, tag, buf_args, s_src, acc):
    W = C + 2
    with Phase(nc, tag) as ph:
        e = EdgeBuffers(ph, k, *buf_args, W)
        e.turn_buffers(ph)
        own_rows = [ph.ps(f"own_rows{f}", [P, 512]) for f in range(2)]
        sums = [ph.ps(f"sums{b}", [P, 512]) for b in range(U)]
        msg = [ph.sb(f"msg{f}", [P, U, W]) for f in range(2)]
        total = [ph.sb(f"total{f}", [P, U, 2]) for f in range(2)]
        leaky = [ph.sb(f"leaky{f}", [P, U, 2]) for f in range(2)]
        expanded, totalled, leaked, raised, used, summed, stored = (
            ph.sem(n) for n in ("expanded", "totalled", "leaked", "raised", "used", "summed", "stored"))
        block = ph.block()

        @block.gpsimd
        def _(pool):
            gather_loop(nc, pool, e.stage, e.staged, e.arrived, e.index, e.source, e.rows, used)

        @block.vector
        def _(dve):
            nc.vector.memset(acc[:, :, :], 0.0).then_inc(stored, 1)
            e.one_hot(nc, dve, 0, 0)

            def body(i):
                for h in range(NB):
                    j = i * NB + h
                    after(dve, summed, (j - 2) * U)
                    e.one_hot(nc, dve, j + 1, (h + 1) % NB)
                    dve.wait_ge(e.arrived[h], (i + 1) * 16 * U)
                    dve.wait_ge(expanded, j + 1)
                    rows = e.rows[:, h * U:(h + 1) * U, :]
                    nc.vector.tensor_tensor(total[h % 2][:, :, :], own_rows[h % 2][:, 0:2 * U].rearrange("p (b c) -> p b c", c=2),
                                            rows[:, :, C:W], ALU.add).then_inc(totalled, 1)
                    dve.wait_ge(totalled, j + 1)
                    after(dve, raised, j - 1)
                    nc.vector.scalar_tensor_tensor(leaky[h % 2][:, :, :], total[h % 2][:, :, :], 0.2, total[h % 2][:, :, :],
                                                   ALU.mult, ALU.max).then_inc(leaked, 1)
                    if not (isinstance(j, int) and j == 0):
                        add_to_nodes(nc, dve, e, sums, acc, W, summed, stored, j - 1)
                    dve.wait_ge(raised, j + 1)
                    after(dve, summed, (j - 1) * U)
                    nc.vector.tensor_tensor(msg[h % 2][:, :, 0:C].rearrange("p b (h d) -> p b h d", h=2),
                                            rows[:, :, 0:C].rearrange("p b (h d) -> p b h d", h=2),
                                            msg[h % 2][:, :, C:W].unsqueeze(3).to_broadcast([P, U, 2, C // 2]),
                                            ALU.mult).then_inc(used, 1)

            rounds(dve, SR, body)
            add_to_nodes(nc, dve, e, sums, acc, W, summed, stored, SR * NB - 1)

        @block.tensor
        def _(pe):
            def expand(j, h):
                after(pe, totalled, j - 1)
                pe.wait_ge(e.moved, j + 1)
                for b in range(U):
                    n = e.node_tile(pe, j * U + b)
                    last = nc.tensor.matmul(own_rows[h % 2][:, b * 2:(b + 1) * 2], e.hot_t[h % 2][:, b, :],
                                            s_src[:, bass.ds(n, 1), :].rearrange("p t c -> p (t c)"),
                                            start=True, stop=True)
                last.then_inc(expanded, 1)

            e.turn_hot(nc, pe, 0, 0)
            expand(0, 0)

            def body(i):
                for h in range(NB):
                    j = i * NB + h
                    e.turn_hot(nc, pe, j + 1, (h + 1) % NB)
                    expand(j + 1, h + 1)
                    pe.wait_ge(used, j + 1)
                    for b in range(U):
                        after(pe, stored, (j - 1) * U + b + 2)
                        nc.tensor.matmul(sums[b][:, 0:W], e.hot[h][:, b, :], msg[h % 2][:, b, :],
                                         start=True, stop=True).then_inc(summed, 1)

            rounds(pe, SR, body)

        @block.scalar
        def _(act):
            e.move_hot(nc, act, 0, 0, expanded, 1)

            def body(i):
                for h in range(NB):
                    j = i * NB + h
                    e.move_hot(nc, act, j + 1, (h + 1) % NB, expanded, 1)
                    act.wait_ge(leaked, j + 1)
                    after(act, summed, (j - 1) * U)
                    nc.scalar.activation(msg[h % 2][:, :, C:W], leaky[h % 2][:, :, :], ACT.Exp, scale=-1.0).then_inc(raised, 1)

            rounds(act, SR, body)


class Marks:

    def __init__(self, ph):
        self.weight = ph.sb("weight", [P, ST])
        self.first = ph.sb("first", [P, ST])
        self.not_first = ph.sb("not_first", [P, ST // 16, P])
        self.not_last = ph.sb("not_last", [P, ST // 16, P])
        self.at_edge = [ph.sb(f"at_edge{n}", [P, ST // 16]) for n in range(2)]
        self.tile_cut = [ph.sb(f"tile_cut{n}", [8, ST]) for n in range(2)]


def segment_softmax(nc, k, tag, marks, score, coef, self_score=None):
    B = ST // 16
    with Phase(nc, tag) as ph:
        two = self_score is not None
        turned_s = ph.sb("turned_s", [P, B, P])
        turned_o = ph.sb("turned_o", [P, B, P]) if two else None
        top = ph.sb("top", [P, B, P])
        run = ph.sb("run", [P, B, P])
        link = [ph.sb(f"link{n}", [8, STP]) for n in range(2)]
        edge = [ph.sb(f"edge{n}", [P, B]) for n in range(2)]
        bank = [ph.ps(f"bank{n}", [P, 512]) for n in range(6)]
        ends = ph.ps("ends", [8, 512])
        enter = ph.ps("enter", [P, 512])
        own, ready, turn, moved, scanned, sent, linked, raised, back, home = (
            ph.sem(n) for n in ("own", "ready", "turn", "moved", "scanned", "sent", "linked", "raised", "back", "home"))
        block = ph.block()
        parts = [score, self_score] if two else [score]
        dest = [turned_s, turned_o]

        @block.tensor
        def _(pe):
            pe.wait_ge(ready, 1)
            for n, s in enumerate(parts):
                for g in range(7):
                    after(pe, moved, 7 * n + g - 5)
                    for b in range(4):
                        last = nc.tensor.transpose(bank[(7 * n + g) % 6][:, b * P:(b + 1) * P],
                                                   s[:, (4 * g + b) * 16:(4 * g + b + 1) * 16, :]
                                                   .rearrange("p t h -> p (t h)"), k.ident[:, :])
                    last.then_inc(turn, 1)
            for n in range(2):
                pe.wait_ge(scanned, n + 1)
                for t in range(16):
                    last = nc.tensor.matmul(ends[:, t:ST:16], k.ident[:, 8 * t:8 * t + 8], edge[n][:, :],
                                            start=True, stop=True)
                last.then_inc(sent, 1)
                pe.wait_ge(linked, n + 1)
                for t in range(16):
                    last = nc.tensor.matmul(enter[:, 0:B], k.spread[:, t, :], link[n][:, t + 2 * n:t + 2 * n + ST - 15:16],
                                            start=(t == 0), stop=(t == 15))
                last.then_inc(sent, 1)
            for n in range(len(parts)):
                pe.wait_ge(raised, n + 1)
                for g in range(7):
                    after(pe, home, 7 * n + g - 5)
                    for b in range(4):
                        last = nc.tensor.transpose(bank[(7 * n + g) % 6][:, b * P:(b + 1) * P], dest[n][:, 4 * g + b, :],
                                                   k.ident[:, :])
                    last.then_inc(back, 1)

        @block.scalar
        def _(act):
            for m in range(7 * len(parts)):
                act.wait_ge(turn, m + 1)
                nc.scalar.activation(dest[m // 7][:, 4 * (m % 7):4 * (m % 7) + 4, :].rearrange("p b e -> p (b e)"),
                                     bank[m % 6][:, :], ACT.Copy).then_inc(moved, 1)
            for n in range(len(parts)):
                act.wait_ge(ready, n + 2)
                nc.scalar.activation(dest[n][:, :, :], dest[n][:, :, :], ACT.Exp).then_inc(raised, 1)
            for m in range(7 * len(parts)):
                act.wait_ge(back, m + 1)
                n, g = m // 7, m % 7
                nc.scalar.activation(coef[:, 64 * g:64 * g + 64, 8 * n:8 * n + 8],
                                     bank[m % 6][:, :].rearrange("p (t h) -> p t h", h=8), ACT.Copy).then_inc(home, 1)

        @block.vector
        def _(dve):
            step = Chain(dve, own)
            step(nc.vector.memset(coef[:, ST:STP, :], 0.0))
            if not two:
                step(nc.vector.tensor_tensor(score[:, :, :], score[:, :, :],
                                             marks.weight[:, :].unsqueeze(2).to_broadcast([P, ST, 8]), ALU.mult))
                nc.vector.scalar_tensor_tensor(score[:, :, :], score[:, :, :], 0.2, score[:, :, :],
                                               ALU.mult, ALU.max).then_inc(ready, 1)
            else:
                nc.vector.memset(edge[0][:, :], 0.0).then_inc(ready, 1)
            nc.vector.memset(link[0][:, 0:1], -BIG)
            step(nc.vector.memset(link[1][:, ST + 1:ST + 2], -BIG))
            dve.wait_ge(moved, 7 * len(parts))
            if two:
                step(nc.vector.tensor_tensor(top[:, :, :], turned_s[:, :, :], turned_o[:, :, :], ALU.max))
            else:
                step(nc.vector.tensor_copy(top[:, :, :], turned_s[:, :, :]))

            def scan(out, cut, data, way):
                flat = [a[:, :, :].rearrange("p b e -> p (b e)")[:, ::way] for a in (out, cut, data)]
                return nc.vector.tensor_tensor_scan(*flat, -BIG, ALU.add, ALU.max)

            for n, (data, res, cut, end, start, way) in enumerate((
                    (top, run, marks.not_first, P - 1, 0, 1), (run, top, marks.not_last, 0, P - 1, -1))):
                step(scan(res, cut, data, way))
                nc.vector.tensor_copy(edge[n][:, :], res[:, :, end]).then_inc(scanned, 1)
                dve.wait_ge(sent, 2 * n + 1)
                nc.vector.tensor_tensor_scan(link[n][:, 1:ST + 1][:, ::way], marks.tile_cut[n][:, ::way],
                                             ends[:, 0:ST][:, ::way], -BIG, ALU.add, ALU.max).then_inc(linked, 1)
                dve.wait_ge(sent, 2 * n + 2)
                step(nc.vector.tensor_tensor(edge[n][:, :], enter[:, 0:B], marks.at_edge[n][:, :], ALU.add))
                step(nc.vector.tensor_tensor(data[:, :, start], data[:, :, start], edge[n][:, :], ALU.max))
                step(scan(res, cut, data, way))
            for n in range(len(parts)):
                nc.vector.tensor_tensor(dest[n][:, :, :], dest[n][:, :, :], top[:, :, :], ALU.subtract).then_inc(ready, 1)
            if two:
                dve.wait_ge(home, 14)
                nc.vector.tensor_tensor(coef[:, 0:ST, 8:16], coef[:, 0:ST, 8:16],
                                        marks.first[:, :].unsqueeze(2).to_broadcast([P, ST, 8]), ALU.mult)


class Sink:

    def __init__(self, dram, col, width):
        self.dram, self.col, self.width = dram, col, width


def project(nc, k, tag, src, width, weights, bias, sinks, evac, out_width=None, post=None, post_steps=0, extra=None):
    chunks = [(c, min(512, width - c)) for c in range(0, width, 512)]
    nch, na, nv = len(chunks), evac.count("a"), evac.count("v")
    with Phase(nc, tag) as ph:
        own_w = isinstance(weights, list)
        w = ph.sb("w", [P, 2, width]) if own_w else weights
        b = ph.sb("b", [P, width]) if bias else None
        copy = [ph.sb(f"copy{u}", [P, C]) for u in range(SLOTS)]
        turned = [ph.sb(f"turned{u}", [P, 2, P]) for u in range(SLOTS)]
        out = [ph.sb(f"out{u}", [P, out_width or width]) for u in range(SLOTS)]
        turn_p = [ph.ps(f"turn_p{n}", [P, 512]) for n in range(3)]
        prod = [ph.ps(f"prod{u}", [P, 512]) for u in range(SLOTS)]
        loaded, copied, turn, moved, multiplied, read_a, read_v, own, posted = (
            ph.sem(n) for n in ("loaded", "copied", "turn", "moved", "multiplied", "read_a", "read_v", "own", "posted"))
        stored = [ph.sem(f"stored{u}") for u in range(SLOTS)]
        bufs = extra(ph) if extra else None
        loads = ([(w[:, :, c:c + m], a.rearrange("(c p) m -> p c m", p=P)) for a, c, m in weights] if own_w else [])
        loads += [(b[:, c:c + m], a.partition_broadcast(P)) for a, c, m in (bias or [])]
        loads += bufs.loads if bufs else []
        block = ph.block()

        def out_free(eng, i, u):
            after(eng, stored[u], i * 16 * len(sinks))

        @block.sync
        def _(sp):
            for dst, a in loads:
                sp.dma_start(dst, a).then_inc(loaded, 16)

            def body(i):
                for u in range(SLOTS):
                    t = i * SLOTS + u
                    if na:
                        sp.wait_ge(read_a, (t + 1) * na)
                    if nv:
                        sp.wait_ge(read_v, (t + 1) * nv)
                    if post:
                        sp.wait_ge(posted, t + 1)
                    for s in sinks:
                        sp.dma_start(s.dram[bass.ds(t * P, P), :], out[u][:, s.col:s.col + s.width]).then_inc(stored[u], 16)

            rounds(sp, ROUNDS, body)
            for u in range(SLOTS):
                sp.wait_ge(stored[u], ROUNDS * 16 * len(sinks))

        @block.scalar
        def _(act):
            def move(t, u):
                act.wait_ge(turn, t + 1)
                after(act, multiplied, (t - SLOTS + 1) * nch)
                nc.scalar.activation(turned[u][:, :, :].rearrange("p c n -> p (c n)"), turn_p[u % 3][:, 0:C],
                                     ACT.Copy).then_inc(moved, 1)

            def read(i, t, u):
                if not na:
                    return
                out_free(act, i, u)
                for n, (c, m) in enumerate(chunks):
                    if evac[n] == "a":
                        act.wait_ge(multiplied, t * nch + n + 1)
                        nc.scalar.activation(out[u][:, c:c + m], prod[(u * nch + n) % SLOTS][:, 0:m], ACT.Copy).then_inc(read_a, 1)

            def body(i):
                for u in range(SLOTS):
                    t = i * SLOTS + u
                    after(act, turn, t - SLOTS + 1)
                    nc.scalar.activation(copy[u][:, :], src[:, bass.ds(t, 1), :].rearrange("p t c -> p (t c)"),
                                         ACT.Copy).then_inc(copied, 1)
                    if not (isinstance(t, int) and t < 1):
                        move(t - 1, (u - 1) % SLOTS)
                    if not (isinstance(t, int) and t < 2):
                        read(i if u >= 2 else i - 1, t - 2, (u - 2) % SLOTS)

            rounds(act, ROUNDS, body)
            move(NT - 1, SLOTS - 1)
            read(ROUNDS - 1, NT - 2, SLOTS - 2)
            read(ROUNDS - 1, NT - 1, SLOTS - 1)

        @block.tensor
        def _(pe):
            pe.wait_ge(loaded, 16 * len(loads)) if loads else None

            def multiply(t, u):
                pe.wait_ge(moved, t + 1)
                for n, (c, m) in enumerate(chunks):
                    lin = u * nch + n - SLOTS
                    t2, n2 = (t - u + lin // nch, lin % nch)
                    kind = evac[n2]
                    sem, per, upto = ((read_a, na, evac[:n2 + 1].count("a")) if kind == "a"
                                      else (read_v, nv, evac[:n2 + 1].count("v")))
                    after(pe, sem, t2 * per + upto)
                    for c2 in range(2):
                        last = nc.tensor.matmul(prod[(u * nch + n) % SLOTS][:, 0:m], turned[u][:, c2, :], w[:, c2, c:c + m],
                                                start=(c2 == 0), stop=(c2 == 1))
                    last.then_inc(multiplied, 1)

            def body(i):
                for u in range(SLOTS):
                    t = i * SLOTS + u
                    pe.wait_ge(copied, t + 1)
                    after(pe, moved, t - 1)
                    for c2 in range(2):
                        last = nc.tensor.transpose(turn_p[u % 3][:, c2 * P:(c2 + 1) * P], copy[u][:, c2 * P:(c2 + 1) * P],
                                                   k.ident[:, :])
                    last.then_inc(turn, 1)
                    if not (isinstance(t, int) and t < 1):
                        multiply(t - 1, (u - 1) % SLOTS)

            rounds(pe, ROUNDS, body)
            multiply(NT - 1, SLOTS - 1)

        @block.vector
        def _(dve):
            if bias or post:
                dve.wait_ge(loaded, 16 * len(loads))

            def body(i):
                for u in range(SLOTS):
                    t = i * SLOTS + u
                    if nv:
                        out_free(dve, i, u)
                    for n, (c, m) in enumerate(chunks):
                        if evac[n] == "v":
                            dve.wait_ge(multiplied, t * nch + n + 1)
                            p = prod[(u * nch + n) % SLOTS][:, 0:m]
                            ins = (nc.vector.tensor_tensor(out[u][:, c:c + m], p, b[:, c:c + m], ALU.add) if bias
                                   else nc.vector.tensor_copy(out[u][:, c:c + m], p))
                            ins.then_inc(read_v, 1)
                    if post:
                        if na:
                            dve.wait_ge(read_a, (t + 1) * na)
                        if nv:
                            dve.wait_ge(read_v, (t + 1) * nv)
                        out_free(dve, i, u)
                        start = t * post_steps
                        step = Chain(dve, own, start)
                        post(dve, step, t, out[u], bufs)
                        nc.vector.memset(bufs.tick[:, :], 0.0).then_inc(posted, 1)

            rounds(dve, ROUNDS, body)


class Extra:
    pass


def fold_heads(nc, step, out, a, b, tmp, heads):
    step(nc.vector.tensor_tensor(tmp, a, b, ALU.mult))
    step(nc.vector.tensor_reduce(out, tmp.rearrange("p (h d) -> p h d", h=heads), AX.X, ALU.add))


def flat_tile(a, t):
    return a[:, bass.ds(t, 1), :].rearrange("p t c -> p (t c)")


class Norm:

    def __init__(self, ph):
        self.stats = ph.sb("stats", [P, NT, 6])
        self.mean, self.var, self.tmp = (ph.sb(n, [P, NT]) for n in ("row_mean", "row_var", "row_tmp"))
        self.varied, self.rooted, self.scaled = (ph.sem(n) for n in ("row_varied", "row_rooted", "row_scaled"))

    def dve(self, nc, dve, step, x, y, gain=None, bias=None):
        with dve.Fori(0, NT) as t:
            nc.vector.bn_stats(flat_tile(self.stats, t), flat_tile(x, t)).then_inc(self.scaled, 1)
        dve.wait_ge(self.scaled, NT)
        st = self.stats
        step(nc.vector.tensor_tensor(self.mean[:, :], st[:, :, 1], st[:, :, 4], ALU.add))
        step(nc.vector.tensor_scalar(self.mean[:, :], self.mean[:, :], 0.5, None, ALU.mult))
        step(nc.vector.tensor_tensor(self.tmp[:, :], st[:, :, 1], st[:, :, 4], ALU.subtract))
        step(nc.vector.scalar_tensor_tensor(self.tmp[:, :], self.tmp[:, :], 0.25, self.tmp[:, :], ALU.mult, ALU.mult))
        step(nc.vector.tensor_tensor(self.var[:, :], st[:, :, 2], st[:, :, 5], ALU.add))
        step(nc.vector.scalar_tensor_tensor(self.var[:, :], self.var[:, :], 1.0 / C, self.tmp[:, :], ALU.mult, ALU.add))
        nc.vector.tensor_scalar(self.var[:, :], self.var[:, :], EPS, None, ALU.add).then_inc(self.varied, 1)
        dve.wait_ge(self.rooted, 1)
        step(nc.vector.reciprocal(self.var[:, :], self.var[:, :]))
        with dve.Fori(0, NT) as t:
            nc.vector.tensor_scalar(flat_tile(y, t), flat_tile(x, t), self.mean[:, bass.ds(t, 1)],
                                    self.var[:, bass.ds(t, 1)], ALU.subtract, ALU.mult).then_inc(self.scaled, 1)
        dve.wait_ge(self.scaled, 2 * NT)
        if gain is not None:
            step(nc.vector.tensor_tensor(y[:, :, :], y[:, :, :], gain[:, :].unsqueeze(1).to_broadcast([P, NT, C]), ALU.mult))
            step(nc.vector.tensor_tensor(y[:, :, :], y[:, :, :], bias[:, :].unsqueeze(1).to_broadcast([P, NT, C]), ALU.add))

    def act(self, nc, act):
        act.wait_ge(self.varied, 1)
        nc.scalar.activation(self.var[:, :], self.var[:, :], ACT.Sqrt).then_inc(self.rooted, 1)


def node_rows(dram, width=C):
    return dram.rearrange("(t p) c -> p t c", p=P)


def attend_update(nc, k, tag, acc, heads, x, guard, residual=None):
    with Phase(nc, tag) as ph:
        norm = Norm(ph)
        hp = ph.sb("hp", [P, NT, C])
        res = ph.sb("res", [P, NT, C]) if residual is not None else None
        pad = ph.sb("pad", [P, 1])
        own, loaded, divided, raised = (ph.sem(n) for n in ("own", "loaded", "divided", "raised"))
        block = ph.block()

        @block.sync
        def _(sp):
            if residual is not None:
                sp.dma_start(res[:, :, :], node_rows(residual)).then_inc(loaded, 16)

        @block.scalar
        def _(act):
            act.wait_ge(divided, 1)
            nc.scalar.activation(acc[:, :, 0:C], acc[:, :, 0:C], ACT.Exp).then_inc(raised, 1)
            norm.act(nc, act)

        @block.vector
        def _(dve):
            step = Chain(dve, own)
            z = acc[:, :, C:C + heads]
            if guard:
                step(nc.vector.tensor_scalar(z, z, guard, None, ALU.add))
            else:
                step(nc.vector.tensor_scalar(pad[:, :], k.row[:, :], float(NL), None, ALU.is_ge))
                step(nc.vector.tensor_scalar(acc[:, NT - 1, C:C + heads], acc[:, NT - 1, C:C + heads], pad[:, 0:1], None, ALU.add))
            step(nc.vector.reciprocal(z, z))
            step(nc.vector.tensor_tensor(hp[:, :, :].rearrange("p t (h d) -> p t h d", h=heads),
                                         acc[:, :, 0:C].rearrange("p t (h d) -> p t h d", h=heads),
                                         z.unsqueeze(3).to_broadcast([P, NT, heads, C // heads]), ALU.mult))
            nc.vector.tensor_scalar(acc[:, :, 0:C], hp[:, :, :], 0.0, None, ALU.min).then_inc(divided, 1)
            dve.wait_ge(raised, 1)
            step(nc.vector.scalar_tensor_tensor(hp[:, :, :], hp[:, :, :], 0.0, acc[:, :, 0:C], ALU.max, ALU.add))
            if residual is not None:
                dve.wait_ge(loaded, 16)
                step(nc.vector.scalar_tensor_tensor(hp[:, :, :], hp[:, :, :], -1.0, res[:, :, :], ALU.add, ALU.add))
                step(nc.vector.tensor_tensor(x[:, :, :], x[:, :, :], hp[:, :, :], ALU.add))
            else:
                step(nc.vector.scalar_tensor_tensor(x[:, :, :], hp[:, :, :], -1.0, x[:, :, :], ALU.add, ALU.add))
            norm.dve(nc, dve, step, x, x)


def norm_into(nc, tag, x, y, gain=None, bias=None, add=None, add_dram=None):
    with Phase(nc, tag) as ph:
        norm = Norm(ph)
        own, loaded = ph.sem("own"), ph.sem("loaded")
        g = ph.sb("g", [P, C]) if gain is not None else None
        b = ph.sb("b", [P, C]) if gain is not None else None
        loads = [(g[:, :], gain.partition_broadcast(P)), (b[:, :], bias.partition_broadcast(P))] if gain is not None else []
        if add_dram is not None:
            loads.append((add[:, :, :], node_rows(add_dram)))
        block = ph.block()

        @block.sync
        def _(sp):
            for dst, a in loads:
                sp.dma_start(dst, a).then_inc(loaded, 16)

        @block.scalar
        def _(act):
            norm.act(nc, act)

        @block.vector
        def _(dve):
            step = Chain(dve, own)
            if loads:
                dve.wait_ge(loaded, 16 * len(loads))
            if add is not None:
                step(nc.vector.tensor_tensor(y[:, :, :], x[:, :, :], add[:, :, :], ALU.add))
            norm.dve(nc, dve, step, x if add is None else y, y, g, b)


def feed_forward(nc, k, tag, y, h, w1, b1, w2, b2):
    FF = w1.shape[1]
    F = FF // P
    with Phase(nc, tag) as ph:
        w1_s = ph.sb("w1", [P, 2, FF])
        w2_s = ph.sb("w2", [P, F, C])
        b1_s = ph.sb("b1", [P, F])
        b2_s = ph.sb("b2", [P, C])
        copy = [ph.sb(f"copy{u}", [P, C]) for u in range(SLOTS)]
        turned = [ph.sb(f"turned{u}", [P, 2, P]) for u in range(SLOTS)]
        inner = [ph.sb(f"inner{u}", [P, F, P]) for u in range(SLOTS)]
        turn_p = [ph.ps(f"turn_p{n}", [P, 512]) for n in range(2)]
        up = [ph.ps(f"up{n}", [P, F // 2, P]) for n in range(4)]
        down = [ph.ps(f"down{n}", [P, 512]) for n in range(2)]
        loaded, copied, turn, moved, raised, bent, lowered, added, own = (
            ph.sem(n) for n in ("loaded", "copied", "turn", "moved", "raised", "bent", "lowered", "added", "own"))
        block = ph.block()

        @block.sync
        def _(sp):
            for dst, a in ((w1_s[:, :, :], w1.rearrange("(c p) f -> p c f", p=P)),
                           (w2_s[:, :, :], w2.rearrange("(f p) c -> p f c", p=P)),
                           (b1_s[:, :], b1.rearrange("(f p) -> p f", p=P)), (b2_s[:, :], b2.partition_broadcast(P))):
                sp.dma_start(dst, a, allow_slow_non_contiguous=True).then_inc(loaded, 16)

        def pair(u):
            return u % 2

        @block.scalar
        def _(act):
            act.wait_ge(loaded, 64)

            def bend(t, u):
                after(act, lowered, t - SLOTS + 1)
                for f in range(F):
                    act.wait_ge(raised, (2 * t + f // (F // 2) + 1))
                    last = nc.scalar.activation(inner[u][:, f, :], up[2 * pair(u) + f // (F // 2)][:, f % (F // 2), :],
                                                ACT.Gelu, bias=b1_s[:, f:f + 1])
                    if f % (F // 2) == F // 2 - 1:
                        last.then_inc(bent, 1)

            def body(i):
                for u in range(SLOTS):
                    t = i * SLOTS + u
                    after(act, turn, t - SLOTS + 1)
                    nc.scalar.activation(copy[u][:, :], flat_tile(y, t), ACT.Copy).then_inc(copied, 1)
                    if not (isinstance(t, int) and t < 1):
                        bend(t - 1, (u - 1) % SLOTS)

            rounds(act, ROUNDS, body)
            bend(NT - 1, SLOTS - 1)

        @block.tensor
        def _(pe):
            pe.wait_ge(loaded, 64)

            def lower(t, u):
                pe.wait_ge(bent, 2 * t + 2)
                after(pe, added, t - 1 if u else t)
                for f in range(F):
                    last = nc.tensor.matmul(down[pair(u)][:, 0:C], inner[u][:, f, :], w2_s[:, f, :], start=(f == 0), stop=(f == F - 1))
                last.then_inc(lowered, 1)

            def body(i):
                for u in range(SLOTS):
                    t = i * SLOTS + u
                    pe.wait_ge(copied, t + 1)
                    after(pe, moved, t)
                    for c in range(2):
                        last = nc.tensor.transpose(turn_p[pair(u)][:, c * P:(c + 1) * P], copy[u][:, c * P:(c + 1) * P], k.ident[:, :])
                    last.then_inc(turn, 1)
                    pe.wait_ge(moved, t + 1)
                    for half in range(2):
                        after(pe, bent, (t if u == 0 else t - 1) * 2)
                        for f in range(half * F // 2, (half + 1) * F // 2):
                            for c in range(2):
                                last = nc.tensor.matmul(up[2 * pair(u) + half][:, f % (F // 2), :], w1_s[:, c, f * P:(f + 1) * P],
                                                        turned[u][:, c, :], start=(c == 0), stop=(c == 1))
                        last.then_inc(raised, 1)
                    if not (isinstance(t, int) and t < 1):
                        lower(t - 1, (u - 1) % SLOTS)

            rounds(pe, ROUNDS, body)
            lower(NT - 1, SLOTS - 1)

        @block.vector
        def _(dve):
            dve.wait_ge(loaded, 64)
            nc.vector.tensor_tensor(h[:, :, :], h[:, :, :], b2_s[:, :].unsqueeze(1).to_broadcast([P, NT, C]),
                                    ALU.add).then_inc(own, 1)
            dve.wait_ge(own, 1)

            def add(t, u):
                dve.wait_ge(lowered, t + 1)
                nc.vector.tensor_tensor(flat_tile(h, t), flat_tile(h, t), down[pair(u)][:, 0:C], ALU.add).then_inc(added, 1)

            def body(i):
                for u in range(SLOTS):
                    t = i * SLOTS + u
                    dve.wait_ge(turn, t + 1)
                    after(dve, raised, (t - SLOTS + 1) * 2)
                    nc.vector.tensor_copy(turned[u][:, :, :].rearrange("p c n -> p (c n)"), turn_p[pair(u)][:, 0:C]).then_inc(moved, 1)
                    if not (isinstance(t, int) and t < 2):
                        add(t - 2, (u - 2) % SLOTS)

            rounds(dve, ROUNDS, body)
            add(NT - 2, SLOTS - 2)
            add(NT - 1, SLOTS - 1)


def self_attend(nc, tag, acc, v_dram):
    with Phase(nc, tag) as ph:
        v = ph.sb("v", [P, NT, C])
        own, loaded = ph.sem("own"), ph.sem("loaded")
        block = ph.block()

        @block.sync
        def _(sp):
            sp.dma_start(v[:, :, :], node_rows(v_dram)).then_inc(loaded, 16)

        @block.vector
        def _(dve):
            step = Chain(dve, own)
            heads = lambda a: a.rearrange("p t (h d) -> p t h d", h=8)
            z, w = acc[:, :, C:C + 8], acc[:, :, C + 8:C + 16]
            step(nc.vector.tensor_tensor(z, z, w, ALU.add))
            step(nc.vector.tensor_scalar(z, z, 0.5, None, ALU.max))
            step(nc.vector.reciprocal(z, z))
            dve.wait_ge(loaded, 16)
            step(nc.vector.tensor_tensor(heads(v[:, :, :]), heads(v[:, :, :]), w.unsqueeze(3).to_broadcast([P, NT, 8, C // 8]), ALU.mult))
            step(nc.vector.tensor_tensor(acc[:, :, 0:C], acc[:, :, 0:C], v[:, :, :], ALU.add))
            step(nc.vector.tensor_tensor(heads(acc[:, :, 0:C]), heads(acc[:, :, 0:C]), z.unsqueeze(3).to_broadcast([P, NT, 8, C // 8]), ALU.mult))


def move(nc, tag, pairs):
    with Phase(nc, tag) as ph:
        done = ph.sem("done")
        block = ph.block()

        @block.sync
        def _(sp):
            for dst, src in pairs:
                sp.dma_start(dst, src).then_inc(done, 16)
            sp.wait_ge(done, 16 * len(pairs))


def load_nodes(nc, x, dram):
    with Phase(nc, "load") as ph:
        done, blank = ph.sem("done"), ph.sem("blank")
        block = ph.block()

        @block.vector
        def _(dve):
            nc.vector.memset(x[:, NT - 1:NT, :], 0.0).then_inc(blank, 1)

        @block.sync
        def _(sp):
            full = (NT - 1) * P
            sp.dma_start(x[:, 0:NT - 1, :], dram[0:full, :].rearrange("(t p) c -> p t c", p=P)).then_inc(done, 16)
            sp.wait_ge(blank, 1)
            sp.dma_start(x[0:NL, NT - 1, :], dram[full:N, :]).then_inc(done, 16)
            sp.wait_ge(done, 32)


def turn_weights(nc, k, w_dram, w):
    with Phase(nc, "w0") as ph:
        rows = ph.sb("rows", [P, 2, C])
        bank = ph.ps("bank", [P, 4, P])
        loaded, turn = ph.sem("loaded"), ph.sem("turn")
        block = ph.block()

        @block.sync
        def _(sp):
            sp.dma_start(rows[:, :, :], w_dram.rearrange("h d c -> d h c")).then_inc(loaded, 16)

        @block.tensor
        def _(pe):
            pe.wait_ge(loaded, 16)
            for c in range(2):
                for h in range(2):
                    last = nc.tensor.transpose(bank[:, 2 * c + h, :], rows[:, h, c * P:(c + 1) * P], k.ident[:, :])
            last.then_inc(turn, 1)

        @block.vector
        def _(dve):
            dve.wait_ge(turn, 1)
            nc.vector.tensor_copy(w[:, :, :].rearrange("p c m -> p (c m)"), bank[:, :, :].rearrange("p a b -> p (a b)"))


def batch_norm_out(nc, k, acc, x, gamma, beta, out):
    with Phase(nc, "bn") as ph:
        norm = Norm(ph)
        g, b = ph.sb("g", [P, C]), ph.sb("b", [P, C])
        mean, scale = ph.sb("node_mean", [P, C]), ph.sb("node_scale", [P, C])
        sq = ph.sb("sq", [P, NT, C])
        col, total = ph.sb("col", [P, C]), ph.ps("total", [P, 2, C])
        pad = ph.sb("pad", [P, 1])
        own, loaded, folded, summed, varied, rooted, ready, stored = (
            ph.sem(n) for n in ("own", "loaded", "folded", "summed", "varied", "rooted", "ready", "stored"))
        block = ph.block()

        @block.sync
        def _(sp):
            sp.dma_start(g[:, :], gamma.partition_broadcast(P)).then_inc(loaded, 16)
            sp.dma_start(b[:, :], beta.partition_broadcast(P)).then_inc(loaded, 16)
            sp.wait_ge(ready, 1)
            full = (NT - 1) * P
            sp.dma_start(out[0:full, :].rearrange("(t p) c -> p t c", p=P), x[:, 0:NT - 1, :]).then_inc(stored, 16)
            sp.dma_start(out[full:N, :], x[0:NL, NT - 1, :]).then_inc(stored, 16)
            sp.wait_ge(stored, 32)

        @block.tensor
        def _(pe):
            for n in range(2):
                pe.wait_ge(folded, n + 1)
                nc.tensor.matmul(total[:, n, :], k.ones[:, :], col[:, :], start=True, stop=True).then_inc(summed, 1)

        @block.scalar
        def _(act):
            act.wait_ge(varied, 1)
            nc.scalar.activation(scale[:, :], scale[:, :], ACT.Sqrt).then_inc(rooted, 1)
            norm.act(nc, act)

        @block.vector
        def _(dve):
            step = Chain(dve, own)
            wide = lambda a: a[:, :].unsqueeze(1).to_broadcast([P, NT, C])
            nc.vector.tensor_reduce(col[:, :], acc[:, :, :].rearrange("p t c -> p c t"), AX.X, ALU.add).then_inc(folded, 1)
            step(nc.vector.tensor_scalar(pad[:, :], k.row[:, :], float(NL), None, ALU.is_lt))
            dve.wait_ge(summed, 1)
            step(nc.vector.tensor_scalar(mean[:, :], total[:, 0, :], 1.0 / N, None, ALU.mult))
            step(nc.vector.tensor_tensor(acc[:, :, :], acc[:, :, :], wide(mean), ALU.subtract))
            step(nc.vector.tensor_scalar(acc[:, NT - 1, :], acc[:, NT - 1, :], pad[:, 0:1], None, ALU.mult))
            step(nc.vector.tensor_tensor(sq[:, :, :], acc[:, :, :], acc[:, :, :], ALU.mult))
            nc.vector.tensor_reduce(col[:, :], sq[:, :, :].rearrange("p t c -> p c t"), AX.X, ALU.add).then_inc(folded, 1)
            dve.wait_ge(summed, 2)
            nc.vector.tensor_scalar(scale[:, :], total[:, 1, :], 1.0 / N, EPS, ALU.mult, ALU.add).then_inc(varied, 1)
            dve.wait_ge(rooted, 1)
            step(nc.vector.reciprocal(scale[:, :], scale[:, :]))
            dve.wait_ge(loaded, 32)
            step(nc.vector.tensor_tensor(scale[:, :], scale[:, :], g[:, :], ALU.mult))
            step(nc.vector.tensor_tensor(acc[:, :, :], acc[:, :, :], wide(scale), ALU.mult))
            step(nc.vector.tensor_tensor(x[:, :, :], x[:, :, :], acc[:, :, :], ALU.add))
            step(nc.vector.tensor_tensor(x[:, :, :], x[:, :, :], wide(b), ALU.add))
            norm.dve(nc, dve, step, x, x)
            nc.vector.memset(pad[:, :], 0.0).then_inc(ready, 1)


def first_layer(nc, k, t, x, scratch):
    with Phase(nc, "l0") as h:
        tile_of, tile_row = h.sb("tile_of", [P, STP]), h.sb("tile_row", [1, STP], i32)
        table = scratch("table_src", (P * ST, 4), i32)
        rows = scratch("rows0", (NP, C + 2))
        sort_edges(nc, k, "src", t["src"], t["dst"], None, None, table, tile_of, tile_row)
        index, local = h.sb("index", [P, STP], i32), h.sb("local", [P, STP])
        load_order(nc, k, "srcload", table, tile_of, [index], local)
        s_src = h.sb("s_src", [P, NT, 2])
        acc = h.sb("acc", [P, NT, C + 2])
        with Phase(nc, "p0") as ph:
            w = ph.sb("w", [P, 2, C])
            turn_weights(nc, k, t["L0_gnn_W"], w)

            def extra(ph):
                e = Extra()
                e.a, e.tmp, e.tick = ph.sb("a", [P, 2, C]), ph.sb("tmp", [P, C]), ph.sb("tick", [P, 1])
                a = t["L0_gnn_a"]
                e.loads = [(e.a[:, s, :].rearrange("p (h d) -> p h d", h=2), a[:, s * P:(s + 1) * P].partition_broadcast(P))
                           for s in range(2)]
                return e

            def post(dve, step, tile, out, e):
                fold_heads(nc, step, s_src[:, bass.ds(tile, 1), :].rearrange("p t c -> p (t c)"), out[:, 0:C], e.a[:, 0, :], e.tmp[:, :], 2)
                fold_heads(nc, step, out[:, C:C + 2], out[:, 0:C], e.a[:, 1, :], e.tmp[:, :], 2)

            project(nc, k, "proj0", x, C, w, [(t["L0_gnn_b"].rearrange("h d -> (h d)"), 0, C)], [Sink(rows, 0, C + 2)], "v",
                    C + 2, post, 4, extra)
        by_source_pass(nc, k, "edge0", (local, tile_row, index, rows), s_src, acc)
        attend_update(nc, k, "up0", acc, 2, x, 0)


def build(nc, t, out, scratch):
    Phase.used = []
    with Phase(nc, "all") as hold:
        k = make_constants(nc, hold)
        x_dram = scratch("x_rows", (NP, C))
        with Phase(nc, "front") as front:
            x = front.sb("x", [P, NT, C])
            load_nodes(nc, x, t["x"])
            first_layer(nc, k, t, x, scratch)
            move(nc, "keep1", [(node_rows(x_dram), x[:, :, :])])
        tile_of, tile_row = hold.sb("tile_of", [P, STP]), hold.sb("tile_row", [1, STP], i32)
        table = scratch("table_dst", (P * ST, 4), i32)
        sort_edges(nc, k, "dst", t["dst"], t["src"], t["edge_type_8"], t["edge_weight"], table, tile_of, tile_row)
        index, rel_index = hold.sb("index", [P, STP], i32), hold.sb("rel_index", [P, STP], i32)
        local = hold.sb("local", [P, STP])
        with Phase(nc, "mid") as mid:
            marks = Marks(mid)
            load_order(nc, k, "dstload", table, tile_of, [index, rel_index], local, marks)
            second_layer(nc, k, t, x_dram, scratch, marks, index, local, tile_row)
            third_layer(nc, k, t, x_dram, scratch, marks, index, local, tile_row)
        with Phase(nc, "last") as last:
            x = last.sb("x", [P, NT, C])
            move(nc, "read3", [(x[:, :, :], node_rows(x_dram))])
            rel_rows = scratch("rel_rows", (NP * 8, C))
            wide = rel_rows.rearrange("(n r) c -> n (r c)", r=8)
            project(nc, k, "proj3", x, 8 * C, [(t["L3_gnn_weight"][r], r * C, C) for r in range(8)], None,
                    [Sink(wide, 0, 8 * C)], "avav")
            acc = last.sb("acc", [P, NT, C])
            sum_pass(nc, k, "edge3", (local, tile_row, rel_index, rel_rows), acc)
            batch_norm_out(nc, k, acc, x, t["L3_gnn_gamma"], t["L3_gnn_beta"], out)


def second_layer(nc, k, t, x_dram, scratch, marks, index, local, tile_row):
    xl, res, al = scratch("xl_rows", (NP, C)), scratch("res_rows", (NP, C)), scratch("al_rows", (NP, 8))
    with Phase(nc, "l1") as h:
        coef = h.sb("coef", [P, STP, 8])
        with Phase(nc, "l1a") as ph:
            score = ph.sb("score", [P, ST, 8])
            right = ph.sb("right", [P, NT, 8])
            with Phase(nc, "l1x") as px:
                x = px.sb("x", [P, NT, C])
                move(nc, "read1", [(x[:, :, :], node_rows(x_dram))])

                def extra(ph):
                    e = Extra()
                    e.att, e.tmp, e.tick = ph.sb("att", [P, 2, C]), ph.sb("tmp", [P, C]), ph.sb("tick", [P, 1])
                    e.loads = [(e.att[:, n, :], t[a].rearrange("a h d -> (a h d)").partition_broadcast(P))
                               for n, a in enumerate(("L1_gnn_att_l", "L1_gnn_att_r"))]
                    return e

                def post(dve, step, tile, out, e):
                    fold_heads(nc, step, out[:, 2 * C:2 * C + 8], out[:, 0:C], e.att[:, 0, :], e.tmp[:, :], 8)
                    fold_heads(nc, step, flat_tile(right, tile), out[:, 0:C], e.att[:, 1, :], e.tmp[:, :], 8)

                project(nc, k, "proj1", x, 2 * C, [(t["L1_gnn_W_lin"], 0, C), (t["L1_gnn_W_res"], C, C)], None,
                        [Sink(xl, 0, C), Sink(res, C, C), Sink(al, 2 * C, 8)], "a", 2 * C + 8, post, 4, extra)
            alpha_pass(nc, k, "edge1a", (local, tile_row, index, al), right, score)
            segment_softmax(nc, k, "soft1", marks, score, coef)
        acc = h.sb("acc", [P, NT, C + 8])
        sum_pass(nc, k, "edge1b", (local, tile_row, index, xl), acc, coef, 8)
        x = h.sb("x", [P, NT, C])
        move(nc, "read1b", [(x[:, :, :], node_rows(x_dram))])
        attend_update(nc, k, "up1", acc, 8, x, 1e-16, res)
        move(nc, "keep2", [(node_rows(x_dram), x[:, :, :])])


def third_layer(nc, k, t, x_dram, scratch, marks, index, local, tile_row):
    w = lambda name: t["L2_gnn_" + name]
    h_rows, k_rows, v_rows = (scratch(n, (NP, C)) for n in ("h_rows", "k_rows", "v_rows"))
    with Phase(nc, "l2") as hold:
        h = hold.sb("h", [P, NT, C])
        with Phase(nc, "l2in") as ph:
            x = ph.sb("x", [P, NT, C])
            move(nc, "read2", [(x[:, :, :], node_rows(x_dram))])
            project(nc, k, "proj2in", x, C, [(w("w_in"), 0, C)], [(w("b_in"), 0, C)], [Sink(h_rows, 0, C)], "v")
        move(nc, "readh", [(h[:, :, :], node_rows(h_rows))])
        for l in range(2):
            with Phase(nc, f"l2_{l}") as layer:
                coef = layer.sb("coef", [P, STP, 16])
                with Phase(nc, f"l2a_{l}") as ph:
                    score, self_score = ph.sb("score", [P, ST, 8]), ph.sb("self_score", [P, ST, 8])
                    with Phase(nc, f"l2q_{l}") as pq:
                        q = pq.sb("q", [P, NT, C + 8])
                        y = (coef[:, :, :].rearrange("p t c -> p (t c)")[:, 0:NT * C]
                             .rearrange("p (t c) -> p t c", c=C))
                        norm_into(nc, f"norm_a{l}", h, y, w("ln1_g")[l], w("ln1_b")[l])

                        def extra(ph):
                            e = Extra()
                            e.tmp, e.tick, e.loads = ph.sb("tmp", [P, C]), ph.sb("tick", [P, 1]), []
                            return e

                        def post(dve, step, tile, out, e):
                            own = flat_tile(q, tile)
                            step(nc.vector.tensor_scalar(own[:, 0:C], out[:, 0:C], 32 ** -0.5, None, ALU.mult))
                            fold_heads(nc, step, own[:, C:C + 8], own[:, 0:C], out[:, C:2 * C], e.tmp[:, :], 8)

                        project(nc, k, f"proj2_{l}", y, 3 * C, [(w(n)[l], c * C, C) for c, n in enumerate(("wq", "wk", "wv"))],
                                [(w(n)[l], c * C, C) for c, n in enumerate(("bq", "bk", "bv"))],
                                [Sink(k_rows, C, C), Sink(v_rows, 2 * C, C)], "vv", None, post, 3, extra)
                        score_pass(nc, k, f"edge2a_{l}", (local, tile_row, index, k_rows), q, score, self_score)
                    segment_softmax(nc, k, f"soft2_{l}", marks, score, coef, self_score)
                with Phase(nc, f"l2b_{l}") as ph:
                    acc = ph.sb("acc", [P, NT, C + 16])
                    sum_pass(nc, k, f"edge2b_{l}", (local, tile_row, index, v_rows), acc, coef, 8, 8)
                    self_attend(nc, f"self_{l}", acc, v_rows)
                    project(nc, k, f"proj2o_{l}", acc[:, :, 0:C], C, [(w("wo")[l], 0, C)], [(w("bo")[l], 0, C)],
                            [Sink(h_rows, 0, C)], "v")
                with Phase(nc, f"l2f_{l}") as ph:
                    y = ph.sb("y", [P, NT, C])
                    move(nc, f"reado_{l}", [(y[:, :, :], node_rows(h_rows))])
                    add_rows(nc, f"addo_{l}", h, y)
                    norm_into(nc, f"norm_b{l}", h, y, w("ln2_g")[l], w("ln2_b")[l])
                    feed_forward(nc, k, f"ffn_{l}", y, h, w("w1")[l], w("b1")[l], w("w2")[l], w("b2")[l])
        with Phase(nc, "l2out") as ph:
            x = ph.sb("x", [P, NT, C])
            norm_into(nc, "norm3", h, h, add=x, add_dram=x_dram)
            move(nc, "keep3", [(node_rows(x_dram), h[:, :, :])])


def add_rows(nc, tag, x, y):
    with Phase(nc, tag) as ph:
        block = ph.block()

        @block.vector
        def _(dve):
            nc.vector.tensor_tensor(x[:, :, :], x[:, :, :], y[:, :, :], ALU.add)

def kernel(**inputs):
    import numpy as _np
    import concourse.bacc as _bacc
    from concourse import mybir as _mybir
    from concourse.bass_utils import run_bass_kernel_spmd as _run

    nc = _bacc.Bacc("TRN2", target_bir_lowering=False, num_devices=1)
    arrays, aps = {}, {}
    for name, value in inputs.items():
        a = _np.ascontiguousarray(value)
        arrays[f"in_{name}"] = a
        aps[name] = nc.dram_tensor(f"in_{name}", a.shape, _mybir.dt.from_np(a.dtype), kind="ExternalInput").ap()
    out = nc.dram_tensor("out", (N, C), _mybir.dt.float32, kind="ExternalOutput").ap()

    def scratch(name, shape, dt=_mybir.dt.float32):
        return nc.dram_tensor(name, shape, dt, kind="Internal").ap()

    build(nc, aps, out, scratch)
    r = _run(nc, [arrays], core_ids=[0])
    return r.results[0]["out"]
```

```python
from contextlib import ExitStack

import concourse.bass as bass
from concourse import mybir

fp32, bf16, i32 = mybir.dt.float32, mybir.dt.bfloat16, mybir.dt.int32
ALU = mybir.AluOpType
ACT = mybir.ActivationFunctionType
AX = mybir.AxisListType

P = 128
N = 3125
E = 53125
C = 256
NT = -(-N // P)
NL = N - (NT - 1) * P
NP = NT * P
EP = 125
ET = E // EP
U = 4
NB = 8
AHEAD = 3
HOTS = 4
ST = 448
SR = ST // (U * NB)
assert (E + NT * (P - 1)) // P <= ST and ET * EP == E and SR * U * NB == ST
STP = ST + AHEAD * U
PACK = 32
NOKEY = 4095
BIG = 1e38
EPS = 1e-5
HIST = 17
LOOK = 5
SLOTS = 5
ROUNDS = NT // SLOTS


def after(eng, sem, value):
    if isinstance(value, int) and value <= 0:
        return
    eng.wait_ge(sem, value)


def rounds(eng, n, body):
    body(0)
    if n > 1:
        with eng.Fori(1, n) as i:
            body(i)


class Chain:

    def __init__(self, eng, sem, base=0):
        self.eng, self.sem, self.n = eng, sem, base

    def __call__(self, ins):
        self.n = self.n + 1
        ins.then_inc(self.sem, 1)
        self.eng.wait_ge(self.sem, self.n)


class Phase:
    used = []

    def __init__(self, nc, tag):
        self.nc, self.tag, self.ctx, self.sems = nc, tag, ExitStack(), []

    def __enter__(self):
        self.ctx.__enter__()
        return self

    def __exit__(self, *a):
        done = self.ctx.__exit__(*a)
        Phase.used += self.sems
        if len(Phase.used) > 120:
            Phase.clear(self.nc)
        return done

    @staticmethod
    def clear(nc):
        nc.clear_and_free_semaphores(Phase.used)
        nc.all_engine_barrier()
        Phase.used = []

    def sb(self, name, shape, dt=fp32):
        return self.ctx.enter_context(self.nc.sbuf_tensor(f"{self.tag}_{name}", shape, dt))

    def ps(self, name, shape, dt=fp32):
        return self.ctx.enter_context(self.nc.psum_tensor(f"{self.tag}_{name}", shape, dt))

    def sem(self, name):
        self.sems.append(self.nc.alloc_semaphore(f"{self.tag}_{name}"))
        return self.sems[-1]

    def block(self):
        return self.ctx.enter_context(self.nc.Block())


class Constants:
    pass


def make_constants(nc, hold):
    k = Constants()
    k.ident = hold.sb("ident", [P, P])
    k.ident_b = hold.sb("ident_b", [P, P], bf16)
    k.ramp = hold.sb("ramp", [P, P])
    k.ramp_b = hold.sb("ramp_b", [P, P], bf16)
    k.row = hold.sb("row", [P, 1])
    k.ones = hold.sb("ones", [P, P])
    k.before = hold.sb("before", [P, P])
    k.above = hold.sb("above", [P, P])
    k.upto = hold.sb("upto", [P, P])
    k.slots = hold.sb("slots", [P, ST])
    k.spread = hold.sb("spread", [8, 16, P])
    with Phase(nc, "const") as ph:
        diff = ph.sb("diff", [P, P], i32)
        ramp_i = ph.sb("ramp_i", [P, ST], i32)
        row_i = ph.sb("row_i", [P, 1], i32)
        spread_i = ph.sb("spread_i", [8, 16, P], i32)
        made = ph.sem("made")
        block = ph.block()

        @block.gpsimd
        def _(pool):
            nc.gpsimd.iota(diff[:, :], pattern=[[1, P]], base=0, channel_multiplier=-1)
            nc.gpsimd.iota(ramp_i[:, :], pattern=[[1, ST]], base=0, channel_multiplier=0)
            nc.gpsimd.iota(row_i[:, :], pattern=[[1, 1]], base=0, channel_multiplier=1)
            nc.gpsimd.iota(spread_i[:, :, :], pattern=[[-8, 16], [1, P]], base=0,
                           channel_multiplier=-1).then_inc(made, 1)
            nc.gpsimd.memset(k.ones[:, :], 1.0)

        @block.vector
        def _(dve):
            dve.wait_ge(made, 1)
            nc.vector.tensor_scalar(k.ident[:, :], diff[:, :], 0.0, None, ALU.is_equal)
            nc.vector.tensor_scalar(k.ident_b[:, :], diff[:, :], 0.0, None, ALU.is_equal)
            nc.vector.tensor_scalar(k.above[:, :], diff[:, :], 0.0, None, ALU.is_gt)
            nc.vector.tensor_scalar(k.upto[:, :], diff[:, :], 0.0, None, ALU.is_ge)
            nc.vector.tensor_scalar(k.before[:, :], diff[:, :], 0.0, None, ALU.is_lt)
            nc.vector.tensor_copy(k.ramp[:, :], ramp_i[:, 0:P])
            nc.vector.tensor_copy(k.ramp_b[:, :], ramp_i[:, 0:P])
            nc.vector.tensor_copy(k.slots[:, :], ramp_i[:, :])
            nc.vector.tensor_copy(k.row[:, :], row_i[:, :])
            nc.vector.tensor_scalar(k.spread[:, :, :], spread_i[:, :, :], 0.0, None, ALU.is_equal)
    return k


class Scatter:
    ROUNDS = ET // LOOK // SLOTS

    def __init__(self, hold, tag, table):
        self.tag, self.table, self.next = tag, table, 0
        self.stage_all = hold.sb(f"{tag}_stage_all", [EP, ET + LOOK, 5], i32)

    def piece(self, nc, ph, pool, n):
        n = min(n, self.ROUNDS - self.next)
        if n < 1:
            return
        first, table, stage_all = self.next * SLOTS, self.table, self.stage_all
        self.next += n
        stage = ph.sb("put_stage", [EP, SLOTS, LOOK, 5], i32)
        staged = ph.sem("put_staged")
        put = [ph.sem(f"put{u}") for u in range(SLOTS)]
        nc.gpsimd.tensor_copy(stage[:, 0, :, :], stage_all[:, first * LOOK:(first + 1) * LOOK, :]).then_inc(staged, 1)

        def body(i):
            for u in range(SLOTS):
                g, v = i * SLOTS + u, (u + 1) % SLOTS
                after(pool, put[v], (i + (1 if v == 0 else 0)) * 16 * LOOK)
                pool.wait_ge(staged, g + 1)
                nc.gpsimd.tensor_copy(stage[:, v, :, :],
                                      stage_all[:, bass.ds((g + first + 1) * LOOK, LOOK), :]).then_inc(staged, 1)
                for j in range(LOOK):
                    pool.indirect_dma_start(
                        out=table[:, :], out_offset=bass.IndirectOffsetOnAxis(ap=stage[:, u, j, 0:1], axis=0),
                        in_=stage[:, u, j, 1:5], in_offset=None).then_inc(put[u], 16)

        rounds(pool, n, body)
        for u in range(SLOTS):
            pool.wait_ge(put[u], n * 16 * LOOK)

    def beside(self, nc, ph, block, n):
        if self.next < self.ROUNDS:
            @block.gpsimd
            def _(pool):
                self.piece(nc, ph, pool, n)

    def rest(self, nc):
        with Phase(nc, self.tag + "_put") as ph:
            block = ph.block()
            self.beside(nc, ph, block, self.ROUNDS)


def sort_edges(nc, k, tag, key, other, etype, weight, scatter, tile_of, tile_row, earlier=None):
    stage_all, table = scatter.stage_all, scatter.table
    arrays = [key, other] + ([etype, weight] if weight is not None else [])
    with ExitStack() as outer:
        def keep(name, shape, dt=fp32):
            return outer.enter_context(nc.sbuf_tensor(f"{tag}_{name}", shape, dt))

        key_c = keep("key_c", [EP, ET])
        count = keep("count", [P, ET + 1, NT])
        hi_hot = keep("hi_hot", [EP, ET, NT], bf16)

        with Phase(nc, tag + "_in") as ph:
            rows = [ph.sb(f"rows{n}", [P, 4, EP], i32) for n in range(len(arrays))]
            rows_f = [ph.sb(f"rows_f{n}", [P, 4, EP]) for n in range(len(arrays))]
            cols = [key_c] + [ph.sb(f"cols{n}", [EP, ET]) for n in range(1, len(arrays))]
            key_i = ph.sb("key_i", [EP, ET], i32)
            part_i = ph.sb("part_i", [EP, ET], i32)
            part_f = ph.sb("part_f", [EP, ET], bf16)
            relation = ph.sb("relation", [EP, ET])
            empty = ph.sb("empty", [P, ST, 4], i32)
            turned = [ph.ps(f"turned{n}", [EP, 512]) for n in range(len(arrays))]
            loaded, cast, turn, own, blank, wiped = (
                ph.sem(n) for n in ("loaded", "cast", "turn", "own", "blank", "wiped"))
            block = ph.block()
            full = ET // P * P

            @block.sync
            def _(sp):
                for n, a in enumerate(arrays):
                    src = a if a.dtype != fp32 else a.bitcast(i32)
                    sp.dma_start(rows[n][:, 0:3, :],
                                 src[0:full * EP].rearrange("(b p e) -> p b e", p=P, e=EP)).then_inc(loaded, 16)
                    sp.dma_start(rows[n][0:ET - full, 3, :],
                                 src[full * EP:E].rearrange("(p e) -> p e", e=EP)).then_inc(loaded, 16)
                sp.wait_ge(blank, 3)
                sp.dma_start(table.rearrange("(p t) w -> p t w", p=P), empty[:, :, :]).then_inc(wiped, 16)
                sp.wait_ge(wiped, 16)

            @block.gpsimd
            def _(pool):
                nc.gpsimd.memset(empty[:, :, :], 0).then_inc(blank, 1)
                pool.wait_ge(blank, 1)
                nc.gpsimd.memset(empty[:, :, 2:3], NOKEY).then_inc(blank, 2)
                if earlier:
                    earlier.piece(nc, ph, pool, 1)

            @block.vector
            def _(dve):
                dve.wait_ge(loaded, 32 * len(arrays))
                for n in range(len(arrays)):
                    for r, m in ((slice(0, 3), P), (slice(3, 4), ET - full)):
                        out, src = rows_f[n][0:m, r, :], rows[n][0:m, r, :]
                        if n == 3:
                            src = src.bitcast(fp32)
                        ins = nc.vector.tensor_copy(out, src)
                        ins.then_inc(cast, 1)
                step = Chain(dve, own)
                for n in range(len(arrays)):
                    dve.wait_ge(turn, n + 1)
                    step(nc.vector.tensor_copy(cols[n][:, :], turned[n][:, 0:ET]))
                step(nc.vector.tensor_copy(key_i[:, :], key_c[:, :]))
                step(nc.vector.tensor_scalar(part_i[:, :], key_i[:, :], 7, None, ALU.arith_shift_right))
                step(nc.vector.tensor_copy(part_f[:, :], part_i[:, :]))
                nc.vector.tensor_tensor(hi_hot[:, :, :], part_f[:, :].unsqueeze(2).to_broadcast([EP, ET, NT]),
                                        k.ramp_b[0:EP, 0:NT].unsqueeze(1).to_broadcast([EP, ET, NT]), ALU.is_equal)
                step(nc.vector.memset(stage_all[:, :, :], 0))
                nc.vector.tensor_copy(stage_all[:, 0:ET, 1], cols[1][:, :])
                nc.vector.tensor_copy(stage_all[:, 0:ET, 3], key_c[:, :])
                if weight is not None:
                    step(nc.vector.scalar_tensor_tensor(relation[:, :], cols[1][:, :], 8.0, cols[2][:, :],
                                                        ALU.mult, ALU.add))
                    nc.vector.tensor_copy(stage_all[:, 0:ET, 2], relation[:, :])
                    nc.vector.tensor_copy(stage_all[:, 0:ET, 4].bitcast(fp32), cols[3][:, :])

            @block.tensor
            def _(pe):
                for n in range(len(arrays)):
                    pe.wait_ge(cast, 2 * n + 2)
                    for b in range(4):
                        m = min(P, ET - b * P)
                        last = nc.tensor.transpose(turned[n][:, b * P:b * P + m], rows_f[n][0:m, b, :],
                                                   k.ident[0:m, 0:m])
                    last.then_inc(turn, 1)

        with Phase(nc, tag + "_hist") as ph:
            lo_hot = [ph.sb(f"lo_hot{u}", [EP, HIST, P], bf16) for u in range(SLOTS)]
            key_i = ph.sb("key_i", [EP, ET], i32)
            low_i = ph.sb("low_i", [EP, ET], i32)
            low = ph.sb("low", [EP, ET], bf16)
            sums = [ph.ps(f"sums{u}", [P, 512]) for u in range(SLOTS)]
            own, hot, summed, counted = (ph.sem(n) for n in ("own", "hot", "summed", "counted"))
            block = ph.block()
            assert ET // HIST == NT
            if earlier:
                earlier.beside(nc, ph, block, 3)

            @block.vector
            def _(dve):
                step = Chain(dve, own)
                step(nc.vector.tensor_copy(key_i[:, :], key_c[:, :]))
                step(nc.vector.tensor_scalar(low_i[:, :], key_i[:, :], P - 1, None, ALU.bitwise_and))
                step(nc.vector.tensor_copy(low[:, :], low_i[:, :]))
                nc.vector.memset(count[:, 0:1, :], 0.0).then_inc(counted, 1)

                def accumulate(g, u):
                    dve.wait_ge(summed, g + 1)
                    dve.wait_ge(counted, g + 1)
                    nc.vector.tensor_tensor(
                        count[:, bass.ds(g * HIST + 1, HIST), :],
                        sums[u][:, 0:HIST * NT].rearrange("p (t h) -> p t h", h=NT),
                        count[:, bass.ds(g * HIST, 1), :].to_broadcast([P, HIST, NT]), ALU.add).then_inc(counted, 1)

                def body(i):
                    for u in range(SLOTS):
                        g = i * SLOTS + u
                        after(dve, summed, g - SLOTS + 1)
                        nc.vector.tensor_tensor(
                            lo_hot[u][:, :, :], low[:, bass.ds(g * HIST, HIST)].unsqueeze(2).to_broadcast([EP, HIST, P]),
                            k.ramp_b[0:EP, :].unsqueeze(1).to_broadcast([EP, HIST, P]), ALU.is_equal).then_inc(hot, 1)
                        if not (isinstance(g, int) and g == 0):
                            accumulate(g - 1, (u - 1) % SLOTS)

                rounds(dve, ET // HIST // SLOTS, body)
                accumulate(ET // HIST - 1, SLOTS - 1)

            @block.tensor
            def _(pe):
                def body(i):
                    for u in range(SLOTS):
                        g = i * SLOTS + u
                        pe.wait_ge(hot, g + 1)
                        after(pe, counted, g - SLOTS + 2)
                        for j in range(HIST):
                            n = HIST - j
                            last = nc.tensor.matmul(
                                sums[u][:, j * NT:HIST * NT].rearrange("p (t h) -> p t h", h=NT), lo_hot[u][:, j, :],
                                hi_hot[:, bass.ds(g * HIST + j, 1), :].to_broadcast([EP, n, NT]),
                                start=(j == 0), stop=(j == HIST - 1))
                        last.then_inc(summed, 1)

                rounds(pe, ET // HIST // SLOTS, body)

        with Phase(nc, tag + "_base") as ph:
            base = ph.sb("base", [P, NT])
            tiles_i = ph.sb("tiles_i", [P, NT], i32)
            tiles = ph.sb("tiles", [P, NT])
            ends = ph.sb("ends", [P, NT])
            col_i = ph.sb("col_i", [NT, 1], i32)
            col = ph.sb("col", [NT, 1])
            end_c = ph.sb("end_c", [NT, 1])
            past = ph.sb("past", [NT, ST])
            packed = ph.sb("packed", [1, STP // U])
            lows = ph.ps("lows", [P, 512])
            totals = ph.ps("totals", [P, 512])
            total_c = ph.ps("total_c", [NT, 512])
            end_p = ph.ps("end_p", [NT, 512])
            which = ph.ps("which", [P, 512])
            own, made, summed = (ph.sem(n) for n in ("own", "made", "summed"))
            block = ph.block()
            final = count[:, ET, :]

            @block.tensor
            def _(pe):
                nc.tensor.matmul(lows[:, 0:NT], k.above[:, :], final, start=True, stop=True)
                nc.tensor.matmul(totals[:, 0:NT], k.ones[:, :], final, start=True, stop=True)
                nc.tensor.matmul(total_c[:, 0:1], final, k.ones[:, 0:1], start=True, stop=True).then_inc(summed, 1)
                pe.wait_ge(made, 1)
                nc.tensor.matmul(end_p[:, 0:1], k.upto[0:NT, 0:NT], col[:, :], start=True, stop=True).then_inc(summed, 1)
                pe.wait_ge(made, 2)
                nc.tensor.matmul(which[:, 0:ST], k.ones[0:NT, :], past[:, :], start=True, stop=True).then_inc(summed, 1)

            @block.vector
            def _(dve):
                step = Chain(dve, own)
                dve.wait_ge(summed, 1)
                for total, whole, out in ((total_c[:, 0:1], col_i[:, :], col[:, :]),
                                          (totals[:, 0:NT], tiles_i[:, :], tiles[:, :])):
                    step(nc.vector.tensor_scalar(whole, total, float(P - 1), None, ALU.add))
                    step(nc.vector.tensor_scalar(whole, whole, 7, None, ALU.arith_shift_right))
                    step(nc.vector.tensor_copy(out, whole))
                nc.vector.memset(base[:, :], 0.0).then_inc(made, 1)
                step(nc.vector.tensor_tensor_scan(ends[:, :], k.ones[:, 0:NT], tiles[:, :], 0.0, ALU.mult, ALU.add))
                dve.wait_ge(summed, 2)
                step(nc.vector.tensor_copy(end_c[:, :], end_p[:, 0:1]))
                nc.vector.tensor_scalar(past[:, :], k.slots[0:NT, :], end_c[:, 0:1], None, ALU.is_ge).then_inc(made, 1)
                step(nc.vector.tensor_tensor(base[:, :], ends[:, :], tiles[:, :], ALU.subtract))
                step(nc.vector.scalar_tensor_tensor(base[:, :], base[:, :], float(P), lows[:, 0:NT], ALU.mult, ALU.add))
                nc.vector.tensor_tensor(count[:, 0:ET, :], count[:, 0:ET, :],
                                        base[:, :].unsqueeze(1).to_broadcast([P, ET, NT]), ALU.add)
                step(nc.vector.memset(tile_of[:, :], float(NT - 1)))
                dve.wait_ge(summed, 3)
                step(nc.vector.tensor_scalar(tile_of[:, 0:ST], which[:, 0:ST], float(NT - 1), None, ALU.min))
                for b in range(U - 2, -1, -1):
                    so_far = tile_of[0:1, U - 1:STP:U] if b == U - 2 else packed[:, :]
                    step(nc.vector.scalar_tensor_tensor(packed[:, :], so_far, float(PACK), tile_of[0:1, b:STP:U],
                                                        ALU.mult, ALU.add))
                nc.vector.tensor_copy(tile_row[:, :], packed[:, :])

        with Phase(nc, tag + "_rank") as ph:
            W = LOOK * EP
            keys = [ph.sb(f"keys{u}", [P, W], i32) for u in range(SLOTS)]
            low_i = [ph.sb(f"low_i{u}", [P, W], i32) for u in range(2)]
            low_hot = [ph.sb(f"low_hot{u}", [P, W]) for u in range(SLOTS)]
            same = ph.sb("same", [EP, LOOK, EP])
            picked = ph.sb("picked", [EP, LOOK, NT])
            rank = ph.sb("rank", [EP, ET])
            slot = ph.sb("slot", [EP, ET])
            slot_i = ph.sb("slot_i", [EP, ET], i32)
            in_tile = ph.sb("in_tile", [EP, ET], i32)
            found = [ph.ps(f"found{u}", [EP, 512]) for u in range(SLOTS)]
            loaded = [ph.sem(f"loaded{u}") for u in range(SLOTS)]
            masked, hot, looked, ranked, took, got, own = (
                ph.sem(n) for n in ("masked", "hot", "looked", "ranked", "took", "got", "own"))
            block = ph.block()
            groups = ET // LOOK
            if earlier:
                earlier.beside(nc, ph, block, 10)

            @block.sync
            def _(sp):
                def body(i):
                    for u in range(SLOTS):
                        g = i * SLOTS + u
                        after(sp, ranked, g - SLOTS + 1)
                        sp.dma_start(keys[u][:, :], key[bass.ds(g * W, W)].partition_broadcast(P)).then_inc(loaded[u], 16)

                rounds(sp, groups // SLOTS, body)

            @block.vector
            def _(dve):
                def take(g, u):
                    dve.wait_ge(looked, g + 1)
                    after(dve, got, g)
                    nc.vector.tensor_tensor(
                        picked[:, :, :], found[u][:, 0:LOOK * NT].rearrange("p (t h) -> p t h", h=NT),
                        hi_hot[:, bass.ds(g * LOOK, LOOK), :], ALU.mult).then_inc(took, 1)
                    dve.wait_ge(took, g + 1)
                    nc.vector.tensor_reduce(slot[:, bass.ds(g * LOOK, LOOK)], picked[:, :, :], AX.X,
                                            ALU.add).then_inc(got, 1)

                def body(i):
                    for u in range(SLOTS):
                        g = i * SLOTS + u
                        dve.wait_ge(loaded[u], i * 16 + 16)
                        after(dve, hot, g - 1)
                        nc.vector.tensor_scalar(low_i[u % 2][:, :], keys[u][:, :], P - 1, None,
                                                ALU.bitwise_and).then_inc(masked, 1)
                        dve.wait_ge(masked, g + 1)
                        after(dve, looked, g - SLOTS + 1)
                        nc.vector.tensor_scalar(low_hot[u][:, :], low_i[u % 2][:, :], k.row[:, 0:1], None,
                                                ALU.is_equal).then_inc(hot, 1)
                        after(dve, ranked, g)
                        for j in range(LOOK):
                            t = g * LOOK + j
                            last = nc.vector.scalar_tensor_tensor(
                                same[:, j, :], keys[u][0:EP, j * EP:(j + 1) * EP], key_c[:, bass.ds(t, 1)],
                                k.before[0:EP, 0:EP], ALU.is_equal, ALU.mult, accum_out=rank[:, bass.ds(t, 1)])
                        last.then_inc(ranked, 1)
                        if not (isinstance(g, int) and g == 0):
                            take(g - 1, (u - 1) % SLOTS)

                rounds(dve, groups // SLOTS, body)
                take(groups - 1, SLOTS - 1)
                step = Chain(dve, own)
                dve.wait_ge(got, groups)
                dve.wait_ge(ranked, groups)
                step(nc.vector.tensor_tensor(slot[:, :], slot[:, :], rank[:, :], ALU.add))
                step(nc.vector.tensor_copy(slot_i[:, :], slot[:, :]))
                step(nc.vector.tensor_scalar(in_tile[:, :], slot_i[:, :], P - 1, None, ALU.bitwise_and))
                step(nc.vector.tensor_scalar(slot_i[:, :], slot_i[:, :], 7, None, ALU.arith_shift_right))
                nc.vector.scalar_tensor_tensor(stage_all[:, 0:ET, 0], in_tile[:, :], float(ST), slot_i[:, :],
                                               ALU.mult, ALU.add)

            @block.tensor
            def _(pe):
                def body(i):
                    for u in range(SLOTS):
                        g = i * SLOTS + u
                        pe.wait_ge(hot, g + 1)
                        after(pe, took, g - SLOTS + 1)
                        for j in range(LOOK):
                            last = nc.tensor.matmul(found[u][:, j * NT:(j + 1) * NT], low_hot[u][:, j * EP:(j + 1) * EP],
                                                    count[:, bass.ds(g * LOOK + j, 1), :].rearrange("p t h -> p (t h)"),
                                                    start=True, stop=True)
                        last.then_inc(looked, 1)

                rounds(pe, groups // SLOTS, body)


def load_order(nc, k, tag, table, tile_of, index, local, more=None):
    with Phase(nc, tag) as ph:
        raw = ph.sb("raw", [P, ST, 4], i32)
        key_f = ph.sb("key_f", [P, ST])
        loaded, own = ph.sem("loaded"), ph.sem("own")
        rows = table.rearrange("(p t) w -> p t w", p=P)
        if more is not None:
            edges, edge_f = [ph.sb(f"edge{n}", [P, ST, 4], i32) for n in range(2)], [ph.sb(f"edge_f{n}", [P, ST]) for n in range(2)]
            wide = [ph.sb(f"wide{n}", [P, ST, 8]) for n in range(2)]
            turned = [ph.ps(f"turned{n}", [P, 512]) for n in range(6)]
            has = [ph.ps(f"has{n}", [8, 512]) for n in range(2)]
            cleared, marked, turn, moved = (ph.sem(n) for n in ("cleared", "marked", "turn", "moved"))
        block = ph.block()

        @block.sync
        def _(sp):
            sp.dma_start(raw[:, :, :], rows).then_inc(loaded, 16)
            if more is not None:
                sp.wait_ge(cleared, 2)
                sp.dma_start(edges[0][1:P, :, :], rows[0:P - 1]).then_inc(loaded, 16)
                sp.dma_start(edges[0][0:1, 1:ST, :], rows[P - 1:P, 0:ST - 1]).then_inc(loaded, 16)
                sp.dma_start(edges[1][0:P - 1, :, :], rows[1:P]).then_inc(loaded, 16)
                sp.dma_start(edges[1][P - 1:P, 0:ST - 1, :], rows[0:1, 1:ST]).then_inc(loaded, 16)

        @block.vector
        def _(dve):
            step = Chain(dve, own)
            if more is not None:
                for n in range(2):
                    nc.vector.memset(edges[n][:, :, :], -1).then_inc(cleared, 1)
            step(nc.vector.memset(index[0][:, :], 0))
            if more is not None:
                step(nc.vector.memset(index[1][:, :], 0))
            step(nc.vector.memset(local[:, :], float(NOKEY)))
            dve.wait_ge(loaded, 80 if more is not None else 16)
            nc.vector.tensor_copy(index[0][:, 0:ST], raw[:, :, 0])
            step(nc.vector.tensor_copy(key_f[:, :], raw[:, :, 2]))
            nc.vector.scalar_tensor_tensor(local[:, 0:ST], tile_of[:, 0:ST], -float(P), key_f[:, :], ALU.mult, ALU.add)
            if more is None:
                return
            nc.vector.tensor_copy(index[1][:, 0:ST], raw[:, :, 1])
            nc.vector.tensor_copy(more.weight[:, :], raw[:, :, 3].bitcast(fp32))
            last_mark = ph.sb("last_mark", [P, ST])
            for n, mark in enumerate((more.first, last_mark)):
                step(nc.vector.tensor_copy(edge_f[n][:, :], edges[n][:, :, 2]))
                step(nc.vector.tensor_tensor(mark[:, :], key_f[:, :], edge_f[n][:, :], ALU.not_equal))
                nc.vector.tensor_copy(wide[n][:, :, :], mark[:, :].unsqueeze(2).to_broadcast([P, ST, 8])).then_inc(marked, 1)
            more.last_mark = last_mark
            for n, (neg, edge) in enumerate(((more.not_first, 0), (more.not_last, P - 1))):
                for g in range(7):
                    dve.wait_ge(turn, 7 * n + g + 1)
                    nc.vector.tensor_scalar(neg[:, 4 * g:4 * g + 4, :],
                                            turned[(7 * n + g) % 6][:, :].rearrange("p (b e) -> p b e", e=P),
                                            -BIG, None, ALU.mult).then_inc(moved, 1)
                dve.wait_ge(moved, 7 * n + 7)
                step(nc.vector.tensor_copy(more.at_edge[n][:, :], neg[:, :, edge]))
                step(nc.vector.memset(neg[:, :, edge], -BIG))
            dve.wait_ge(turn, 15)
            for n in range(2):
                nc.vector.tensor_scalar(more.tile_cut[n][:, :], has[n][:, 0:ST], 1.0, -BIG, ALU.min, ALU.mult)

        if more is not None:
            @block.tensor
            def _(pe):
                for n in range(2):
                    pe.wait_ge(marked, n + 1)
                    for g in range(7):
                        after(pe, moved, 7 * n + g - 6 + 1)
                        for b in range(4):
                            last = nc.tensor.transpose(turned[(7 * n + g) % 6][:, b * P:(b + 1) * P],
                                                       wide[n][:, (4 * g + b) * 16:(4 * g + b + 1) * 16, :]
                                                       .rearrange("p t h -> p (t h)"), k.ident[:, :])
                        last.then_inc(turn, 1)
                for n, mark in enumerate((more.first, more.last_mark)):
                    last = nc.tensor.matmul(has[n][:, 0:ST], k.ones[:, 0:8], mark[:, :], start=True, stop=True)
                last.then_inc(turn, 1)


def gather_loop(nc, pool, stage, staged, arrived, index, source, dest, used, per_batch=1):
    nc.gpsimd.tensor_copy(stage[:, 0:U], index[:, 0:U]).then_inc(staged, 1)

    def body(i):
        for h in range(NB):
            j, v = i * NB + h, (h + 1) % NB
            pool.wait_ge(staged, j + 1)
            after(pool, used, (j + 2 - NB) * per_batch)
            nc.gpsimd.tensor_copy(stage[:, v * U:(v + 1) * U], index[:, bass.ds((j + 1) * U, U)]).then_inc(staged, 1)
            for b in range(U):
                pool.indirect_dma_start(
                    out=dest[:, h * U + b, :], out_offset=None, in_=source[:, :],
                    in_offset=bass.IndirectOffsetOnAxis(ap=stage[:, h * U + b:h * U + b + 1], axis=0)).then_inc(arrived[h], 16)

    rounds(pool, SR, body)


class EdgeBuffers:

    def __init__(self, ph, k, local, tile_row, index, source, width, hot_dt=fp32):
        self.k, self.local, self.tile_row, self.index, self.source = k, local, tile_row, index, source
        self.rows = ph.sb("rows", [P, NB * U, width])
        self.stage = ph.sb("stage", [P, NB * U], i32)
        self.hot = [ph.sb(f"hot{h}", [P, U, P], hot_dt) for h in range(HOTS)]
        self.staged, self.hotted = ph.sem("staged"), ph.sem("hotted")
        self.arrived = [ph.sem(f"arrived{h}") for h in range(NB)]

    def turn_buffers(self, ph):
        self.turned = [ph.ps(f"turned{h}", [P, 512]) for h in range(2)]
        self.hot_t = [ph.sb(f"hot_t{h}", [P, U, P]) for h in range(2)]
        self.turn, self.moved = ph.sem("turn"), ph.sem("moved")

    def one_hot(self, nc, dve, j, h):
        nc.vector.tensor_tensor(self.hot[h % HOTS][:, :, :],
                                self.local[:, bass.ds(j * U, U)].unsqueeze(2).to_broadcast([P, U, P]),
                                self.k.ramp[:, :].unsqueeze(1).to_broadcast([P, U, P]), ALU.is_equal).then_inc(self.hotted, 1)

    def turn_hot(self, nc, pe, j, h):
        pe.wait_ge(self.hotted, j + 1)
        after(pe, self.moved, j - 1)
        for b in range(U):
            last = nc.tensor.matmul(self.turned[h % 2][:, b * P:(b + 1) * P], self.hot[h % HOTS][:, b, :],
                                    self.k.ident_b[:, :], start=True, stop=True)
        last.then_inc(self.turn, 1)

    def move_hot(self, nc, act, j, h, expanded):
        act.wait_ge(self.turn, j + 1)
        after(act, expanded, j - 1)
        nc.scalar.activation(self.hot_t[h % 2][:, :, :].rearrange("p b e -> p (b e)"), self.turned[h % 2][:, :],
                             ACT.Copy).then_inc(self.moved, 1)

    def node_tiles(self, nc, eng, j):
        packed = eng.value_load(self.tile_row[0:1, bass.ds(j, 1)], min_val=0, max_val=PACK ** U - 1)
        return [nc.s_assert_within((packed // PACK ** b) % PACK, 0, NT - 1,
                                   skip_runtime_bounds_check_because="the sort clips every node tile to NT - 1")
                for b in range(U)]


def alpha_pass(nc, k, tag, buf_args, key_rows, alpha):
    with Phase(nc, tag) as ph:
        e = EdgeBuffers(ph, k, *buf_args, 8, bf16)
        e.turn_buffers(ph)
        own_rows = [ph.ps(f"own_rows{h}", [P, 512]) for h in range(4)]
        expanded, added = ph.sem("expanded"), ph.sem("added")
        block = ph.block()

        @block.gpsimd
        def _(pool):
            gather_loop(nc, pool, e.stage, e.staged, e.arrived, e.index, e.source, e.rows, added)

        @block.vector
        def _(dve):
            for j in range(AHEAD):
                e.one_hot(nc, dve, j, j)

            def body(i):
                for h in range(NB):
                    j = i * NB + h
                    after(dve, e.turn, j + AHEAD - HOTS + 1)
                    e.one_hot(nc, dve, j + AHEAD, h + AHEAD)
                    dve.wait_ge(e.arrived[h], (i + 1) * 16 * U)
                    dve.wait_ge(expanded, j + 1)
                    nc.vector.tensor_tensor(alpha[:, bass.ds(j * U, U), :],
                                            own_rows[h % 4][:, 0:U * 8].rearrange("p (b c) -> p b c", c=8),
                                            e.rows[:, h * U:(h + 1) * U, :], ALU.add).then_inc(added, 1)

            rounds(dve, SR, body)

        @block.tensor
        def _(pe):
            def expand(j, h):
                after(pe, added, j - 3)
                pe.wait_ge(e.moved, j + 1)
                for b, n in enumerate(e.node_tiles(nc, pe, j)):
                    last = nc.tensor.matmul(own_rows[h % 4][:, b * 8:(b + 1) * 8], e.hot_t[h % 2][:, b, :],
                                            key_rows[:, bass.ds(n, 1), :].rearrange("p t c -> p (t c)"),
                                            start=True, stop=True)
                last.then_inc(expanded, 1)

            e.turn_hot(nc, pe, 0, 0)
            e.turn_hot(nc, pe, 1, 1)
            expand(0, 0)
            e.turn_hot(nc, pe, 2, 2)
            expand(1, 1)

            def body(i):
                for h in range(NB):
                    j = i * NB + h
                    e.turn_hot(nc, pe, j + 3, h + 3)
                    expand(j + 2, h + 2)

            rounds(pe, SR, body)

        @block.scalar
        def _(act):
            for j in range(AHEAD):
                e.move_hot(nc, act, j, j, expanded)

            def body(i):
                for h in range(NB):
                    e.move_hot(nc, act, i * NB + h + AHEAD, h + AHEAD, expanded)

            rounds(act, SR, body)


def score_pass(nc, k, tag, buf_args, q_rows, score, self_score):
    with Phase(nc, tag) as ph:
        e = EdgeBuffers(ph, k, *buf_args, C, bf16)
        e.turn_buffers(ph)
        own_rows = [ph.ps(f"own_rows{n}", [P, U, C]) for n in range(2)]
        own_self = [ph.ps(f"own_self{n}", [P, 512]) for n in range(2)]
        expanded, own_selves, multiplied, copied, used = (
            ph.sem(n) for n in ("expanded", "own_selves", "multiplied", "copied", "used"))
        block = ph.block()

        @block.gpsimd
        def _(pool):
            gather_loop(nc, pool, e.stage, e.staged, e.arrived, e.index, e.source, e.rows, used)

        @block.vector
        def _(dve):
            for j in range(AHEAD):
                e.one_hot(nc, dve, j, j)

            def body(i):
                for h in range(NB):
                    j = i * NB + h
                    dve.wait_ge(e.arrived[h], (i + 1) * 16 * U)
                    dve.wait_ge(expanded, j + 1)
                    rows = e.rows[:, h * U:(h + 1) * U, :]
                    nc.vector.tensor_tensor(rows, own_rows[h % 2][:, :, :], rows, ALU.mult).then_inc(multiplied, 1)
                    after(dve, e.turn, j + AHEAD - HOTS + 1)
                    e.one_hot(nc, dve, j + AHEAD, h + AHEAD)
                    dve.wait_ge(multiplied, j + 1)
                    nc.vector.tensor_reduce(score[:, bass.ds(j * U, U), :], rows.rearrange("p b (h d) -> p b h d", h=8),
                                            AX.X, ALU.add).then_inc(used, 1)

            rounds(dve, SR, body)

        @block.tensor
        def _(pe):
            def expand(j, h):
                pe.wait_ge(e.moved, j + 1)
                after(pe, copied, j - 1)
                tiles = e.node_tiles(nc, pe, j)
                for b in range(U):
                    last = nc.tensor.matmul(own_self[h % 2][:, b * 8:(b + 1) * 8], e.hot_t[h % 2][:, b, :],
                                            q_rows[:, bass.ds(tiles[b], 1), C:C + 8].rearrange("p t c -> p (t c)"),
                                            start=True, stop=True)
                last.then_inc(own_selves, 1)
                after(pe, multiplied, j - 1)
                for b in range(U):
                    last = nc.tensor.matmul(own_rows[h % 2][:, b, :], e.hot_t[h % 2][:, b, :],
                                            q_rows[:, bass.ds(tiles[b], 1), 0:C].rearrange("p t c -> p (t c)"),
                                            start=True, stop=True)
                last.then_inc(expanded, 1)

            e.turn_hot(nc, pe, 0, 0)
            e.turn_hot(nc, pe, 1, 1)
            expand(0, 0)

            def body(i):
                for h in range(NB):
                    j = i * NB + h
                    e.turn_hot(nc, pe, j + 2, h + 2)
                    expand(j + 1, h + 1)

            rounds(pe, SR, body)

        @block.scalar
        def _(act):
            e.move_hot(nc, act, 0, 0, expanded)
            e.move_hot(nc, act, 1, 1, expanded)

            def body(i):
                for h in range(NB):
                    j = i * NB + h
                    act.wait_ge(own_selves, j + 1)
                    nc.scalar.activation(self_score[:, bass.ds(j * U, U), :],
                                         own_self[h % 2][:, 0:U * 8].rearrange("p (b c) -> p b c", c=8),
                                         ACT.Copy).then_inc(copied, 1)
                    e.move_hot(nc, act, j + 2, h + 2, expanded)

            rounds(act, SR, body)


def add_to_nodes(nc, dve, e, sums, acc, width, summed, stored, j):
    for b, n in enumerate(e.node_tiles(nc, dve, j)):
        dve.wait_ge(summed, j * U + b + 1)
        dve.wait_ge(stored, j * U + b + 1)
        into = acc[:, bass.ds(n, 1), :].rearrange("p t c -> p (t c)")
        nc.vector.tensor_tensor(into, into, sums[b][:, 0:width], ALU.add).then_inc(stored, 1)


def sum_pass(nc, k, tag, buf_args, acc, coef=None, heads=0, extra=0):
    width = C + heads + extra
    with Phase(nc, tag) as ph:
        e = EdgeBuffers(ph, k, *buf_args, C)
        sums = [ph.ps(f"sums{b}", [P, 512]) for b in range(2 * U)]
        if heads:
            msg = [ph.sb(f"msg{f}", [P, U, width]) for f in range(2)]
        weighed, copied, summed, stored, used = (ph.sem(n) for n in ("weighed", "copied", "summed", "stored", "used"))
        block = ph.block()

        @block.gpsimd
        def _(pool):
            gather_loop(nc, pool, e.stage, e.staged, e.arrived, e.index, e.source, e.rows, *((used, 1) if heads else (summed, U)))

        @block.vector
        def _(dve):
            nc.vector.memset(acc[:, :, :], 0.0).then_inc(stored, 1)
            e.one_hot(nc, dve, 0, 0)
            e.one_hot(nc, dve, 1, 1)

            def body(i):
                for h in range(NB):
                    j = i * NB + h
                    if heads:
                        dve.wait_ge(e.arrived[h], (i + 1) * 16 * U)
                        after(dve, summed, (j - 1) * U)
                        nc.vector.tensor_tensor(
                            msg[h % 2][:, :, 0:C].rearrange("p b (h d) -> p b h d", h=heads),
                            e.rows[:, h * U:(h + 1) * U, :].rearrange("p b (h d) -> p b h d", h=heads),
                            coef[:, bass.ds(j * U, U), 0:heads].unsqueeze(3).to_broadcast([P, U, heads, C // heads]),
                            ALU.mult).then_inc(used, 1)
                    after(dve, summed, (j + 3 - HOTS) * U)
                    e.one_hot(nc, dve, j + 2, h + 2)
                    if not (isinstance(j, int) and j == 0):
                        add_to_nodes(nc, dve, e, sums[(h + 1) % 2 * U:], acc, width, summed, stored, j - 1)

            rounds(dve, SR, body)
            add_to_nodes(nc, dve, e, sums[U:], acc, width, summed, stored, SR * NB - 1)

        @block.tensor
        def _(pe):
            def body(i):
                for h in range(NB):
                    j = i * NB + h
                    pe.wait_ge(e.hotted, j + 1)
                    if heads:
                        pe.wait_ge(used, j + 1)
                        pe.wait_ge(copied, j + 1)
                    else:
                        pe.wait_ge(e.arrived[h], (i + 1) * 16 * U)
                    for b in range(U):
                        after(pe, stored, (j - 2) * U + b + 2)
                        rhs = msg[h % 2][:, b, :] if heads else e.rows[:, h * U + b, :]
                        last = nc.tensor.matmul(sums[h % 2 * U + b][:, 0:width], e.hot[h % HOTS][:, b, :], rhs, start=True, stop=True)
                        last.then_inc(summed, 1)

            rounds(pe, SR, body)

        if heads:
            @block.scalar
            def _(act):
                def body(i):
                    for h in range(NB):
                        j = i * NB + h
                        after(act, summed, (j - 1) * U)
                        nc.scalar.activation(msg[h % 2][:, :, C:width], coef[:, bass.ds(j * U, U), 0:heads + extra],
                                             ACT.Copy).then_inc(copied, 1)

                rounds(act, SR, body)


def by_source_pass(nc, k, tag, buf_args, s_src, acc):
    W = C + 2
    with Phase(nc, tag) as ph:
        e = EdgeBuffers(ph, k, *buf_args, W, bf16)
        e.turn_buffers(ph)
        own_rows = [ph.ps(f"own_rows{f}", [P, 512]) for f in range(2)]
        sums = [ph.ps(f"sums{b}", [P, 512]) for b in range(U)]
        wide_hot = [ph.sb(f"wide_hot{f}", [P, U, P]) for f in range(4)]
        msg = [ph.sb(f"msg{f}", [P, U, W]) for f in range(4)]
        total = [ph.sb(f"total{f}", [P, U, 2]) for f in range(2)]
        leaky = [ph.sb(f"leaky{f}", [P, U, 2]) for f in range(2)]
        expanded, totalled, leaked, raised, used, summed, stored, widened = (
            ph.sem(n) for n in ("expanded", "totalled", "leaked", "raised", "used", "summed", "stored", "widened"))
        block = ph.block()

        @block.gpsimd
        def _(pool):
            gather_loop(nc, pool, e.stage, e.staged, e.arrived, e.index, e.source, e.rows, used)

        @block.vector
        def _(dve):
            def total_of(j, h, i):
                dve.wait_ge(e.arrived[h], (i + 1) * 16 * U)
                dve.wait_ge(expanded, j + 1)
                nc.vector.tensor_tensor(total[h % 2][:, :, :], own_rows[h % 2][:, 0:2 * U].rearrange("p (b c) -> p b c", c=2),
                                        e.rows[:, h * U:(h + 1) * U, C:W], ALU.add).then_inc(totalled, 1)
                dve.wait_ge(totalled, j + 1)
                after(dve, raised, j - 1)
                nc.vector.scalar_tensor_tensor(leaky[h % 2][:, :, :], total[h % 2][:, :, :], 0.2, total[h % 2][:, :, :],
                                               ALU.mult, ALU.max).then_inc(leaked, 1)

            nc.vector.memset(acc[:, :, :], 0.0).then_inc(stored, 1)
            for j in range(AHEAD):
                e.one_hot(nc, dve, j, j)
            total_of(0, 0, 0)

            def step(i, h, j, with_next=True):
                if with_next:
                    after(dve, widened, j + AHEAD - HOTS + 1)
                    after(dve, e.turn, j + AHEAD - HOTS + 1)
                    e.one_hot(nc, dve, j + AHEAD, h + AHEAD)
                    total_of(j + 1, (h + 1) % NB, i + (h + 1) // NB)
                dve.wait_ge(raised, j + 1)
                nc.vector.tensor_tensor(msg[h % 4][:, :, 0:C].rearrange("p b (h d) -> p b h d", h=2),
                                        e.rows[:, h * U:(h + 1) * U, 0:C].rearrange("p b (h d) -> p b h d", h=2),
                                        msg[h % 4][:, :, C:W].unsqueeze(3).to_broadcast([P, U, 2, C // 2]),
                                        ALU.mult).then_inc(used, 1)
                if not (isinstance(j, int) and j == 0):
                    add_to_nodes(nc, dve, e, sums, acc, W, summed, stored, j - 1)

            def body(i):
                for h in range(NB):
                    step(i, h, i * NB + h)

            body(0)
            with dve.Fori(1, SR - 1) as i:
                body(i)
            for h in range(NB):
                step(SR - 1, h, (SR - 1) * NB + h, h < NB - 1)
            add_to_nodes(nc, dve, e, sums, acc, W, summed, stored, SR * NB - 1)

        @block.tensor
        def _(pe):
            def expand(j, h):
                after(pe, totalled, j - 1)
                pe.wait_ge(e.moved, j + 1)
                for b, n in enumerate(e.node_tiles(nc, pe, j)):
                    last = nc.tensor.matmul(own_rows[h % 2][:, b * 2:(b + 1) * 2], e.hot_t[h % 2][:, b, :],
                                            s_src[:, bass.ds(n, 1), :].rearrange("p t c -> p (t c)"),
                                            start=True, stop=True)
                last.then_inc(expanded, 1)

            e.turn_hot(nc, pe, 0, 0)
            e.turn_hot(nc, pe, 1, 1)
            expand(0, 0)
            e.turn_hot(nc, pe, 2, 2)
            expand(1, 1)

            def step(h, j, with_next=True):
                if with_next:
                    e.turn_hot(nc, pe, j + 3, h + 3)
                    expand(j + 2, h + 2)
                pe.wait_ge(used, j + 1)
                pe.wait_ge(widened, j + 1)
                for b in range(U):
                    after(pe, stored, (j - 1) * U + b + 2)
                    nc.tensor.matmul(sums[b][:, 0:W], wide_hot[h % 4][:, b, :], msg[h % 4][:, b, :],
                                     start=True, stop=True).then_inc(summed, 1)

            def body(i):
                for h in range(NB):
                    step(h, i * NB + h)

            body(0)
            with pe.Fori(1, SR - 1) as i:
                body(i)
            for h in range(NB):
                step(h, (SR - 1) * NB + h, h < NB - 2)

        @block.scalar
        def _(act):
            def widen(j, h):
                act.wait_ge(e.hotted, j + 1)
                after(act, summed, (j - 3) * U)
                nc.scalar.activation(wide_hot[h % 4][:, :, :], e.hot[h % HOTS][:, :, :], ACT.Copy).then_inc(widened, 1)

            def raise_of(j, h):
                act.wait_ge(leaked, j + 1)
                after(act, summed, (j - 3) * U)
                nc.scalar.activation(msg[h % 4][:, :, C:W], leaky[h % 2][:, :, :], ACT.Exp, scale=-1.0).then_inc(raised, 1)

            e.move_hot(nc, act, 0, 0, expanded)
            e.move_hot(nc, act, 1, 1, expanded)
            widen(0, 0)
            widen(1, 1)
            e.move_hot(nc, act, 2, 2, expanded)
            raise_of(0, 0)

            def step(h, j, left=NB):
                if left > 0:
                    raise_of(j + 1, h + 1)
                if left > 2:
                    e.move_hot(nc, act, j + 3, h + 3, expanded)
                if left > 1:
                    widen(j + 2, h + 2)

            def body(i):
                for h in range(NB):
                    step(h, i * NB + h)

            body(0)
            with act.Fori(1, SR - 1) as i:
                body(i)
            for h in range(NB):
                step(h, (SR - 1) * NB + h, NB - 1 - h)


class Marks:

    def __init__(self, ph):
        self.weight = ph.sb("weight", [P, ST])
        self.first = ph.sb("first", [P, ST])
        self.not_first = ph.sb("not_first", [P, ST // 16, P])
        self.not_last = ph.sb("not_last", [P, ST // 16, P])
        self.at_edge = [ph.sb(f"at_edge{n}", [P, ST // 16]) for n in range(2)]
        self.tile_cut = [ph.sb(f"tile_cut{n}", [8, ST]) for n in range(2)]


def segment_softmax(nc, k, tag, marks, score, coef, self_score=None):
    B = ST // 16
    with Phase(nc, tag) as ph:
        two = self_score is not None
        turned_s = ph.sb("turned_s", [P, B, P])
        turned_o = ph.sb("turned_o", [P, B, P]) if two else None
        top = ph.sb("top", [P, B, P])
        run = ph.sb("run", [P, B, P])
        link = [ph.sb(f"link{n}", [8, STP]) for n in range(2)]
        edge = [ph.sb(f"edge{n}", [P, B]) for n in range(2)]
        bank = [ph.ps(f"bank{n}", [P, 512]) for n in range(6)]
        ends = ph.ps("ends", [8, 512])
        enter = ph.ps("enter", [P, 512])
        own, ready, turn, moved, scanned, sent, linked, raised, back, home = (
            ph.sem(n) for n in ("own", "ready", "turn", "moved", "scanned", "sent", "linked", "raised", "back", "home"))
        block = ph.block()
        parts = [score, self_score] if two else [score]
        dest = [turned_s, turned_o]

        @block.tensor
        def _(pe):
            pe.wait_ge(ready, 1)
            for n, s in enumerate(parts):
                for g in range(7):
                    after(pe, moved, 7 * n + g - 5)
                    for b in range(4):
                        last = nc.tensor.transpose(bank[(7 * n + g) % 6][:, b * P:(b + 1) * P],
                                                   s[:, (4 * g + b) * 16:(4 * g + b + 1) * 16, :]
                                                   .rearrange("p t h -> p (t h)"), k.ident[:, :])
                    last.then_inc(turn, 1)
            for n in range(2):
                pe.wait_ge(scanned, n + 1)
                for t in range(16):
                    last = nc.tensor.matmul(ends[:, t:ST:16], k.ident[:, 8 * t:8 * t + 8], edge[n][:, :],
                                            start=True, stop=True)
                last.then_inc(sent, 1)
                pe.wait_ge(linked, n + 1)
                for t in range(16):
                    last = nc.tensor.matmul(enter[:, 0:B], k.spread[:, t, :], link[n][:, t + 2 * n:t + 2 * n + ST - 15:16],
                                            start=(t == 0), stop=(t == 15))
                last.then_inc(sent, 1)
            for n in range(len(parts)):
                pe.wait_ge(raised, n + 1)
                for g in range(7):
                    after(pe, home, 7 * n + g - 5)
                    for b in range(4):
                        last = nc.tensor.transpose(bank[(7 * n + g) % 6][:, b * P:(b + 1) * P], dest[n][:, 4 * g + b, :],
                                                   k.ident[:, :])
                    last.then_inc(back, 1)

        @block.scalar
        def _(act):
            for m in range(7 * len(parts)):
                act.wait_ge(turn, m + 1)
                nc.scalar.activation(dest[m // 7][:, 4 * (m % 7):4 * (m % 7) + 4, :].rearrange("p b e -> p (b e)"),
                                     bank[m % 6][:, :], ACT.Copy).then_inc(moved, 1)
            for n in range(len(parts)):
                act.wait_ge(ready, n + 2)
                nc.scalar.activation(dest[n][:, :, :], dest[n][:, :, :], ACT.Exp).then_inc(raised, 1)
            for m in range(7 * len(parts)):
                act.wait_ge(back, m + 1)
                n, g = m // 7, m % 7
                nc.scalar.activation(coef[:, 64 * g:64 * g + 64, 8 * n:8 * n + 8],
                                     bank[m % 6][:, :].rearrange("p (t h) -> p t h", h=8), ACT.Copy).then_inc(home, 1)

        @block.vector
        def _(dve):
            step = Chain(dve, own)
            step(nc.vector.memset(coef[:, ST:STP, :], 0.0))
            if not two:
                step(nc.vector.tensor_tensor(score[:, :, :], score[:, :, :],
                                             marks.weight[:, :].unsqueeze(2).to_broadcast([P, ST, 8]), ALU.mult))
                nc.vector.scalar_tensor_tensor(score[:, :, :], score[:, :, :], 0.2, score[:, :, :],
                                               ALU.mult, ALU.max).then_inc(ready, 1)
            else:
                nc.vector.memset(edge[0][:, :], 0.0).then_inc(ready, 1)
            nc.vector.memset(link[0][:, 0:1], -BIG)
            step(nc.vector.memset(link[1][:, ST + 1:ST + 2], -BIG))
            dve.wait_ge(moved, 7 * len(parts))
            if two:
                step(nc.vector.tensor_tensor(top[:, :, :], turned_s[:, :, :], turned_o[:, :, :], ALU.max))
            else:
                step(nc.vector.tensor_copy(top[:, :, :], turned_s[:, :, :]))

            def scan(out, cut, data, way):
                flat = [a[:, :, :].rearrange("p b e -> p (b e)")[:, ::way] for a in (out, cut, data)]
                return nc.vector.tensor_tensor_scan(*flat, -BIG, ALU.add, ALU.max)

            for n, (data, res, cut, end, start, way) in enumerate((
                    (top, run, marks.not_first, P - 1, 0, 1), (run, top, marks.not_last, 0, P - 1, -1))):
                step(scan(res, cut, data, way))
                nc.vector.tensor_copy(edge[n][:, :], res[:, :, end]).then_inc(scanned, 1)
                dve.wait_ge(sent, 2 * n + 1)
                nc.vector.tensor_tensor_scan(link[n][:, 1:ST + 1][:, ::way], marks.tile_cut[n][:, ::way],
                                             ends[:, 0:ST][:, ::way], -BIG, ALU.add, ALU.max).then_inc(linked, 1)
                dve.wait_ge(sent, 2 * n + 2)
                step(nc.vector.tensor_tensor(edge[n][:, :], enter[:, 0:B], marks.at_edge[n][:, :], ALU.add))
                step(nc.vector.tensor_tensor(data[:, :, start], data[:, :, start], edge[n][:, :], ALU.max))
                step(scan(res, cut, data, way))
            for n in range(len(parts)):
                nc.vector.tensor_tensor(dest[n][:, :, :], dest[n][:, :, :], top[:, :, :], ALU.subtract).then_inc(ready, 1)
            if two:
                dve.wait_ge(home, 14)
                nc.vector.tensor_tensor(coef[:, 0:ST, 8:16], coef[:, 0:ST, 8:16],
                                        marks.first[:, :].unsqueeze(2).to_broadcast([P, ST, 8]), ALU.mult)


class Sink:

    def __init__(self, dram, col, width):
        self.dram, self.col, self.width = dram, col, width


def project(nc, k, tag, src, width, weights, bias, sinks, evac, out_width=None, post=None, post_steps=0, extra=None,
            scatter=None, scatter_rounds=0):
    chunks = [(c, min(512, width - c)) for c in range(0, width, 512)]
    nch, na, nv = len(chunks), evac.count("a"), evac.count("v")
    with Phase(nc, tag) as ph:
        own_w = isinstance(weights, list)
        w = ph.sb("w", [P, 2, width]) if own_w else weights
        b = ph.sb("b", [P, width]) if bias else None
        copy = [ph.sb(f"copy{u}", [P, C]) for u in range(SLOTS)]
        turned = [ph.sb(f"turned{u}", [P, 2, P]) for u in range(SLOTS)]
        out = [ph.sb(f"out{u}", [P, out_width or width]) for u in range(SLOTS)]
        turn_p = [ph.ps(f"turn_p{n}", [P, 512]) for n in range(3)]
        prod = [ph.ps(f"prod{u}", [P, 512]) for u in range(SLOTS)]
        loaded, copied, turn, moved, multiplied, read_a, read_v, own, posted = (
            ph.sem(n) for n in ("loaded", "copied", "turn", "moved", "multiplied", "read_a", "read_v", "own", "posted"))
        stored = [ph.sem(f"stored{u}") for u in range(SLOTS)]
        bufs = extra(ph) if extra else None
        loads = ([(w[:, :, c:c + m], a.rearrange("(c p) m -> p c m", p=P)) for a, c, m in weights] if own_w else [])
        loads += [(b[:, c:c + m], a.partition_broadcast(P)) for a, c, m in (bias or [])]
        loads += bufs.loads if bufs else []
        block = ph.block()
        if scatter:
            scatter.beside(nc, ph, block, scatter_rounds)

        def out_free(eng, i, u):
            if not sinks:
                return
            after(eng, stored[u], i * 16 * len(sinks))

        @block.sync
        def _(sp):
            for dst, a in loads:
                sp.dma_start(dst, a).then_inc(loaded, 16)

            def body(i):
                for u in range(SLOTS):
                    t = i * SLOTS + u
                    if na:
                        sp.wait_ge(read_a, (t + 1) * na)
                    if nv:
                        sp.wait_ge(read_v, (t + 1) * nv)
                    if post:
                        sp.wait_ge(posted, t + 1)
                    for s in sinks:
                        sp.dma_start(s.dram[bass.ds(t * P, P), :], out[u][:, s.col:s.col + s.width]).then_inc(stored[u], 16)

            if sinks:
                rounds(sp, ROUNDS, body)
                for u in range(SLOTS):
                    sp.wait_ge(stored[u], ROUNDS * 16 * len(sinks))

        @block.scalar
        def _(act):
            def move(t, u):
                act.wait_ge(turn, t + 1)
                after(act, multiplied, (t - SLOTS + 1) * nch)
                nc.scalar.activation(turned[u][:, :, :].rearrange("p c n -> p (c n)"), turn_p[u % 3][:, 0:C],
                                     ACT.Copy).then_inc(moved, 1)

            def read(i, t, u):
                if not na:
                    return
                out_free(act, i, u)
                for n, (c, m) in enumerate(chunks):
                    if evac[n] == "a":
                        act.wait_ge(multiplied, t * nch + n + 1)
                        nc.scalar.activation(out[u][:, c:c + m], prod[(u * nch + n) % SLOTS][:, 0:m], ACT.Copy).then_inc(read_a, 1)

            def body(i):
                for u in range(SLOTS):
                    t = i * SLOTS + u
                    after(act, turn, t - SLOTS + 1)
                    nc.scalar.activation(copy[u][:, :], src[:, bass.ds(t, 1), :].rearrange("p t c -> p (t c)"),
                                         ACT.Copy).then_inc(copied, 1)
                    if not (isinstance(t, int) and t < 1):
                        move(t - 1, (u - 1) % SLOTS)
                    if not (isinstance(t, int) and t < 2):
                        read(i if u >= 2 else i - 1, t - 2, (u - 2) % SLOTS)

            rounds(act, ROUNDS, body)
            move(NT - 1, SLOTS - 1)
            read(ROUNDS - 1, NT - 2, SLOTS - 2)
            read(ROUNDS - 1, NT - 1, SLOTS - 1)

        @block.tensor
        def _(pe):
            pe.wait_ge(loaded, 16 * len(loads)) if loads else None

            def multiply(t, u):
                pe.wait_ge(moved, t + 1)
                for n, (c, m) in enumerate(chunks):
                    lin = u * nch + n - SLOTS
                    t2, n2 = (t - u + lin // nch, lin % nch)
                    kind = evac[n2]
                    sem, per, upto = ((read_a, na, evac[:n2 + 1].count("a")) if kind == "a"
                                      else (read_v, nv, evac[:n2 + 1].count("v")))
                    after(pe, sem, t2 * per + upto)
                    for c2 in range(2):
                        last = nc.tensor.matmul(prod[(u * nch + n) % SLOTS][:, 0:m], turned[u][:, c2, :], w[:, c2, c:c + m],
                                                start=(c2 == 0), stop=(c2 == 1))
                    last.then_inc(multiplied, 1)

            def body(i):
                for u in range(SLOTS):
                    t = i * SLOTS + u
                    pe.wait_ge(copied, t + 1)
                    after(pe, moved, t - 1)
                    for c2 in range(2):
                        last = nc.tensor.transpose(turn_p[u % 3][:, c2 * P:(c2 + 1) * P], copy[u][:, c2 * P:(c2 + 1) * P],
                                                   k.ident[:, :])
                    last.then_inc(turn, 1)
                    if not (isinstance(t, int) and t < 1):
                        multiply(t - 1, (u - 1) % SLOTS)

            rounds(pe, ROUNDS, body)
            multiply(NT - 1, SLOTS - 1)

        @block.vector
        def _(dve):
            if bias or post:
                dve.wait_ge(loaded, 16 * len(loads))

            def body(i):
                for u in range(SLOTS):
                    t = i * SLOTS + u
                    if nv:
                        out_free(dve, i, u)
                    for n, (c, m) in enumerate(chunks):
                        if evac[n] == "v":
                            dve.wait_ge(multiplied, t * nch + n + 1)
                            p = prod[(u * nch + n) % SLOTS][:, 0:m]
                            ins = (nc.vector.tensor_tensor(out[u][:, c:c + m], p, b[:, c:c + m], ALU.add) if bias
                                   else nc.vector.tensor_copy(out[u][:, c:c + m], p))
                            ins.then_inc(read_v, 1)
                    if post:
                        if na:
                            dve.wait_ge(read_a, (t + 1) * na)
                        if nv:
                            dve.wait_ge(read_v, (t + 1) * nv)
                        out_free(dve, i, u)
                        start = t * post_steps
                        step = Chain(dve, own, start)
                        post(dve, step, t, out[u], bufs)
                        nc.vector.memset(bufs.tick[:, :], 0.0).then_inc(posted, 1)

            rounds(dve, ROUNDS, body)


class Extra:
    pass


def fold_heads(nc, step, out, a, b, tmp, heads):
    step(nc.vector.tensor_tensor(tmp, a, b, ALU.mult))
    step(nc.vector.tensor_reduce(out, tmp.rearrange("p (h d) -> p h d", h=heads), AX.X, ALU.add))


def flat_tile(a, t):
    return a[:, bass.ds(t, 1), :].rearrange("p t c -> p (t c)")


class Norm:

    def __init__(self, ph):
        self.stats = ph.sb("stats", [P, NT, 6])
        self.mean, self.var, self.tmp = (ph.sb(n, [P, NT]) for n in ("row_mean", "row_var", "row_tmp"))
        self.varied, self.rooted, self.scaled = (ph.sem(n) for n in ("row_varied", "row_rooted", "row_scaled"))

    def dve(self, nc, dve, step, x, y, gain=None, bias=None):
        with dve.Fori(0, ROUNDS) as i:
            for u in range(SLOTS):
                nc.vector.bn_stats(flat_tile(self.stats, i * SLOTS + u), flat_tile(x, i * SLOTS + u)).then_inc(self.scaled, 1)
        dve.wait_ge(self.scaled, NT)
        st = self.stats
        step(nc.vector.tensor_tensor(self.mean[:, :], st[:, :, 1], st[:, :, 4], ALU.add))
        step(nc.vector.tensor_scalar(self.mean[:, :], self.mean[:, :], 0.5, None, ALU.mult))
        step(nc.vector.tensor_tensor(self.tmp[:, :], st[:, :, 1], st[:, :, 4], ALU.subtract))
        step(nc.vector.scalar_tensor_tensor(self.tmp[:, :], self.tmp[:, :], 0.25, self.tmp[:, :], ALU.mult, ALU.mult))
        step(nc.vector.tensor_tensor(self.var[:, :], st[:, :, 2], st[:, :, 5], ALU.add))
        step(nc.vector.scalar_tensor_tensor(self.var[:, :], self.var[:, :], 1.0 / C, self.tmp[:, :], ALU.mult, ALU.add))
        nc.vector.tensor_scalar(self.var[:, :], self.var[:, :], EPS, None, ALU.add).then_inc(self.varied, 1)
        dve.wait_ge(self.rooted, 1)
        step(nc.vector.reciprocal(self.var[:, :], self.var[:, :]))
        with dve.Fori(0, ROUNDS) as i:
            for u in range(SLOTS):
                t = i * SLOTS + u
                nc.vector.tensor_scalar(flat_tile(y, t), flat_tile(x, t), self.mean[:, bass.ds(t, 1)],
                                        self.var[:, bass.ds(t, 1)], ALU.subtract, ALU.mult).then_inc(self.scaled, 1)
        dve.wait_ge(self.scaled, 2 * NT)
        if gain is not None:
            step(nc.vector.tensor_tensor(y[:, :, :], y[:, :, :], gain[:, :].unsqueeze(1).to_broadcast([P, NT, C]), ALU.mult))
            step(nc.vector.tensor_tensor(y[:, :, :], y[:, :, :], bias[:, :].unsqueeze(1).to_broadcast([P, NT, C]), ALU.add))

    def act(self, nc, act):
        act.wait_ge(self.varied, 1)
        nc.scalar.activation(self.var[:, :], self.var[:, :], ACT.Sqrt).then_inc(self.rooted, 1)


def node_rows(dram, width=C):
    return dram.rearrange("(t p) c -> p t c", p=P)


def attend_update(nc, k, tag, acc, heads, x, guard, residual=None, scatter=None):
    with Phase(nc, tag) as ph:
        norm = Norm(ph)
        hp = ph.sb("hp", [P, NT, C])
        res = ph.sb("res", [P, NT, C]) if residual is not None else None
        pad = ph.sb("pad", [P, 1])
        own, loaded, divided, raised = (ph.sem(n) for n in ("own", "loaded", "divided", "raised"))
        block = ph.block()
        if scatter:
            scatter.beside(nc, ph, block, 2)

        @block.sync
        def _(sp):
            if residual is not None:
                sp.dma_start(res[:, :, :], node_rows(residual)).then_inc(loaded, 16)

        @block.scalar
        def _(act):
            act.wait_ge(divided, 1)
            nc.scalar.activation(acc[:, :, 0:C], acc[:, :, 0:C], ACT.Exp).then_inc(raised, 1)
            norm.act(nc, act)

        @block.vector
        def _(dve):
            step = Chain(dve, own)
            z = acc[:, :, C:C + heads]
            if guard:
                step(nc.vector.tensor_scalar(z, z, guard, None, ALU.add))
            else:
                step(nc.vector.tensor_scalar(pad[:, :], k.row[:, :], float(NL), None, ALU.is_ge))
                step(nc.vector.tensor_scalar(acc[:, NT - 1, C:C + heads], acc[:, NT - 1, C:C + heads], pad[:, 0:1], None, ALU.add))
            step(nc.vector.reciprocal(z, z))
            step(nc.vector.tensor_tensor(hp[:, :, :].rearrange("p t (h d) -> p t h d", h=heads),
                                         acc[:, :, 0:C].rearrange("p t (h d) -> p t h d", h=heads),
                                         z.unsqueeze(3).to_broadcast([P, NT, heads, C // heads]), ALU.mult))
            nc.vector.tensor_scalar(acc[:, :, 0:C], hp[:, :, :], 0.0, None, ALU.min).then_inc(divided, 1)
            dve.wait_ge(raised, 1)
            step(nc.vector.scalar_tensor_tensor(hp[:, :, :], hp[:, :, :], 0.0, acc[:, :, 0:C], ALU.max, ALU.add))
            if residual is not None:
                dve.wait_ge(loaded, 16)
                step(nc.vector.scalar_tensor_tensor(hp[:, :, :], hp[:, :, :], -1.0, res[:, :, :], ALU.add, ALU.add))
                step(nc.vector.tensor_tensor(x[:, :, :], x[:, :, :], hp[:, :, :], ALU.add))
            else:
                step(nc.vector.scalar_tensor_tensor(x[:, :, :], hp[:, :, :], -1.0, x[:, :, :], ALU.add, ALU.add))
            norm.dve(nc, dve, step, x, x)


def norm_into(nc, tag, x, y, gain=None, bias=None, add=None, add_dram=None):
    with Phase(nc, tag) as ph:
        norm = Norm(ph)
        own, loaded = ph.sem("own"), ph.sem("loaded")
        g = ph.sb("g", [P, C]) if gain is not None else None
        b = ph.sb("b", [P, C]) if gain is not None else None
        loads = [(g[:, :], gain.partition_broadcast(P)), (b[:, :], bias.partition_broadcast(P))] if gain is not None else []
        if add_dram is not None:
            loads.append((add[:, :, :], node_rows(add_dram)))
        block = ph.block()

        @block.sync
        def _(sp):
            for dst, a in loads:
                sp.dma_start(dst, a).then_inc(loaded, 16)

        @block.scalar
        def _(act):
            norm.act(nc, act)

        @block.vector
        def _(dve):
            step = Chain(dve, own)
            if loads:
                dve.wait_ge(loaded, 16 * len(loads))
            if add is not None:
                step(nc.vector.tensor_tensor(y[:, :, :], x[:, :, :], add[:, :, :], ALU.add))
            norm.dve(nc, dve, step, x if add is None else y, y, g, b)


def feed_forward(nc, k, tag, y, h, w1, b1, w2, b2):
    FF = w1.shape[1]
    F = FF // P
    with Phase(nc, tag) as ph:
        w1_s = ph.sb("w1", [P, 2, FF])
        w2_s = ph.sb("w2", [P, F, C])
        b1_s = ph.sb("b1", [P, F])
        b2_s = ph.sb("b2", [P, C])
        copy = [ph.sb(f"copy{u}", [P, C]) for u in range(SLOTS)]
        turned = [ph.sb(f"turned{u}", [P, 2, P]) for u in range(SLOTS)]
        inner = [ph.sb(f"inner{u}", [P, F, P]) for u in range(SLOTS)]
        turn_p = [ph.ps(f"turn_p{n}", [P, 512]) for n in range(2)]
        up = [ph.ps(f"up{n}", [P, F // 2, P]) for n in range(4)]
        down = [ph.ps(f"down{n}", [P, 512]) for n in range(2)]
        loaded, copied, turn, moved, raised, bent, lowered, added, own = (
            ph.sem(n) for n in ("loaded", "copied", "turn", "moved", "raised", "bent", "lowered", "added", "own"))
        block = ph.block()

        @block.sync
        def _(sp):
            for dst, a in ((w1_s[:, :, :], w1.rearrange("(c p) f -> p c f", p=P)),
                           (w2_s[:, :, :], w2.rearrange("(f p) c -> p f c", p=P)),
                           (b1_s[:, :], b1.rearrange("(f p) -> p f", p=P)), (b2_s[:, :], b2.partition_broadcast(P))):
                sp.dma_start(dst, a, allow_slow_non_contiguous=True).then_inc(loaded, 16)

        def pair(u):
            return u % 2

        @block.scalar
        def _(act):
            act.wait_ge(loaded, 64)

            def bend(t, u):
                after(act, lowered, t - SLOTS + 1)
                for f in range(F):
                    act.wait_ge(raised, (2 * t + f // (F // 2) + 1))
                    last = nc.scalar.activation(inner[u][:, f, :], up[2 * pair(u) + f // (F // 2)][:, f % (F // 2), :],
                                                ACT.Gelu, bias=b1_s[:, f:f + 1])
                    if f % (F // 2) == F // 2 - 1:
                        last.then_inc(bent, 1)

            def body(i):
                for u in range(SLOTS):
                    t = i * SLOTS + u
                    after(act, turn, t - SLOTS + 1)
                    nc.scalar.activation(copy[u][:, :], flat_tile(y, t), ACT.Copy).then_inc(copied, 1)
                    if not (isinstance(t, int) and t < 1):
                        bend(t - 1, (u - 1) % SLOTS)

            rounds(act, ROUNDS, body)
            bend(NT - 1, SLOTS - 1)

        @block.tensor
        def _(pe):
            pe.wait_ge(loaded, 64)

            def lower(t, u):
                pe.wait_ge(bent, 2 * t + 2)
                after(pe, added, t - 1 if u else t)
                for f in range(F):
                    last = nc.tensor.matmul(down[pair(u)][:, 0:C], inner[u][:, f, :], w2_s[:, f, :], start=(f == 0), stop=(f == F - 1))
                last.then_inc(lowered, 1)

            def body(i):
                for u in range(SLOTS):
                    t = i * SLOTS + u
                    pe.wait_ge(copied, t + 1)
                    after(pe, moved, t)
                    for c in range(2):
                        last = nc.tensor.transpose(turn_p[pair(u)][:, c * P:(c + 1) * P], copy[u][:, c * P:(c + 1) * P], k.ident[:, :])
                    last.then_inc(turn, 1)
                    pe.wait_ge(moved, t + 1)
                    for half in range(2):
                        after(pe, bent, (t if u == 0 else t - 1) * 2)
                        for f in range(half * F // 2, (half + 1) * F // 2):
                            for c in range(2):
                                last = nc.tensor.matmul(up[2 * pair(u) + half][:, f % (F // 2), :], w1_s[:, c, f * P:(f + 1) * P],
                                                        turned[u][:, c, :], start=(c == 0), stop=(c == 1))
                        last.then_inc(raised, 1)
                    if not (isinstance(t, int) and t < 1):
                        lower(t - 1, (u - 1) % SLOTS)

            rounds(pe, ROUNDS, body)
            lower(NT - 1, SLOTS - 1)

        @block.vector
        def _(dve):
            dve.wait_ge(loaded, 64)
            nc.vector.tensor_tensor(h[:, :, :], h[:, :, :], b2_s[:, :].unsqueeze(1).to_broadcast([P, NT, C]),
                                    ALU.add).then_inc(own, 1)
            dve.wait_ge(own, 1)

            def add(t, u):
                dve.wait_ge(lowered, t + 1)
                nc.vector.tensor_tensor(flat_tile(h, t), flat_tile(h, t), down[pair(u)][:, 0:C], ALU.add).then_inc(added, 1)

            def body(i):
                for u in range(SLOTS):
                    t = i * SLOTS + u
                    dve.wait_ge(turn, t + 1)
                    after(dve, raised, (t - SLOTS + 1) * 2)
                    nc.vector.tensor_copy(turned[u][:, :, :].rearrange("p c n -> p (c n)"), turn_p[pair(u)][:, 0:C]).then_inc(moved, 1)
                    if not (isinstance(t, int) and t < 2):
                        add(t - 2, (u - 2) % SLOTS)

            rounds(dve, ROUNDS, body)
            add(NT - 2, SLOTS - 2)
            add(NT - 1, SLOTS - 1)


def self_attend(nc, tag, acc, v_dram):
    with Phase(nc, tag) as ph:
        v = ph.sb("v", [P, NT, C])
        own, loaded = ph.sem("own"), ph.sem("loaded")
        block = ph.block()

        @block.sync
        def _(sp):
            sp.dma_start(v[:, :, :], node_rows(v_dram)).then_inc(loaded, 16)

        @block.vector
        def _(dve):
            step = Chain(dve, own)
            heads = lambda a: a.rearrange("p t (h d) -> p t h d", h=8)
            z, w = acc[:, :, C:C + 8], acc[:, :, C + 8:C + 16]
            step(nc.vector.tensor_tensor(z, z, w, ALU.add))
            step(nc.vector.tensor_scalar(z, z, 0.5, None, ALU.max))
            step(nc.vector.reciprocal(z, z))
            dve.wait_ge(loaded, 16)
            step(nc.vector.tensor_tensor(heads(v[:, :, :]), heads(v[:, :, :]), w.unsqueeze(3).to_broadcast([P, NT, 8, C // 8]), ALU.mult))
            step(nc.vector.tensor_tensor(acc[:, :, 0:C], acc[:, :, 0:C], v[:, :, :], ALU.add))
            step(nc.vector.tensor_tensor(heads(acc[:, :, 0:C]), heads(acc[:, :, 0:C]), z.unsqueeze(3).to_broadcast([P, NT, 8, C // 8]), ALU.mult))


def move(nc, tag, pairs):
    with Phase(nc, tag) as ph:
        done = ph.sem("done")
        block = ph.block()

        @block.sync
        def _(sp):
            for dst, src in pairs:
                sp.dma_start(dst, src).then_inc(done, 16)
            sp.wait_ge(done, 16 * len(pairs))


def load_nodes(nc, x, dram):
    with Phase(nc, "load") as ph:
        done, blank = ph.sem("done"), ph.sem("blank")
        block = ph.block()

        @block.vector
        def _(dve):
            nc.vector.memset(x[:, NT - 1:NT, :], 0.0).then_inc(blank, 1)

        @block.sync
        def _(sp):
            full = (NT - 1) * P
            sp.dma_start(x[:, 0:NT - 1, :], dram[0:full, :].rearrange("(t p) c -> p t c", p=P)).then_inc(done, 16)
            sp.wait_ge(blank, 1)
            sp.dma_start(x[0:NL, NT - 1, :], dram[full:N, :]).then_inc(done, 16)
            sp.wait_ge(done, 32)


def turn_weights(nc, k, w_dram, w):
    with Phase(nc, "w0") as ph:
        rows = ph.sb("rows", [P, 2, C])
        bank = ph.ps("bank", [P, 4, P])
        loaded, turn = ph.sem("loaded"), ph.sem("turn")
        block = ph.block()

        @block.sync
        def _(sp):
            sp.dma_start(rows[:, :, :], w_dram.rearrange("h d c -> d h c")).then_inc(loaded, 16)

        @block.tensor
        def _(pe):
            pe.wait_ge(loaded, 16)
            for c in range(2):
                for h in range(2):
                    last = nc.tensor.transpose(bank[:, 2 * c + h, :], rows[:, h, c * P:(c + 1) * P], k.ident[:, :])
            last.then_inc(turn, 1)

        @block.vector
        def _(dve):
            dve.wait_ge(turn, 1)
            nc.vector.tensor_copy(w[:, :, :].rearrange("p c m -> p (c m)"), bank[:, :, :].rearrange("p a b -> p (a b)"))


def batch_norm_out(nc, k, acc, x, gamma, beta, out):
    with Phase(nc, "bn") as ph:
        norm = Norm(ph)
        g, b = ph.sb("g", [P, C]), ph.sb("b", [P, C])
        mean, scale = ph.sb("node_mean", [P, C]), ph.sb("node_scale", [P, C])
        sq = ph.sb("sq", [P, NT, C])
        col, total = ph.sb("col", [P, C]), ph.ps("total", [P, 2, C])
        pad = ph.sb("pad", [P, 1])
        own, loaded, folded, summed, varied, rooted, ready, stored = (
            ph.sem(n) for n in ("own", "loaded", "folded", "summed", "varied", "rooted", "ready", "stored"))
        block = ph.block()

        @block.sync
        def _(sp):
            sp.dma_start(g[:, :], gamma.partition_broadcast(P)).then_inc(loaded, 16)
            sp.dma_start(b[:, :], beta.partition_broadcast(P)).then_inc(loaded, 16)
            sp.wait_ge(ready, 1)
            full = (NT - 1) * P
            sp.dma_start(out[0:full, :].rearrange("(t p) c -> p t c", p=P), x[:, 0:NT - 1, :]).then_inc(stored, 16)
            sp.dma_start(out[full:N, :], x[0:NL, NT - 1, :]).then_inc(stored, 16)
            sp.wait_ge(stored, 32)

        @block.tensor
        def _(pe):
            for n in range(2):
                pe.wait_ge(folded, n + 1)
                nc.tensor.matmul(total[:, n, :], k.ones[:, :], col[:, :], start=True, stop=True).then_inc(summed, 1)

        @block.scalar
        def _(act):
            act.wait_ge(varied, 1)
            nc.scalar.activation(scale[:, :], scale[:, :], ACT.Sqrt).then_inc(rooted, 1)
            norm.act(nc, act)

        @block.vector
        def _(dve):
            step = Chain(dve, own)
            wide = lambda a: a[:, :].unsqueeze(1).to_broadcast([P, NT, C])
            nc.vector.tensor_reduce(col[:, :], acc[:, :, :].rearrange("p t c -> p c t"), AX.X, ALU.add).then_inc(folded, 1)
            step(nc.vector.tensor_scalar(pad[:, :], k.row[:, :], float(NL), None, ALU.is_lt))
            dve.wait_ge(summed, 1)
            step(nc.vector.tensor_scalar(mean[:, :], total[:, 0, :], 1.0 / N, None, ALU.mult))
            step(nc.vector.tensor_tensor(acc[:, :, :], acc[:, :, :], wide(mean), ALU.subtract))
            step(nc.vector.tensor_scalar(acc[:, NT - 1, :], acc[:, NT - 1, :], pad[:, 0:1], None, ALU.mult))
            step(nc.vector.tensor_tensor(sq[:, :, :], acc[:, :, :], acc[:, :, :], ALU.mult))
            nc.vector.tensor_reduce(col[:, :], sq[:, :, :].rearrange("p t c -> p c t"), AX.X, ALU.add).then_inc(folded, 1)
            dve.wait_ge(summed, 2)
            nc.vector.tensor_scalar(scale[:, :], total[:, 1, :], 1.0 / N, EPS, ALU.mult, ALU.add).then_inc(varied, 1)
            dve.wait_ge(rooted, 1)
            step(nc.vector.reciprocal(scale[:, :], scale[:, :]))
            dve.wait_ge(loaded, 32)
            step(nc.vector.tensor_tensor(scale[:, :], scale[:, :], g[:, :], ALU.mult))
            step(nc.vector.tensor_tensor(acc[:, :, :], acc[:, :, :], wide(scale), ALU.mult))
            step(nc.vector.tensor_tensor(x[:, :, :], x[:, :, :], acc[:, :, :], ALU.add))
            step(nc.vector.tensor_tensor(x[:, :, :], x[:, :, :], wide(b), ALU.add))
            norm.dve(nc, dve, step, x, x)
            nc.vector.memset(pad[:, :], 0.0).then_inc(ready, 1)


def first_layer(nc, k, t, x, scratch, by_src, by_dst, tile_of, tile_row):
    with Phase(nc, "l0") as h:
        rows = scratch("rows0", (NP, C + 2))
        index, local = h.sb("index", [P, STP], i32), h.sb("local", [P, STP])
        s_src = h.sb("s_src", [P, NT, 2])
        acc = h.sb("acc", [P, NT, C + 2])
        with Phase(nc, "p0") as ph:
            w = ph.sb("w", [P, 2, C])
            turn_weights(nc, k, t["L0_gnn_W"], w)

            def extra(ph):
                e = Extra()
                e.a, e.tmp, e.tick = ph.sb("a", [P, 2, C]), ph.sb("tmp", [P, C]), ph.sb("tick", [P, 1])
                a = t["L0_gnn_a"]
                e.loads = [(e.a[:, s, :].rearrange("p (h d) -> p h d", h=2), a[:, s * P:(s + 1) * P].partition_broadcast(P))
                           for s in range(2)]
                return e

            def post(dve, step, tile, out, e):
                fold_heads(nc, step, s_src[:, bass.ds(tile, 1), :].rearrange("p t c -> p (t c)"), out[:, 0:C], e.a[:, 0, :], e.tmp[:, :], 2)
                fold_heads(nc, step, out[:, C:C + 2], out[:, 0:C], e.a[:, 1, :], e.tmp[:, :], 2)

            project(nc, k, "proj0", x, C, w, [(t["L0_gnn_b"].rearrange("h d -> (h d)"), 0, C)], [Sink(rows, 0, C + 2)], "v",
                    C + 2, post, 4, extra, by_src, by_src.ROUNDS)
        load_order(nc, k, "srcload", by_src.table, tile_of, [index], local)
        by_source_pass(nc, k, "edge0", (local, tile_row, index, rows), s_src, acc)
        attend_update(nc, k, "up0", acc, 2, x, 0, None, by_dst)


def build(nc, t, out, scratch):
    Phase.used = []
    with Phase(nc, "all") as hold:
        k = make_constants(nc, hold)
        x_dram = scratch("x_rows", (NP, C))
        tile_of, tile_row = hold.sb("tile_of", [P, STP]), hold.sb("tile_row", [1, STP // U], i32)
        index, rel_index = hold.sb("index", [P, STP], i32), hold.sb("rel_index", [P, STP], i32)
        local = hold.sb("local", [P, STP])
        x = hold.sb("x", [P, NT, C])
        marks = Marks(hold)
        xl, res, al = scratch("xl_rows", (NP, C)), scratch("res_rows", (NP, C)), scratch("al_rows", (NP, 8))
        load_nodes(nc, x, t["x"])
        with Phase(nc, "front") as front:
            src_tile_of, src_tile_row = front.sb("tile_of", [P, STP]), front.sb("tile_row", [1, STP // U], i32)
            by_dst = Scatter(front, "dst", scratch("table_dst", (P * ST, 4), i32))
            by_src = Scatter(front, "src", scratch("table_src", (P * ST, 4), i32))
            sort_edges(nc, k, "src", t["src"], t["dst"], None, None, by_src, src_tile_of, src_tile_row)
            sort_edges(nc, k, "dst", t["dst"], t["src"], t["edge_type_8"], t["edge_weight"], by_dst, tile_of, tile_row, by_src)
            first_layer(nc, k, t, x, scratch, by_src, by_dst, src_tile_of, src_tile_row)
            with Phase(nc, "l1s") as ph:
                right = ph.sb("right", [P, NT, 8])
                second_rows(nc, k, t, x, right, xl, res, al, by_dst)
                by_dst.rest(nc)
                load_order(nc, k, "dstload", by_dst.table, tile_of, [index, rel_index], local, marks)
                coef = ph.sb("coef", [P, STP, 8])
                with Phase(nc, "l1a") as pa:
                    score = pa.sb("score", [P, ST, 8])
                    alpha_pass(nc, k, "edge1a", (local, tile_row, index, al), right, score)
                    segment_softmax(nc, k, "soft1", marks, score, coef)
                acc = ph.sb("acc", [P, NT, C + 8])
                sum_pass(nc, k, "edge1b", (local, tile_row, index, xl), acc, coef, 8)
                attend_update(nc, k, "up1", acc, 8, x, 1e-16, res)
        move(nc, "keep2", [(node_rows(x_dram), x[:, :, :])])
        third_layer(nc, k, t, x, x_dram, scratch, marks, index, local, tile_row)
        with Phase(nc, "last") as last:
            rel_rows = scratch("rel_rows", (NP * 8, C))
            wide = rel_rows.rearrange("(n r) c -> n (r c)", r=8)
            project(nc, k, "proj3", x, 8 * C, [(t["L3_gnn_weight"][r], r * C, C) for r in range(8)], None,
                    [Sink(wide, 0, 8 * C)], "avav")
            acc = last.sb("acc", [P, NT, C])
            sum_pass(nc, k, "edge3", (local, tile_row, rel_index, rel_rows), acc)
            batch_norm_out(nc, k, acc, x, t["L3_gnn_gamma"], t["L3_gnn_beta"], out)


def second_rows(nc, k, t, x, right, xl, res, al, by_dst):
    def extra(ph):
        e = Extra()
        e.att, e.tmp, e.tick = ph.sb("att", [P, 2, C]), ph.sb("tmp", [P, C]), ph.sb("tick", [P, 1])
        e.loads = [(e.att[:, n, :], t[a].rearrange("a h d -> (a h d)").partition_broadcast(P))
                   for n, a in enumerate(("L1_gnn_att_l", "L1_gnn_att_r"))]
        return e

    def post(dve, step, tile, out, e):
        fold_heads(nc, step, out[:, 2 * C:2 * C + 8], out[:, 0:C], e.att[:, 0, :], e.tmp[:, :], 8)
        fold_heads(nc, step, flat_tile(right, tile), out[:, 0:C], e.att[:, 1, :], e.tmp[:, :], 8)

    project(nc, k, "proj1", x, 2 * C, [(t["L1_gnn_W_lin"], 0, C), (t["L1_gnn_W_res"], C, C)], None,
            [Sink(xl, 0, C), Sink(res, C, C), Sink(al, 2 * C, 8)], "a", 2 * C + 8, post, 4, extra, by_dst, 2)


def third_layer(nc, k, t, h, x_dram, scratch, marks, index, local, tile_row):
    w = lambda name: t["L2_gnn_" + name]
    k_rows, v_rows = (scratch(n, (NP, C)) for n in ("k_rows", "v_rows"))

    def ticker(ph):
        e = Extra()
        e.tmp, e.tick, e.loads = ph.sb("tmp", [P, C]), ph.sb("tick", [P, 1]), []
        return e

    def replace(dve, step, tile, out, e):
        step(nc.vector.tensor_copy(flat_tile(h, tile), out[:, 0:C]))

    def add(dve, step, tile, out, e):
        step(nc.vector.tensor_tensor(flat_tile(h, tile), flat_tile(h, tile), out[:, 0:C], ALU.add))

    project(nc, k, "proj2in", h, C, [(w("w_in"), 0, C)], [(w("b_in"), 0, C)], [], "v", None, replace, 1, ticker)
    for l in range(2):
        with Phase(nc, f"l2_{l}") as layer:
            coef = layer.sb("coef", [P, STP, 16])
            with Phase(nc, f"l2a_{l}") as ph:
                score, self_score = ph.sb("score", [P, ST, 8]), ph.sb("self_score", [P, ST, 8])
                with Phase(nc, f"l2q_{l}") as pq:
                    q = pq.sb("q", [P, NT, C + 8])
                    y = (coef[:, :, :].rearrange("p t c -> p (t c)")[:, 0:NT * C]
                         .rearrange("p (t c) -> p t c", c=C))
                    norm_into(nc, f"norm_a{l}", h, y, w("ln1_g")[l], w("ln1_b")[l])

                    def post(dve, step, tile, out, e):
                        own = flat_tile(q, tile)
                        step(nc.vector.tensor_scalar(own[:, 0:C], out[:, 0:C], 32 ** -0.5, None, ALU.mult))
                        fold_heads(nc, step, own[:, C:C + 8], own[:, 0:C], out[:, C:2 * C], e.tmp[:, :], 8)

                    project(nc, k, f"proj2_{l}", y, 3 * C, [(w(n)[l], c * C, C) for c, n in enumerate(("wq", "wk", "wv"))],
                            [(w(n)[l], c * C, C) for c, n in enumerate(("bq", "bk", "bv"))],
                            [Sink(k_rows, C, C), Sink(v_rows, 2 * C, C)], "vv", None, post, 3, ticker)
                    score_pass(nc, k, f"edge2a_{l}", (local, tile_row, index, k_rows), q, score, self_score)
                segment_softmax(nc, k, f"soft2_{l}", marks, score, coef, self_score)
            with Phase(nc, f"l2b_{l}") as ph:
                acc = ph.sb("acc", [P, NT, C + 16])
                sum_pass(nc, k, f"edge2b_{l}", (local, tile_row, index, v_rows), acc, coef, 8, 8)
                self_attend(nc, f"self_{l}", acc, v_rows)
                project(nc, k, f"proj2o_{l}", acc[:, :, 0:C], C, [(w("wo")[l], 0, C)], [(w("bo")[l], 0, C)],
                        [], "v", None, add, 1, ticker)
            with Phase(nc, f"l2f_{l}") as ph:
                y = ph.sb("y", [P, NT, C])
                norm_into(nc, f"norm_b{l}", h, y, w("ln2_g")[l], w("ln2_b")[l])
                feed_forward(nc, k, f"ffn_{l}", y, h, w("w1")[l], w("b1")[l], w("w2")[l], w("b2")[l])
    with Phase(nc, "l2out") as ph:
        before = ph.sb("before", [P, NT, C])
        norm_into(nc, "norm3", h, h, add=before, add_dram=x_dram)


def kernel(**inputs):
    import numpy as _np
    import concourse.bacc as _bacc
    from concourse import mybir as _mybir
    from concourse.bass_utils import run_bass_kernel_spmd as _run

    nc = _bacc.Bacc("TRN2", target_bir_lowering=False, num_devices=1)
    arrays, aps = {}, {}
    for name, value in inputs.items():
        a = _np.ascontiguousarray(value)
        arrays[f"in_{name}"] = a
        aps[name] = nc.dram_tensor(f"in_{name}", a.shape, _mybir.dt.from_np(a.dtype), kind="ExternalInput").ap()
    out = nc.dram_tensor("out", (N, C), _mybir.dt.float32, kind="ExternalOutput").ap()

    def scratch(name, shape, dt=_mybir.dt.float32):
        return nc.dram_tensor(name, shape, dt, kind="Internal").ap()

    build(nc, aps, out, scratch)
    r = _run(nc, [arrays], core_ids=[0])
    return r.results[0]["out"]
```

```python
from contextlib import ExitStack

import concourse.bass as bass
from concourse import mybir

fp32, bf16, i32 = mybir.dt.float32, mybir.dt.bfloat16, mybir.dt.int32
ALU = mybir.AluOpType
ACT = mybir.ActivationFunctionType
AX = mybir.AxisListType

P = 128
N = 3125
E = 53125
C = 256
NT = -(-N // P)
NL = N - (NT - 1) * P
NP = NT * P
EP = 125
ET = E // EP
U = 4
NB = 8
AHEAD = 3
HOTS = 4
ST = 448
SR = ST // (U * NB)
BT = 110
LASTB = BT - (SR - 1) * NB
assert (E + NT * (P - 1)) // P <= BT * U <= ST and BT % 2 == 0 and 2 < LASTB <= NB and ET * EP == E and SR * U * NB == ST
STP = ST + AHEAD * U
PACK = 32
NOKEY = 4095
BIG = 1e38
EPS = 1e-5
HIST = 17
LOOK = 5
SLOTS = 5
ROUNDS = NT // SLOTS


def after(eng, sem, value):
    if isinstance(value, int) and value <= 0:
        return
    eng.wait_ge(sem, value)


def rounds(eng, n, body):
    body(0)
    if n > 1:
        with eng.Fori(1, n) as i:
            body(i)


def edge_rounds(eng, body):
    body(0, NB)
    with eng.Fori(1, SR - 1) as i:
        body(i, NB)
    body(SR - 1, LASTB)


class Chain:

    def __init__(self, eng, sem, base=0):
        self.eng, self.sem, self.n = eng, sem, base

    def __call__(self, ins):
        self.n = self.n + 1
        ins.then_inc(self.sem, 1)
        self.eng.wait_ge(self.sem, self.n)


class Phase:
    used = []

    def __init__(self, nc, tag):
        self.nc, self.tag, self.ctx, self.sems = nc, tag, ExitStack(), []

    def __enter__(self):
        self.ctx.__enter__()
        return self

    def __exit__(self, *a):
        done = self.ctx.__exit__(*a)
        Phase.used += self.sems
        if len(Phase.used) > 120:
            Phase.clear(self.nc)
        return done

    @staticmethod
    def clear(nc):
        nc.clear_and_free_semaphores(Phase.used)
        nc.all_engine_barrier()
        Phase.used = []

    def sb(self, name, shape, dt=fp32):
        return self.ctx.enter_context(self.nc.sbuf_tensor(f"{self.tag}_{name}", shape, dt))

    def ps(self, name, shape, dt=fp32):
        return self.ctx.enter_context(self.nc.psum_tensor(f"{self.tag}_{name}", shape, dt))

    def sem(self, name):
        self.sems.append(self.nc.alloc_semaphore(f"{self.tag}_{name}"))
        return self.sems[-1]

    def block(self):
        return self.ctx.enter_context(self.nc.Block())


class Constants:
    pass


def make_constants(nc, hold):
    k = Constants()
    k.ident = hold.sb("ident", [P, P])
    k.ident_b = hold.sb("ident_b", [P, P], bf16)
    k.ramp = hold.sb("ramp", [P, P])
    k.ramp_b = hold.sb("ramp_b", [P, P], bf16)
    k.row = hold.sb("row", [P, 1])
    k.ones = hold.sb("ones", [P, P])
    k.before = hold.sb("before", [P, P])
    k.above = hold.sb("above", [P, P])
    k.upto = hold.sb("upto", [P, P])
    k.slots = hold.sb("slots", [P, ST])
    k.spread = hold.sb("spread", [8, 16, P])
    with Phase(nc, "const") as ph:
        diff = ph.sb("diff", [P, P], i32)
        ramp_i = ph.sb("ramp_i", [P, ST], i32)
        row_i = ph.sb("row_i", [P, 1], i32)
        spread_i = ph.sb("spread_i", [8, 16, P], i32)
        made = ph.sem("made")
        block = ph.block()

        @block.gpsimd
        def _(pool):
            nc.gpsimd.iota(diff[:, :], pattern=[[1, P]], base=0, channel_multiplier=-1)
            nc.gpsimd.iota(ramp_i[:, :], pattern=[[1, ST]], base=0, channel_multiplier=0)
            nc.gpsimd.iota(row_i[:, :], pattern=[[1, 1]], base=0, channel_multiplier=1)
            nc.gpsimd.iota(spread_i[:, :, :], pattern=[[-8, 16], [1, P]], base=0,
                           channel_multiplier=-1).then_inc(made, 1)
            nc.gpsimd.memset(k.ones[:, :], 1.0)

        @block.vector
        def _(dve):
            dve.wait_ge(made, 1)
            nc.vector.tensor_scalar(k.ident[:, :], diff[:, :], 0.0, None, ALU.is_equal)
            nc.vector.tensor_scalar(k.ident_b[:, :], diff[:, :], 0.0, None, ALU.is_equal)
            nc.vector.tensor_scalar(k.above[:, :], diff[:, :], 0.0, None, ALU.is_gt)
            nc.vector.tensor_scalar(k.upto[:, :], diff[:, :], 0.0, None, ALU.is_ge)
            nc.vector.tensor_scalar(k.before[:, :], diff[:, :], 0.0, None, ALU.is_lt)
            nc.vector.tensor_copy(k.ramp[:, :], ramp_i[:, 0:P])
            nc.vector.tensor_copy(k.ramp_b[:, :], ramp_i[:, 0:P])
            nc.vector.tensor_copy(k.slots[:, :], ramp_i[:, :])
            nc.vector.tensor_copy(k.row[:, :], row_i[:, :])
            nc.vector.tensor_scalar(k.spread[:, :, :], spread_i[:, :, :], 0.0, None, ALU.is_equal)
    return k


class Scatter:
    ROUNDS = ET // LOOK // SLOTS

    def __init__(self, hold, tag, table):
        self.tag, self.table, self.next = tag, table, 0
        self.stage_all = hold.sb(f"{tag}_stage_all", [EP, ET + LOOK, 5], i32)

    def piece(self, nc, ph, pool, n, ready=None):
        n = min(n, self.ROUNDS - self.next)
        if n < 1:
            return
        first, table, stage_all = self.next * SLOTS, self.table, self.stage_all
        self.next += n
        stage = ph.sb(self.tag + "_put_stage", [EP, SLOTS, LOOK, 5], i32)
        staged = ph.sem(self.tag + "_put_staged")
        put = [ph.sem(f"{self.tag}_put{u}") for u in range(SLOTS)]
        if ready:
            pool.wait_ge(ready, 1)
        nc.gpsimd.tensor_copy(stage[:, 0, :, :], stage_all[:, first * LOOK:(first + 1) * LOOK, :]).then_inc(staged, 1)

        def body(i):
            for u in range(SLOTS):
                g, v = i * SLOTS + u, (u + 1) % SLOTS
                after(pool, put[v], (i + (1 if v == 0 else 0)) * 16 * LOOK)
                pool.wait_ge(staged, g + 1)
                if ready and v == 0:
                    pool.wait_ge(ready, i + 2)
                nc.gpsimd.tensor_copy(stage[:, v, :, :],
                                      stage_all[:, bass.ds((g + first + 1) * LOOK, LOOK), :]).then_inc(staged, 1)
                for j in range(LOOK):
                    pool.indirect_dma_start(
                        out=table[:, :], out_offset=bass.IndirectOffsetOnAxis(ap=stage[:, u, j, 0:1], axis=0),
                        in_=stage[:, u, j, 1:5], in_offset=None).then_inc(put[u], 16)

        rounds(pool, n, body)
        for u in range(SLOTS):
            pool.wait_ge(put[u], n * 16 * LOOK)


def scatter_beside(nc, ph, block, *pieces):
    @block.gpsimd
    def _(pool):
        for scatter, n in pieces:
            scatter.piece(nc, ph, pool, n)


def sort_edges(nc, k, tag, key, other, etype, weight, scatter, tile_of, tile_row, earlier=None, nodes=None):
    stage_all, table = scatter.stage_all, scatter.table
    arrays = [key, other] + ([etype, weight] if weight is not None else [])
    with ExitStack() as outer:
        def keep(name, shape, dt=fp32):
            return outer.enter_context(nc.sbuf_tensor(f"{tag}_{name}", shape, dt))

        key_c = keep("key_c", [EP, ET])
        count = keep("count", [P, ET + 1, NT])
        hi_hot = keep("hi_hot", [EP, ET, NT], bf16)

        with Phase(nc, tag + "_in") as ph:
            rows = [ph.sb(f"rows{n}", [P, 4, EP], i32) for n in range(len(arrays))]
            rows_f = [ph.sb(f"rows_f{n}", [P, 4, EP]) for n in range(len(arrays))]
            cols = [key_c] + [ph.sb(f"cols{n}", [EP, ET]) for n in range(1, len(arrays))]
            key_i = ph.sb("key_i", [EP, ET], i32)
            part_i = ph.sb("part_i", [EP, ET], i32)
            part_f = ph.sb("part_f", [EP, ET], bf16)
            relation = ph.sb("relation", [EP, ET])
            empty = ph.sb("empty", [P, ST, 4], i32)
            turned = [ph.ps(f"turned{n}", [EP, 512]) for n in range(len(arrays))]
            loaded, cast, turn, own, blank, wiped, fetched, padded = (
                ph.sem(n) for n in ("loaded", "cast", "turn", "own", "blank", "wiped", "fetched", "padded"))
            block = ph.block()
            full = ET // P * P

            @block.sync
            def _(sp):
                for n, a in enumerate(arrays):
                    src = a if a.dtype != fp32 else a.bitcast(i32)
                    sp.dma_start(rows[n][:, 0:3, :],
                                 src[0:full * EP].rearrange("(b p e) -> p b e", p=P, e=EP)).then_inc(loaded, 16)
                    sp.dma_start(rows[n][0:ET - full, 3, :],
                                 src[full * EP:E].rearrange("(p e) -> p e", e=EP)).then_inc(loaded, 16)
                if nodes:
                    x, dram = nodes
                    head = (NT - 1) * P
                    sp.dma_start(x[:, 0:NT - 1, :], dram[0:head, :].rearrange("(t p) c -> p t c", p=P)).then_inc(fetched, 16)
                    sp.wait_ge(padded, 1)
                    sp.dma_start(x[0:NL, NT - 1, :], dram[head:N, :]).then_inc(fetched, 16)
                sp.wait_ge(blank, 3)
                sp.dma_start(table.rearrange("(p t) w -> p t w", p=P), empty[:, :, :]).then_inc(wiped, 16)
                sp.wait_ge(wiped, 16)
                if nodes:
                    sp.wait_ge(fetched, 32)

            @block.gpsimd
            def _(pool):
                nc.gpsimd.memset(empty[:, :, :], 0).then_inc(blank, 1)
                pool.wait_ge(blank, 1)
                nc.gpsimd.memset(empty[:, :, 2:3], NOKEY).then_inc(blank, 2)
                if earlier:
                    earlier.piece(nc, ph, pool, 1)

            @block.vector
            def _(dve):
                if nodes:
                    nc.vector.memset(nodes[0][:, NT - 1:NT, :], 0.0).then_inc(padded, 1)
                dve.wait_ge(loaded, 32 * len(arrays))
                for n in range(len(arrays)):
                    for r, m in ((slice(0, 3), P), (slice(3, 4), ET - full)):
                        out, src = rows_f[n][0:m, r, :], rows[n][0:m, r, :]
                        if n == 3:
                            src = src.bitcast(fp32)
                        ins = nc.vector.tensor_copy(out, src)
                        ins.then_inc(cast, 1)
                step = Chain(dve, own)
                for n in range(len(arrays)):
                    dve.wait_ge(turn, n + 1)
                    step(nc.vector.tensor_copy(cols[n][:, :], turned[n][:, 0:ET]))
                step(nc.vector.tensor_copy(key_i[:, :], key_c[:, :]))
                step(nc.vector.tensor_scalar(part_i[:, :], key_i[:, :], 7, None, ALU.arith_shift_right))
                step(nc.vector.tensor_copy(part_f[:, :], part_i[:, :]))
                nc.vector.tensor_tensor(hi_hot[:, :, :], part_f[:, :].unsqueeze(2).to_broadcast([EP, ET, NT]),
                                        k.ramp_b[0:EP, 0:NT].unsqueeze(1).to_broadcast([EP, ET, NT]), ALU.is_equal)
                step(nc.vector.memset(stage_all[:, :, :], 0))
                nc.vector.tensor_copy(stage_all[:, 0:ET, 1], cols[1][:, :])
                nc.vector.tensor_copy(stage_all[:, 0:ET, 3], key_c[:, :])
                if weight is not None:
                    step(nc.vector.scalar_tensor_tensor(relation[:, :], cols[1][:, :], 8.0, cols[2][:, :],
                                                        ALU.mult, ALU.add))
                    nc.vector.tensor_copy(stage_all[:, 0:ET, 2], relation[:, :])
                    nc.vector.tensor_copy(stage_all[:, 0:ET, 4].bitcast(fp32), cols[3][:, :])

            @block.tensor
            def _(pe):
                for n in range(len(arrays)):
                    pe.wait_ge(cast, 2 * n + 2)
                    for b in range(4):
                        m = min(P, ET - b * P)
                        last = nc.tensor.transpose(turned[n][:, b * P:b * P + m], rows_f[n][0:m, b, :],
                                                   k.ident[0:m, 0:m])
                    last.then_inc(turn, 1)

        with Phase(nc, tag + "_hist") as ph:
            lo_hot = [ph.sb(f"lo_hot{u}", [EP, HIST, P], bf16) for u in range(SLOTS)]
            key_i = ph.sb("key_i", [EP, ET], i32)
            low_i = ph.sb("low_i", [EP, ET], i32)
            low = ph.sb("low", [EP, ET], bf16)
            sums = [ph.ps(f"sums{u}", [P, 512]) for u in range(SLOTS)]
            own, hot, summed, counted = (ph.sem(n) for n in ("own", "hot", "summed", "counted"))
            block = ph.block()
            assert ET // HIST == NT
            if earlier:
                scatter_beside(nc, ph, block, (earlier, 3))

            @block.vector
            def _(dve):
                step = Chain(dve, own)
                step(nc.vector.tensor_copy(key_i[:, :], key_c[:, :]))
                step(nc.vector.tensor_scalar(low_i[:, :], key_i[:, :], P - 1, None, ALU.bitwise_and))
                step(nc.vector.tensor_copy(low[:, :], low_i[:, :]))
                nc.vector.memset(count[:, 0:1, :], 0.0).then_inc(counted, 1)

                def accumulate(g, u):
                    dve.wait_ge(summed, g + 1)
                    dve.wait_ge(counted, g + 1)
                    nc.vector.tensor_tensor(
                        count[:, bass.ds(g * HIST + 1, HIST), :],
                        sums[u][:, 0:HIST * NT].rearrange("p (t h) -> p t h", h=NT),
                        count[:, bass.ds(g * HIST, 1), :].to_broadcast([P, HIST, NT]), ALU.add).then_inc(counted, 1)

                def body(i):
                    for u in range(SLOTS):
                        g = i * SLOTS + u
                        after(dve, summed, g - SLOTS + 1)
                        nc.vector.tensor_tensor(
                            lo_hot[u][:, :, :], low[:, bass.ds(g * HIST, HIST)].unsqueeze(2).to_broadcast([EP, HIST, P]),
                            k.ramp_b[0:EP, :].unsqueeze(1).to_broadcast([EP, HIST, P]), ALU.is_equal).then_inc(hot, 1)
                        if not (isinstance(g, int) and g == 0):
                            accumulate(g - 1, (u - 1) % SLOTS)

                rounds(dve, ET // HIST // SLOTS, body)
                accumulate(ET // HIST - 1, SLOTS - 1)

            @block.tensor
            def _(pe):
                def body(i):
                    for u in range(SLOTS):
                        g = i * SLOTS + u
                        pe.wait_ge(hot, g + 1)
                        after(pe, counted, g - SLOTS + 2)
                        for j in range(HIST):
                            n = HIST - j
                            last = nc.tensor.matmul(
                                sums[u][:, j * NT:HIST * NT].rearrange("p (t h) -> p t h", h=NT), lo_hot[u][:, j, :],
                                hi_hot[:, bass.ds(g * HIST + j, 1), :].to_broadcast([EP, n, NT]),
                                start=(j == 0), stop=(j == HIST - 1))
                        last.then_inc(summed, 1)

                rounds(pe, ET // HIST // SLOTS, body)

        with Phase(nc, tag + "_base") as ph:
            base = ph.sb("base", [P, NT])
            tiles_i = ph.sb("tiles_i", [P, NT], i32)
            tiles = ph.sb("tiles", [P, NT])
            ends = ph.sb("ends", [P, NT])
            col_i = ph.sb("col_i", [NT, 1], i32)
            col = ph.sb("col", [NT, 1])
            end_c = ph.sb("end_c", [NT, 1])
            past = ph.sb("past", [NT, ST])
            packed = ph.sb("packed", [1, STP // U])
            lows = ph.ps("lows", [P, 512])
            totals = ph.ps("totals", [P, 512])
            total_c = ph.ps("total_c", [NT, 512])
            end_p = ph.ps("end_p", [NT, 512])
            which = ph.ps("which", [P, 512])
            own, made, summed = (ph.sem(n) for n in ("own", "made", "summed"))
            block = ph.block()
            final = count[:, ET, :]

            @block.tensor
            def _(pe):
                nc.tensor.matmul(lows[:, 0:NT], k.above[:, :], final, start=True, stop=True)
                nc.tensor.matmul(totals[:, 0:NT], k.ones[:, :], final, start=True, stop=True)
                nc.tensor.matmul(total_c[:, 0:1], final, k.ones[:, 0:1], start=True, stop=True).then_inc(summed, 1)
                pe.wait_ge(made, 1)
                nc.tensor.matmul(end_p[:, 0:1], k.upto[0:NT, 0:NT], col[:, :], start=True, stop=True).then_inc(summed, 1)
                pe.wait_ge(made, 2)
                nc.tensor.matmul(which[:, 0:ST], k.ones[0:NT, :], past[:, :], start=True, stop=True).then_inc(summed, 1)

            @block.vector
            def _(dve):
                step = Chain(dve, own)
                dve.wait_ge(summed, 1)
                for total, whole, out in ((total_c[:, 0:1], col_i[:, :], col[:, :]),
                                          (totals[:, 0:NT], tiles_i[:, :], tiles[:, :])):
                    step(nc.vector.tensor_scalar(whole, total, float(P - 1), None, ALU.add))
                    step(nc.vector.tensor_scalar(whole, whole, 7, None, ALU.arith_shift_right))
                    step(nc.vector.tensor_copy(out, whole))
                nc.vector.memset(base[:, :], 0.0).then_inc(made, 1)
                step(nc.vector.tensor_tensor_scan(ends[:, :], k.ones[:, 0:NT], tiles[:, :], 0.0, ALU.mult, ALU.add))
                dve.wait_ge(summed, 2)
                step(nc.vector.tensor_copy(end_c[:, :], end_p[:, 0:1]))
                nc.vector.tensor_scalar(past[:, :], k.slots[0:NT, :], end_c[:, 0:1], None, ALU.is_ge).then_inc(made, 1)
                step(nc.vector.tensor_tensor(base[:, :], ends[:, :], tiles[:, :], ALU.subtract))
                step(nc.vector.scalar_tensor_tensor(base[:, :], base[:, :], float(P), lows[:, 0:NT], ALU.mult, ALU.add))
                nc.vector.tensor_tensor(count[:, 0:ET, :], count[:, 0:ET, :],
                                        base[:, :].unsqueeze(1).to_broadcast([P, ET, NT]), ALU.add)
                step(nc.vector.memset(tile_of[:, :], float(NT - 1)))
                dve.wait_ge(summed, 3)
                step(nc.vector.tensor_scalar(tile_of[:, 0:ST], which[:, 0:ST], float(NT - 1), None, ALU.min))
                for b in range(U - 2, -1, -1):
                    so_far = tile_of[0:1, U - 1:STP:U] if b == U - 2 else packed[:, :]
                    step(nc.vector.scalar_tensor_tensor(packed[:, :], so_far, float(PACK), tile_of[0:1, b:STP:U],
                                                        ALU.mult, ALU.add))
                nc.vector.tensor_copy(tile_row[:, :], packed[:, :])

        with Phase(nc, tag + "_rank") as ph:
            W = LOOK * EP
            keys = [ph.sb(f"keys{u}", [P, W], i32) for u in range(SLOTS)]
            low_i = [ph.sb(f"low_i{u}", [P, W], i32) for u in range(2)]
            low_hot = [ph.sb(f"low_hot{u}", [P, W]) for u in range(SLOTS)]
            same = ph.sb("same", [EP, LOOK, EP])
            picked = ph.sb("picked", [EP, LOOK, NT])
            rank = ph.sb("rank", [EP, ET])
            slot = ph.sb("slot", [EP, ET])
            slot_i = ph.sb("slot_i", [EP, ET], i32)
            in_tile = ph.sb("in_tile", [EP, ET], i32)
            tile_i = ph.sb("tile_i", [EP, ET], i32)
            found = [ph.ps(f"found{u}", [EP, 512]) for u in range(SLOTS)]
            loaded = [ph.sem(f"loaded{u}") for u in range(SLOTS)]
            masked, hot, looked, ranked, took, got, own, finished = (
                ph.sem(n) for n in ("masked", "hot", "looked", "ranked", "took", "got", "own", "finished"))
            block = ph.block()
            groups = ET // LOOK

            @block.gpsimd
            def _(pool):
                scatter.piece(nc, ph, pool, 11, finished)

            @block.sync
            def _(sp):
                def body(i):
                    for u in range(SLOTS):
                        g = i * SLOTS + u
                        after(sp, ranked, g - SLOTS + 1)
                        sp.dma_start(keys[u][:, :], key[bass.ds(g * W, W)].partition_broadcast(P)).then_inc(loaded[u], 16)

                rounds(sp, groups // SLOTS, body)

            @block.vector
            def _(dve):
                def mask(i, g, u):
                    dve.wait_ge(loaded[u], i * 16 + 16)
                    after(dve, hot, g - 1)
                    nc.vector.tensor_scalar(low_i[u % 2][:, :], keys[u][:, :], P - 1, None,
                                            ALU.bitwise_and).then_inc(masked, 1)

                def take(g, u, between=None):
                    dve.wait_ge(looked, g + 1)
                    after(dve, got, g)
                    nc.vector.tensor_tensor(
                        picked[:, :, :], found[u][:, 0:LOOK * NT].rearrange("p (t h) -> p t h", h=NT),
                        hi_hot[:, bass.ds(g * LOOK, LOOK), :], ALU.mult).then_inc(took, 1)
                    if between:
                        between()
                    dve.wait_ge(took, g + 1)
                    nc.vector.tensor_reduce(slot[:, bass.ds(g * LOOK, LOOK)], picked[:, :, :], AX.X,
                                            ALU.add).then_inc(got, 1)

                def finish(i):
                    mine = lambda a: a[:, bass.ds(i * SLOTS * LOOK, SLOTS * LOOK)]
                    step = Chain(dve, own, i * 2)
                    dve.wait_ge(got, (i + 1) * SLOTS)
                    dve.wait_ge(ranked, (i + 1) * SLOTS)
                    step(nc.vector.tensor_tensor(mine(slot_i), mine(slot), mine(rank), ALU.add))
                    nc.vector.tensor_scalar(mine(in_tile), mine(slot_i), P - 1, None, ALU.bitwise_and)
                    step(nc.vector.tensor_scalar(mine(tile_i), mine(slot_i), 7, None, ALU.arith_shift_right))
                    nc.vector.scalar_tensor_tensor(stage_all[:, bass.ds(i * SLOTS * LOOK, SLOTS * LOOK), 0], mine(in_tile),
                                                   float(ST), mine(tile_i), ALU.mult, ALU.add).then_inc(finished, 1)

                def rank_in_tile(g, u):
                    after(dve, ranked, g)
                    for j in range(LOOK):
                        t = g * LOOK + j
                        last = nc.vector.scalar_tensor_tensor(
                            same[:, j, :], keys[u][0:EP, j * EP:(j + 1) * EP], key_c[:, bass.ds(t, 1)],
                            k.before[0:EP, 0:EP], ALU.is_equal, ALU.mult, accum_out=rank[:, bass.ds(t, 1)])
                    last.then_inc(ranked, 1)

                mask(0, 0, 0)

                def body(i):
                    for u in range(SLOTS):
                        g, v = i * SLOTS + u, (u + 1) % SLOTS
                        dve.wait_ge(masked, g + 1)
                        after(dve, looked, g - SLOTS + 1)
                        nc.vector.tensor_scalar(low_hot[u][:, :], low_i[u % 2][:, :], k.row[:, 0:1], None,
                                                ALU.is_equal).then_inc(hot, 1)
                        rank_in_tile(g, u)
                        if u:
                            take(g - 1, u - 1, (lambda: mask(i, g + 1, v)) if v else None)
                        else:
                            mask(i, g + 1, v)
                            if not (isinstance(g, int) and g == 0):
                                take(g - 1, SLOTS - 1)
                                finish(i - 1)

                body(0)
                with dve.Fori(1, groups // SLOTS) as i:
                    mask(i, i * SLOTS, 0)
                    body(i)
                take(groups - 1, SLOTS - 1)
                finish(groups // SLOTS - 1)

            @block.tensor
            def _(pe):
                def body(i):
                    for u in range(SLOTS):
                        g = i * SLOTS + u
                        pe.wait_ge(hot, g + 1)
                        after(pe, took, g - SLOTS + 1)
                        for j in range(LOOK):
                            last = nc.tensor.matmul(found[u][:, j * NT:(j + 1) * NT], low_hot[u][:, j * EP:(j + 1) * EP],
                                                    count[:, bass.ds(g * LOOK + j, 1), :].rearrange("p t h -> p (t h)"),
                                                    start=True, stop=True)
                        last.then_inc(looked, 1)

                rounds(pe, groups // SLOTS, body)


def load_order(nc, k, tag, table, tile_of, index, local, more=None):
    with Phase(nc, tag) as ph:
        raw = ph.sb("raw", [P, ST, 4], i32)
        key_f = ph.sb("key_f", [P, ST])
        loaded, own = ph.sem("loaded"), ph.sem("own")
        rows = table.rearrange("(p t) w -> p t w", p=P)
        if more is not None:
            edges, edge_f = [ph.sb(f"edge{n}", [P, ST, 4], i32) for n in range(2)], [ph.sb(f"edge_f{n}", [P, ST]) for n in range(2)]
            wide = [ph.sb(f"wide{n}", [P, ST, 8]) for n in range(2)]
            turned = [ph.ps(f"turned{n}", [P, 512]) for n in range(6)]
            has = [ph.ps(f"has{n}", [8, 512]) for n in range(2)]
            cleared, marked, turn, moved = (ph.sem(n) for n in ("cleared", "marked", "turn", "moved"))
        block = ph.block()

        @block.sync
        def _(sp):
            sp.dma_start(raw[:, :, :], rows).then_inc(loaded, 16)
            if more is not None:
                sp.wait_ge(cleared, 2)
                sp.dma_start(edges[0][1:P, :, :], rows[0:P - 1]).then_inc(loaded, 16)
                sp.dma_start(edges[0][0:1, 1:ST, :], rows[P - 1:P, 0:ST - 1]).then_inc(loaded, 16)
                sp.dma_start(edges[1][0:P - 1, :, :], rows[1:P]).then_inc(loaded, 16)
                sp.dma_start(edges[1][P - 1:P, 0:ST - 1, :], rows[0:1, 1:ST]).then_inc(loaded, 16)

        @block.vector
        def _(dve):
            step = Chain(dve, own)
            if more is not None:
                for n in range(2):
                    nc.vector.memset(edges[n][:, :, :], -1).then_inc(cleared, 1)
            step(nc.vector.memset(index[0][:, :], 0))
            if more is not None:
                step(nc.vector.memset(index[1][:, :], 0))
            step(nc.vector.memset(local[:, :], float(NOKEY)))
            dve.wait_ge(loaded, 80 if more is not None else 16)
            nc.vector.tensor_copy(index[0][:, 0:ST], raw[:, :, 0])
            step(nc.vector.tensor_copy(key_f[:, :], raw[:, :, 2]))
            nc.vector.scalar_tensor_tensor(local[:, 0:ST], tile_of[:, 0:ST], -float(P), key_f[:, :], ALU.mult, ALU.add)
            if more is None:
                return
            nc.vector.tensor_copy(index[1][:, 0:ST], raw[:, :, 1])
            nc.vector.tensor_copy(more.weight[:, :], raw[:, :, 3].bitcast(fp32))
            last_mark = ph.sb("last_mark", [P, ST])
            for n, mark in enumerate((more.first, last_mark)):
                step(nc.vector.tensor_copy(edge_f[n][:, :], edges[n][:, :, 2]))
                step(nc.vector.tensor_tensor(mark[:, :], key_f[:, :], edge_f[n][:, :], ALU.not_equal))
                nc.vector.tensor_copy(wide[n][:, :, :], mark[:, :].unsqueeze(2).to_broadcast([P, ST, 8])).then_inc(marked, 1)
            more.last_mark = last_mark
            for n, (neg, edge) in enumerate(((more.not_first, 0), (more.not_last, P - 1))):
                for g in range(7):
                    dve.wait_ge(turn, 7 * n + g + 1)
                    nc.vector.tensor_scalar(neg[:, 4 * g:4 * g + 4, :],
                                            turned[(7 * n + g) % 6][:, :].rearrange("p (b e) -> p b e", e=P),
                                            -BIG, None, ALU.mult).then_inc(moved, 1)
                dve.wait_ge(moved, 7 * n + 7)
                step(nc.vector.tensor_copy(more.at_edge[n][:, :], neg[:, :, edge]))
                step(nc.vector.memset(neg[:, :, edge], -BIG))
            dve.wait_ge(turn, 15)
            for n in range(2):
                nc.vector.tensor_scalar(more.tile_cut[n][:, :], has[n][:, 0:ST], 1.0, -BIG, ALU.min, ALU.mult)

        if more is not None:
            @block.tensor
            def _(pe):
                for n in range(2):
                    pe.wait_ge(marked, n + 1)
                    for g in range(7):
                        after(pe, moved, 7 * n + g - 6 + 1)
                        for b in range(4):
                            last = nc.tensor.transpose(turned[(7 * n + g) % 6][:, b * P:(b + 1) * P],
                                                       wide[n][:, (4 * g + b) * 16:(4 * g + b + 1) * 16, :]
                                                       .rearrange("p t h -> p (t h)"), k.ident[:, :])
                        last.then_inc(turn, 1)
                for n, mark in enumerate((more.first, more.last_mark)):
                    last = nc.tensor.matmul(has[n][:, 0:ST], k.ones[:, 0:8], mark[:, :], start=True, stop=True)
                last.then_inc(turn, 1)


def gather_loop(nc, pool, stage, staged, arrived, index, source, dest, used, per_batch=1):
    nc.gpsimd.tensor_copy(stage[:, 0:U], index[:, 0:U]).then_inc(staged, 1)

    def body(i, batches):
        for h in range(batches):
            j, v = i * NB + h, (h + 1) % NB
            pool.wait_ge(staged, j + 1)
            after(pool, used, (j + 2 - NB) * per_batch)
            nc.gpsimd.tensor_copy(stage[:, v * U:(v + 1) * U], index[:, bass.ds((j + 1) * U, U)]).then_inc(staged, 1)
            for b in range(U):
                pool.indirect_dma_start(
                    out=dest[:, h * U + b, :], out_offset=None, in_=source[:, :],
                    in_offset=bass.IndirectOffsetOnAxis(ap=stage[:, h * U + b:h * U + b + 1], axis=0)).then_inc(arrived[h], 16)

    edge_rounds(pool, body)


class EdgeBuffers:

    def __init__(self, ph, k, local, tile_row, index, source, width, hot_dt=fp32):
        self.k, self.local, self.tile_row, self.index, self.source = k, local, tile_row, index, source
        self.rows = ph.sb("rows", [P, NB * U, width])
        self.stage = ph.sb("stage", [P, NB * U], i32)
        self.hot = [ph.sb(f"hot{h}", [P, U, P], hot_dt) for h in range(HOTS)]
        self.staged, self.hotted = ph.sem("staged"), ph.sem("hotted")
        self.arrived = [ph.sem(f"arrived{h}") for h in range(NB)]

    def turn_buffers(self, ph):
        self.turned = [ph.ps(f"turned{h}", [P, 512]) for h in range(2)]
        self.hot_t = [ph.sb(f"hot_t{h}", [P, U, P]) for h in range(2)]
        self.turn, self.moved = ph.sem("turn"), ph.sem("moved")

    def one_hot(self, nc, dve, j, h):
        nc.vector.tensor_tensor(self.hot[h % HOTS][:, :, :],
                                self.local[:, bass.ds(j * U, U)].unsqueeze(2).to_broadcast([P, U, P]),
                                self.k.ramp[:, :].unsqueeze(1).to_broadcast([P, U, P]), ALU.is_equal).then_inc(self.hotted, 1)

    def turn_hot(self, nc, pe, j, h):
        pe.wait_ge(self.hotted, j + 1)
        after(pe, self.moved, j - 1)
        for b in range(U):
            last = nc.tensor.matmul(self.turned[h % 2][:, b * P:(b + 1) * P], self.hot[h % HOTS][:, b, :],
                                    self.k.ident_b[:, :], start=True, stop=True)
        last.then_inc(self.turn, 1)

    def move_hot(self, nc, act, j, h, expanded):
        act.wait_ge(self.turn, j + 1)
        after(act, expanded, j - 1)
        nc.scalar.activation(self.hot_t[h % 2][:, :, :].rearrange("p b e -> p (b e)"), self.turned[h % 2][:, :],
                             ACT.Copy).then_inc(self.moved, 1)

    def node_tiles(self, nc, eng, j):
        packed = eng.value_load(self.tile_row[0:1, bass.ds(j, 1)], min_val=0, max_val=PACK ** U - 1)
        return [nc.s_assert_within((packed // PACK ** b) % PACK, 0, NT - 1,
                                   skip_runtime_bounds_check_because="the sort clips every node tile to NT - 1")
                for b in range(U)]


def alpha_pass(nc, k, tag, buf_args, key_rows, alpha):
    with Phase(nc, tag) as ph:
        e = EdgeBuffers(ph, k, *buf_args, 8, bf16)
        e.turn_buffers(ph)
        own_rows = [ph.ps(f"own_rows{h}", [P, 512]) for h in range(4)]
        expanded, added = ph.sem("expanded"), ph.sem("added")
        block = ph.block()

        @block.gpsimd
        def _(pool):
            gather_loop(nc, pool, e.stage, e.staged, e.arrived, e.index, e.source, e.rows, added)

        @block.vector
        def _(dve):
            nc.vector.memset(alpha[:, BT * U:ST, :], 0.0)
            for j in range(AHEAD):
                e.one_hot(nc, dve, j, j)

            def body(i, batches):
                for h in range(batches):
                    j = i * NB + h
                    after(dve, e.turn, j + AHEAD - HOTS + 1)
                    e.one_hot(nc, dve, j + AHEAD, h + AHEAD)
                    dve.wait_ge(e.arrived[h], (i + 1) * 16 * U)
                    dve.wait_ge(expanded, j + 1)
                    nc.vector.tensor_tensor(alpha[:, bass.ds(j * U, U), :],
                                            own_rows[h % 4][:, 0:U * 8].rearrange("p (b c) -> p b c", c=8),
                                            e.rows[:, h * U:(h + 1) * U, :], ALU.add).then_inc(added, 1)

            edge_rounds(dve, body)

        @block.tensor
        def _(pe):
            def expand(j, h):
                after(pe, added, j - 3)
                pe.wait_ge(e.moved, j + 1)
                for b, n in enumerate(e.node_tiles(nc, pe, j)):
                    last = nc.tensor.matmul(own_rows[h % 4][:, b * 8:(b + 1) * 8], e.hot_t[h % 2][:, b, :],
                                            key_rows[:, bass.ds(n, 1), :].rearrange("p t c -> p (t c)"),
                                            start=True, stop=True)
                last.then_inc(expanded, 1)

            e.turn_hot(nc, pe, 0, 0)
            e.turn_hot(nc, pe, 1, 1)
            expand(0, 0)
            e.turn_hot(nc, pe, 2, 2)
            expand(1, 1)

            def body(i, batches):
                for h in range(batches):
                    j = i * NB + h
                    e.turn_hot(nc, pe, j + 3, h + 3)
                    expand(j + 2, h + 2)

            edge_rounds(pe, body)

        @block.scalar
        def _(act):
            for j in range(AHEAD):
                e.move_hot(nc, act, j, j, expanded)

            def body(i, batches):
                for h in range(batches):
                    e.move_hot(nc, act, i * NB + h + AHEAD, h + AHEAD, expanded)

            edge_rounds(act, body)


def score_pass(nc, k, tag, buf_args, q_rows, score, self_score):
    with Phase(nc, tag) as ph:
        e = EdgeBuffers(ph, k, *buf_args, C, bf16)
        e.turn_buffers(ph)
        own_rows = [ph.ps(f"own_rows{n}", [P, U, C]) for n in range(2)]
        own_self = [ph.ps(f"own_self{n}", [P, 512]) for n in range(2)]
        expanded, own_selves, multiplied, copied, used = (
            ph.sem(n) for n in ("expanded", "own_selves", "multiplied", "copied", "used"))
        block = ph.block()

        @block.gpsimd
        def _(pool):
            gather_loop(nc, pool, e.stage, e.staged, e.arrived, e.index, e.source, e.rows, used)

        @block.vector
        def _(dve):
            nc.vector.memset(score[:, BT * U:ST, :], 0.0)
            nc.vector.memset(self_score[:, BT * U:ST, :], 0.0)
            for j in range(AHEAD):
                e.one_hot(nc, dve, j, j)

            def body(i, batches):
                for h in range(batches):
                    j = i * NB + h
                    dve.wait_ge(e.arrived[h], (i + 1) * 16 * U)
                    dve.wait_ge(expanded, j + 1)
                    rows = e.rows[:, h * U:(h + 1) * U, :]
                    nc.vector.tensor_tensor(rows, own_rows[h % 2][:, :, :], rows, ALU.mult).then_inc(multiplied, 1)
                    after(dve, e.turn, j + AHEAD - HOTS + 1)
                    e.one_hot(nc, dve, j + AHEAD, h + AHEAD)
                    dve.wait_ge(multiplied, j + 1)
                    nc.vector.tensor_reduce(score[:, bass.ds(j * U, U), :], rows.rearrange("p b (h d) -> p b h d", h=8),
                                            AX.X, ALU.add).then_inc(used, 1)

            edge_rounds(dve, body)

        @block.tensor
        def _(pe):
            def expand(j, h):
                pe.wait_ge(e.moved, j + 1)
                after(pe, copied, j - 1)
                tiles = e.node_tiles(nc, pe, j)
                for b in range(U):
                    last = nc.tensor.matmul(own_self[h % 2][:, b * 8:(b + 1) * 8], e.hot_t[h % 2][:, b, :],
                                            q_rows[:, bass.ds(tiles[b], 1), C:C + 8].rearrange("p t c -> p (t c)"),
                                            start=True, stop=True)
                last.then_inc(own_selves, 1)
                after(pe, multiplied, j - 1)
                for b in range(U):
                    last = nc.tensor.matmul(own_rows[h % 2][:, b, :], e.hot_t[h % 2][:, b, :],
                                            q_rows[:, bass.ds(tiles[b], 1), 0:C].rearrange("p t c -> p (t c)"),
                                            start=True, stop=True)
                last.then_inc(expanded, 1)

            e.turn_hot(nc, pe, 0, 0)
            e.turn_hot(nc, pe, 1, 1)
            expand(0, 0)

            def body(i, batches):
                for h in range(batches):
                    j = i * NB + h
                    e.turn_hot(nc, pe, j + 2, h + 2)
                    expand(j + 1, h + 1)

            edge_rounds(pe, body)

        @block.scalar
        def _(act):
            e.move_hot(nc, act, 0, 0, expanded)
            e.move_hot(nc, act, 1, 1, expanded)

            def body(i, batches):
                for h in range(batches):
                    j = i * NB + h
                    act.wait_ge(own_selves, j + 1)
                    nc.scalar.activation(self_score[:, bass.ds(j * U, U), :],
                                         own_self[h % 2][:, 0:U * 8].rearrange("p (b c) -> p b c", c=8),
                                         ACT.Copy).then_inc(copied, 1)
                    e.move_hot(nc, act, j + 2, h + 2, expanded)

            edge_rounds(act, body)


def add_to_nodes(nc, dve, e, sums, acc, width, summed, stored, j, between=()):
    if isinstance(j, int) and j < 0:
        for other in between:
            other()
        return
    for b, n in enumerate(e.node_tiles(nc, dve, j)):
        dve.wait_ge(summed, j * U + b + 1)
        dve.wait_ge(stored, j * U + b + 1)
        into = acc[:, bass.ds(n, 1), :].rearrange("p t c -> p (t c)")
        nc.vector.tensor_tensor(into, into, sums[b][:, 0:width], ALU.add).then_inc(stored, 1)
        if b < len(between):
            between[b]()


def sum_pass(nc, k, tag, buf_args, acc, coef=None, heads=0, extra=0):
    width = C + heads + extra
    with Phase(nc, tag) as ph:
        e = EdgeBuffers(ph, k, *buf_args, C)
        sums = [ph.ps(f"sums{b}", [P, 512]) for b in range(2 * U)]
        if heads:
            msg = [ph.sb(f"msg{f}", [P, U, width]) for f in range(2)]
        weighed, copied, summed, stored, used = (ph.sem(n) for n in ("weighed", "copied", "summed", "stored", "used"))
        block = ph.block()

        @block.gpsimd
        def _(pool):
            gather_loop(nc, pool, e.stage, e.staged, e.arrived, e.index, e.source, e.rows, *((used, 2) if heads else (summed, U)))

        @block.vector
        def _(dve):
            nc.vector.memset(acc[:, :, :], 0.0).then_inc(stored, 1)
            e.one_hot(nc, dve, 0, 0)
            e.one_hot(nc, dve, 1, 1)

            def body(i, batches):
                for h in range(batches):
                    j = i * NB + h

                    def weigh(f):
                        dve.wait_ge(e.arrived[h], (i + 1) * 16 * U)
                        after(dve, summed, (j - 1) * U)
                        H = U // 2
                        nc.vector.tensor_tensor(
                            msg[h % 2][:, f * H:(f + 1) * H, 0:C].rearrange("p b (h d) -> p b h d", h=heads),
                            e.rows[:, h * U + f * H:h * U + (f + 1) * H, :].rearrange("p b (h d) -> p b h d", h=heads),
                            coef[:, bass.ds(j * U + f * H, H), 0:heads].unsqueeze(3).to_broadcast([P, H, heads, C // heads]),
                            ALU.mult).then_inc(used, 1)

                    def mark():
                        after(dve, summed, (j + 3 - HOTS) * U)
                        e.one_hot(nc, dve, j + 2, h + 2)

                    add_to_nodes(nc, dve, e, sums[(h + 1) % 2 * U:], acc, width, summed, stored, j - 1,
                                 [lambda: weigh(0), lambda: weigh(1), mark] if heads else [mark])

            edge_rounds(dve, body)
            add_to_nodes(nc, dve, e, sums[U:], acc, width, summed, stored, BT - 1)

        @block.tensor
        def _(pe):
            def body(i, batches):
                for h in range(batches):
                    j = i * NB + h
                    pe.wait_ge(e.hotted, j + 1)
                    if heads:
                        pe.wait_ge(used, 2 * j + 2)
                        pe.wait_ge(copied, j + 1)
                    else:
                        pe.wait_ge(e.arrived[h], (i + 1) * 16 * U)
                    for b in range(U):
                        after(pe, stored, (j - 2) * U + b + 2)
                        rhs = msg[h % 2][:, b, :] if heads else e.rows[:, h * U + b, :]
                        last = nc.tensor.matmul(sums[h % 2 * U + b][:, 0:width], e.hot[h % HOTS][:, b, :], rhs, start=True, stop=True)
                        last.then_inc(summed, 1)

            edge_rounds(pe, body)

        if heads:
            @block.scalar
            def _(act):
                def body(i, batches):
                    for h in range(batches):
                        j = i * NB + h
                        after(act, summed, (j - 1) * U)
                        nc.scalar.activation(msg[h % 2][:, :, C:width], coef[:, bass.ds(j * U, U), 0:heads + extra],
                                             ACT.Copy).then_inc(copied, 1)

                edge_rounds(act, body)


def by_source_pass(nc, k, tag, buf_args, s_src, acc):
    W = C + 2
    with Phase(nc, tag) as ph:
        e = EdgeBuffers(ph, k, *buf_args, W, bf16)
        e.turn_buffers(ph)
        own_rows = [ph.ps(f"own_rows{f}", [P, 512]) for f in range(2)]
        sums = [ph.ps(f"sums{b}", [P, 512]) for b in range(U)]
        wide_hot = [ph.sb(f"wide_hot{f}", [P, U, P]) for f in range(4)]
        msg = [ph.sb(f"msg{f}", [P, U, W]) for f in range(4)]
        total = [ph.sb(f"total{f}", [P, U, 2]) for f in range(2)]
        leaky = [ph.sb(f"leaky{f}", [P, U, 2]) for f in range(2)]
        expanded, totalled, leaked, raised, used, summed, stored, widened = (
            ph.sem(n) for n in ("expanded", "totalled", "leaked", "raised", "used", "summed", "stored", "widened"))
        block = ph.block()

        @block.gpsimd
        def _(pool):
            gather_loop(nc, pool, e.stage, e.staged, e.arrived, e.index, e.source, e.rows, used)

        @block.vector
        def _(dve):
            def total_of(j, h, i):
                dve.wait_ge(e.arrived[h], (i + 1) * 16 * U)
                dve.wait_ge(expanded, j + 1)
                nc.vector.tensor_tensor(total[h % 2][:, :, :], own_rows[h % 2][:, 0:2 * U].rearrange("p (b c) -> p b c", c=2),
                                        e.rows[:, h * U:(h + 1) * U, C:W], ALU.add).then_inc(totalled, 1)

            def leaky_of(j, h):
                dve.wait_ge(totalled, j + 1)
                after(dve, raised, j - 1)
                nc.vector.scalar_tensor_tensor(leaky[h % 2][:, :, :], total[h % 2][:, :, :], 0.2, total[h % 2][:, :, :],
                                               ALU.mult, ALU.max).then_inc(leaked, 1)

            def weigh(j, h):
                dve.wait_ge(raised, j + 1)
                nc.vector.tensor_tensor(msg[h % 4][:, :, 0:C].rearrange("p b (h d) -> p b h d", h=2),
                                        e.rows[:, h * U:(h + 1) * U, 0:C].rearrange("p b (h d) -> p b h d", h=2),
                                        msg[h % 4][:, :, C:W].unsqueeze(3).to_broadcast([P, U, 2, C // 2]),
                                        ALU.mult).then_inc(used, 1)

            nc.vector.memset(acc[:, :, :], 0.0).then_inc(stored, 1)
            for j in range(HOTS):
                e.one_hot(nc, dve, j, j)
            total_of(0, 0, 0)
            leaky_of(0, 0)

            def step(i, h, j, with_next=True):
                v = (h + 1) % NB
                weigh(j, h)

                def mark():
                    after(dve, widened, j + 1)
                    after(dve, e.turn, j + 1)
                    e.one_hot(nc, dve, j + 4, h + 4)

                add_to_nodes(nc, dve, e, sums, acc, W, summed, stored, j - 1,
                             [lambda: total_of(j + 1, v, i + (h + 1) // NB), lambda: leaky_of(j + 1, v), mark]
                             if with_next else [])

            def body(i):
                for h in range(NB):
                    step(i, h, i * NB + h)

            body(0)
            with dve.Fori(1, SR - 1) as i:
                body(i)
            for h in range(LASTB):
                step(SR - 1, h, (SR - 1) * NB + h, h < LASTB - 1)
            add_to_nodes(nc, dve, e, sums, acc, W, summed, stored, BT - 1)

        @block.tensor
        def _(pe):
            def expand(j, h):
                after(pe, totalled, j - 1)
                pe.wait_ge(e.moved, j + 1)
                for b, n in enumerate(e.node_tiles(nc, pe, j)):
                    last = nc.tensor.matmul(own_rows[h % 2][:, b * 2:(b + 1) * 2], e.hot_t[h % 2][:, b, :],
                                            s_src[:, bass.ds(n, 1), :].rearrange("p t c -> p (t c)"),
                                            start=True, stop=True)
                last.then_inc(expanded, 1)

            e.turn_hot(nc, pe, 0, 0)
            e.turn_hot(nc, pe, 1, 1)
            expand(0, 0)
            e.turn_hot(nc, pe, 2, 2)
            expand(1, 1)

            def step(h, j, with_next=True):
                if with_next:
                    e.turn_hot(nc, pe, j + 3, h + 3)
                    expand(j + 2, h + 2)
                pe.wait_ge(used, j + 1)
                pe.wait_ge(widened, j + 1)
                for b in range(U):
                    after(pe, stored, (j - 1) * U + b + 2)
                    nc.tensor.matmul(sums[b][:, 0:W], wide_hot[h % 4][:, b, :], msg[h % 4][:, b, :],
                                     start=True, stop=True).then_inc(summed, 1)

            def body(i):
                for h in range(NB):
                    step(h, i * NB + h)

            body(0)
            with pe.Fori(1, SR - 1) as i:
                body(i)
            for h in range(LASTB):
                step(h, (SR - 1) * NB + h, h < LASTB - 2)

        @block.scalar
        def _(act):
            def widen(j, h):
                act.wait_ge(e.hotted, j + 1)
                after(act, summed, (j - 3) * U)
                nc.scalar.activation(wide_hot[h % 4][:, :, :], e.hot[h % HOTS][:, :, :], ACT.Copy).then_inc(widened, 1)

            def raise_of(j, h):
                act.wait_ge(leaked, j + 1)
                after(act, summed, (j - 3) * U)
                nc.scalar.activation(msg[h % 4][:, :, C:W], leaky[h % 2][:, :, :], ACT.Exp, scale=-1.0).then_inc(raised, 1)

            e.move_hot(nc, act, 0, 0, expanded)
            e.move_hot(nc, act, 1, 1, expanded)
            widen(0, 0)
            widen(1, 1)
            e.move_hot(nc, act, 2, 2, expanded)
            raise_of(0, 0)

            def step(h, j, left=NB):
                if left > 0:
                    raise_of(j + 1, h + 1)
                if left > 2:
                    e.move_hot(nc, act, j + 3, h + 3, expanded)
                if left > 1:
                    widen(j + 2, h + 2)

            def body(i):
                for h in range(NB):
                    step(h, i * NB + h)

            body(0)
            with act.Fori(1, SR - 1) as i:
                body(i)
            for h in range(LASTB):
                step(h, (SR - 1) * NB + h, LASTB - 1 - h)


class Marks:

    def __init__(self, ph):
        self.weight = ph.sb("weight", [P, ST])
        self.first = ph.sb("first", [P, ST])
        self.not_first = ph.sb("not_first", [P, ST // 16, P])
        self.not_last = ph.sb("not_last", [P, ST // 16, P])
        self.at_edge = [ph.sb(f"at_edge{n}", [P, ST // 16]) for n in range(2)]
        self.tile_cut = [ph.sb(f"tile_cut{n}", [8, ST]) for n in range(2)]


def segment_softmax(nc, k, tag, marks, score, coef, self_score=None):
    B = ST // 16
    with Phase(nc, tag) as ph:
        two = self_score is not None
        turned_s = ph.sb("turned_s", [P, B, P])
        turned_o = ph.sb("turned_o", [P, B, P]) if two else None
        top = ph.sb("top", [P, B, P])
        run = ph.sb("run", [P, B, P])
        link = [ph.sb(f"link{n}", [8, STP]) for n in range(2)]
        edge = [ph.sb(f"edge{n}", [P, B]) for n in range(2)]
        bank = [ph.ps(f"bank{n}", [P, 512]) for n in range(6)]
        ends = ph.ps("ends", [8, 512])
        enter = ph.ps("enter", [P, 512])
        own, ready, turn, moved, scanned, sent, linked, raised, back, home = (
            ph.sem(n) for n in ("own", "ready", "turn", "moved", "scanned", "sent", "linked", "raised", "back", "home"))
        block = ph.block()
        parts = [score, self_score] if two else [score]
        dest = [turned_s, turned_o]

        @block.tensor
        def _(pe):
            pe.wait_ge(ready, 1)
            for n, s in enumerate(parts):
                for g in range(7):
                    after(pe, moved, 7 * n + g - 5)
                    for b in range(4):
                        last = nc.tensor.transpose(bank[(7 * n + g) % 6][:, b * P:(b + 1) * P],
                                                   s[:, (4 * g + b) * 16:(4 * g + b + 1) * 16, :]
                                                   .rearrange("p t h -> p (t h)"), k.ident[:, :])
                    last.then_inc(turn, 1)
            for n in range(2):
                pe.wait_ge(scanned, n + 1)
                for t in range(16):
                    last = nc.tensor.matmul(ends[:, t:ST:16], k.ident[:, 8 * t:8 * t + 8], edge[n][:, :],
                                            start=True, stop=True)
                last.then_inc(sent, 1)
                pe.wait_ge(linked, n + 1)
                for t in range(16):
                    last = nc.tensor.matmul(enter[:, 0:B], k.spread[:, t, :], link[n][:, t + 2 * n:t + 2 * n + ST - 15:16],
                                            start=(t == 0), stop=(t == 15))
                last.then_inc(sent, 1)
            for n in range(len(parts)):
                pe.wait_ge(raised, n + 1)
                for g in range(7):
                    after(pe, home, 7 * n + g - 5)
                    for b in range(4):
                        last = nc.tensor.transpose(bank[(7 * n + g) % 6][:, b * P:(b + 1) * P], dest[n][:, 4 * g + b, :],
                                                   k.ident[:, :])
                    last.then_inc(back, 1)

        @block.scalar
        def _(act):
            for m in range(7 * len(parts)):
                act.wait_ge(turn, m + 1)
                nc.scalar.activation(dest[m // 7][:, 4 * (m % 7):4 * (m % 7) + 4, :].rearrange("p b e -> p (b e)"),
                                     bank[m % 6][:, :], ACT.Copy).then_inc(moved, 1)
            for n in range(len(parts)):
                act.wait_ge(ready, n + 2)
                nc.scalar.activation(dest[n][:, :, :], dest[n][:, :, :], ACT.Exp).then_inc(raised, 1)
            for m in range(7 * len(parts)):
                act.wait_ge(back, m + 1)
                n, g = m // 7, m % 7
                nc.scalar.activation(coef[:, 64 * g:64 * g + 64, 8 * n:8 * n + 8],
                                     bank[m % 6][:, :].rearrange("p (t h) -> p t h", h=8), ACT.Copy).then_inc(home, 1)

        @block.vector
        def _(dve):
            step = Chain(dve, own)
            step(nc.vector.memset(coef[:, ST:STP, :], 0.0))
            if not two:
                step(nc.vector.tensor_tensor(score[:, :, :], score[:, :, :],
                                             marks.weight[:, :].unsqueeze(2).to_broadcast([P, ST, 8]), ALU.mult))
                nc.vector.scalar_tensor_tensor(score[:, :, :], score[:, :, :], 0.2, score[:, :, :],
                                               ALU.mult, ALU.max).then_inc(ready, 1)
            else:
                nc.vector.memset(edge[0][:, :], 0.0).then_inc(ready, 1)
            nc.vector.memset(link[0][:, 0:1], -BIG)
            step(nc.vector.memset(link[1][:, ST + 1:ST + 2], -BIG))
            dve.wait_ge(moved, 7 * len(parts))
            if two:
                step(nc.vector.tensor_tensor(top[:, :, :], turned_s[:, :, :], turned_o[:, :, :], ALU.max))
            else:
                step(nc.vector.tensor_copy(top[:, :, :], turned_s[:, :, :]))

            def scan(out, cut, data, way):
                flat = [a[:, :, :].rearrange("p b e -> p (b e)")[:, ::way] for a in (out, cut, data)]
                return nc.vector.tensor_tensor_scan(*flat, -BIG, ALU.add, ALU.max)

            for n, (data, res, cut, end, start, way) in enumerate((
                    (top, run, marks.not_first, P - 1, 0, 1), (run, top, marks.not_last, 0, P - 1, -1))):
                step(scan(res, cut, data, way))
                nc.vector.tensor_copy(edge[n][:, :], res[:, :, end]).then_inc(scanned, 1)
                dve.wait_ge(sent, 2 * n + 1)
                nc.vector.tensor_tensor_scan(link[n][:, 1:ST + 1][:, ::way], marks.tile_cut[n][:, ::way],
                                             ends[:, 0:ST][:, ::way], -BIG, ALU.add, ALU.max).then_inc(linked, 1)
                dve.wait_ge(sent, 2 * n + 2)
                step(nc.vector.tensor_tensor(edge[n][:, :], enter[:, 0:B], marks.at_edge[n][:, :], ALU.add))
                step(nc.vector.tensor_tensor(data[:, :, start], data[:, :, start], edge[n][:, :], ALU.max))
                step(scan(res, cut, data, way))
            for n in range(len(parts)):
                nc.vector.tensor_tensor(dest[n][:, :, :], dest[n][:, :, :], top[:, :, :], ALU.subtract).then_inc(ready, 1)
            if two:
                dve.wait_ge(home, 14)
                nc.vector.tensor_tensor(coef[:, 0:ST, 8:16], coef[:, 0:ST, 8:16],
                                        marks.first[:, :].unsqueeze(2).to_broadcast([P, ST, 8]), ALU.mult)


class Sink:

    def __init__(self, dram, col, width):
        self.dram, self.col, self.width = dram, col, width


def project(nc, k, tag, src, width, weights, bias, sinks, evac, out_width=None, post=None, post_steps=0, extra=None,
            pieces=(), affine=None):
    chunks = [(c, min(512, width - c)) for c in range(0, width, 512)]
    nch, na, nv = len(chunks), evac.count("a"), evac.count("v")
    with Phase(nc, tag) as ph:
        own_w = isinstance(weights, list)
        w = ph.sb("w", [P, 2, width]) if own_w else weights
        b = ph.sb("b", [P, width]) if bias else None
        copy = [ph.sb(f"copy{u}", [P, C]) for u in range(SLOTS)]
        turned = [ph.sb(f"turned{u}", [P, 2, P]) for u in range(SLOTS)]
        out = [ph.sb(f"out{u}", [P, out_width or width]) for u in range(SLOTS)]
        turn_p = [ph.ps(f"turn_p{n}", [P, 512]) for n in range(3)]
        prod = [ph.ps(f"prod{u}", [P, 512]) for u in range(SLOTS)]
        loaded, copied, turn, moved, multiplied, read_a, read_v, own, posted = (
            ph.sem(n) for n in ("loaded", "copied", "turn", "moved", "multiplied", "read_a", "read_v", "own", "posted"))
        stored = [ph.sem(f"stored{u}") for u in range(SLOTS)]
        bufs = extra(ph) if extra else None
        loads = ([(w[:, :, c:c + m], a.rearrange("(c p) m -> p c m", p=P)) for a, c, m in weights] if own_w else [])
        loads += [(b[:, c:c + m], a.partition_broadcast(P)) for a, c, m in (bias or [])]
        loads += bufs.loads if bufs else []
        block = ph.block()
        if pieces:
            scatter_beside(nc, ph, block, *pieces)

        def out_free(eng, i, u):
            if not sinks:
                return
            after(eng, stored[u], i * 16 * len(sinks))

        @block.sync
        def _(sp):
            for dst, a in loads:
                sp.dma_start(dst, a).then_inc(loaded, 16)

            def body(i):
                for u in range(SLOTS):
                    t = i * SLOTS + u
                    if na:
                        sp.wait_ge(read_a, (t + 1) * na)
                    if nv:
                        sp.wait_ge(read_v, (t + 1) * nv)
                    if post:
                        sp.wait_ge(posted, t + 1)
                    for s in sinks:
                        sp.dma_start(s.dram[bass.ds(t * P, P), :], out[u][:, s.col:s.col + s.width]).then_inc(stored[u], 16)

            if sinks:
                rounds(sp, ROUNDS, body)
                for u in range(SLOTS):
                    sp.wait_ge(stored[u], ROUNDS * 16 * len(sinks))

        @block.scalar
        def _(act):
            def move(t, u):
                act.wait_ge(turn, t + 1)
                after(act, multiplied, (t - SLOTS + 1) * nch)
                if affine:
                    for c in range(2):
                        last = nc.scalar.activation(turned[u][:, c, :], turn_p[u % 3][:, c * P:(c + 1) * P], ACT.Identity,
                                                    bias=affine.bias[:, c:c + 1], scale=affine.gain[:, c:c + 1])
                    last.then_inc(moved, 1)
                    return
                nc.scalar.activation(turned[u][:, :, :].rearrange("p c n -> p (c n)"), turn_p[u % 3][:, 0:C],
                                     ACT.Copy).then_inc(moved, 1)

            def read(i, t, u):
                if not na:
                    return
                out_free(act, i, u)
                for n, (c, m) in enumerate(chunks):
                    if evac[n] == "a":
                        act.wait_ge(multiplied, t * nch + n + 1)
                        nc.scalar.activation(out[u][:, c:c + m], prod[(u * nch + n) % SLOTS][:, 0:m], ACT.Copy).then_inc(read_a, 1)

            def body(i):
                for u in range(SLOTS):
                    t = i * SLOTS + u
                    after(act, turn, t - SLOTS + 1)
                    (affine.copy(nc, copy[u][:, :], src, t) if affine else
                     nc.scalar.activation(copy[u][:, :], flat_tile(src, t), ACT.Copy)).then_inc(copied, 1)
                    if not (isinstance(t, int) and t < 1):
                        move(t - 1, (u - 1) % SLOTS)
                    if not (isinstance(t, int) and t < 2):
                        read(i if u >= 2 else i - 1, t - 2, (u - 2) % SLOTS)

            rounds(act, ROUNDS, body)
            move(NT - 1, SLOTS - 1)
            read(ROUNDS - 1, NT - 2, SLOTS - 2)
            read(ROUNDS - 1, NT - 1, SLOTS - 1)

        @block.tensor
        def _(pe):
            pe.wait_ge(loaded, 16 * len(loads)) if loads else None

            def multiply(t, u):
                pe.wait_ge(moved, t + 1)
                for n, (c, m) in enumerate(chunks):
                    lin = u * nch + n - SLOTS
                    t2, n2 = (t - u + lin // nch, lin % nch)
                    kind = evac[n2]
                    sem, per, upto = ((read_a, na, evac[:n2 + 1].count("a")) if kind == "a"
                                      else (read_v, nv, evac[:n2 + 1].count("v")))
                    after(pe, sem, t2 * per + upto)
                    for c2 in range(2):
                        last = nc.tensor.matmul(prod[(u * nch + n) % SLOTS][:, 0:m], turned[u][:, c2, :], w[:, c2, c:c + m],
                                                start=(c2 == 0), stop=(c2 == 1))
                    last.then_inc(multiplied, 1)

            def body(i):
                for u in range(SLOTS):
                    t = i * SLOTS + u
                    pe.wait_ge(copied, t + 1)
                    after(pe, moved, t - 1)
                    for c2 in range(2):
                        last = nc.tensor.transpose(turn_p[u % 3][:, c2 * P:(c2 + 1) * P], copy[u][:, c2 * P:(c2 + 1) * P],
                                                   k.ident[:, :])
                    last.then_inc(turn, 1)
                    if not (isinstance(t, int) and t < 1):
                        multiply(t - 1, (u - 1) % SLOTS)

            rounds(pe, ROUNDS, body)
            multiply(NT - 1, SLOTS - 1)

        @block.vector
        def _(dve):
            if bias or post:
                dve.wait_ge(loaded, 16 * len(loads))

            def body(i):
                for u in range(SLOTS):
                    t = i * SLOTS + u
                    if nv:
                        out_free(dve, i, u)
                    for n, (c, m) in enumerate(chunks):
                        if evac[n] == "v":
                            dve.wait_ge(multiplied, t * nch + n + 1)
                            p = prod[(u * nch + n) % SLOTS][:, 0:m]
                            ins = (nc.vector.tensor_tensor(out[u][:, c:c + m], p, b[:, c:c + m], ALU.add) if bias
                                   else nc.vector.tensor_copy(out[u][:, c:c + m], p))
                            ins.then_inc(read_v, 1)
                    if post:
                        if na:
                            dve.wait_ge(read_a, (t + 1) * na)
                        if nv:
                            dve.wait_ge(read_v, (t + 1) * nv)
                        out_free(dve, i, u)
                        start = t * post_steps
                        step = Chain(dve, own, start)
                        post(dve, step, t, out[u], bufs)
                        nc.vector.memset(bufs.tick[:, :], 0.0).then_inc(posted, 1)

            rounds(dve, ROUNDS, body)


class Extra:
    pass


def fold_heads(nc, step, out, a, b, tmp, heads):
    step(nc.vector.tensor_tensor(tmp, a, b, ALU.mult))
    step(nc.vector.tensor_reduce(out, tmp.rearrange("p (h d) -> p h d", h=heads), AX.X, ALU.add))


def flat_tile(a, t):
    return a[:, bass.ds(t, 1), :].rearrange("p t c -> p (t c)")


class Norm:

    def __init__(self, ph):
        self.stats = ph.sb("stats", [P, NT, 6])
        self.mean, self.var, self.tmp = (ph.sb(n, [P, NT]) for n in ("row_mean", "row_var", "row_tmp"))
        self.varied, self.rooted, self.scaled = (ph.sem(n) for n in ("row_varied", "row_rooted", "row_scaled"))

    def statistics(self, nc, dve, step, x):
        with dve.Fori(0, ROUNDS) as i:
            for u in range(SLOTS):
                nc.vector.bn_stats(flat_tile(self.stats, i * SLOTS + u), flat_tile(x, i * SLOTS + u)).then_inc(self.scaled, 1)
        dve.wait_ge(self.scaled, NT)
        st = self.stats
        step(nc.vector.tensor_tensor(self.mean[:, :], st[:, :, 1], st[:, :, 4], ALU.add))
        step(nc.vector.tensor_scalar(self.mean[:, :], self.mean[:, :], 0.5, None, ALU.mult))
        step(nc.vector.tensor_tensor(self.tmp[:, :], st[:, :, 1], st[:, :, 4], ALU.subtract))
        step(nc.vector.scalar_tensor_tensor(self.tmp[:, :], self.tmp[:, :], 0.25, self.tmp[:, :], ALU.mult, ALU.mult))
        step(nc.vector.tensor_tensor(self.var[:, :], st[:, :, 2], st[:, :, 5], ALU.add))
        step(nc.vector.scalar_tensor_tensor(self.var[:, :], self.var[:, :], 1.0 / C, self.tmp[:, :], ALU.mult, ALU.add))
        nc.vector.tensor_scalar(self.var[:, :], self.var[:, :], EPS, None, ALU.add).then_inc(self.varied, 1)

    def dve(self, nc, dve, step, x, y):
        self.statistics(nc, dve, step, x)
        dve.wait_ge(self.rooted, 1)
        step(nc.vector.reciprocal(self.var[:, :], self.var[:, :]))
        with dve.Fori(0, ROUNDS) as i:
            for u in range(SLOTS):
                t = i * SLOTS + u
                nc.vector.tensor_scalar(flat_tile(y, t), flat_tile(x, t), self.mean[:, bass.ds(t, 1)],
                                        self.var[:, bass.ds(t, 1)], ALU.subtract, ALU.mult).then_inc(self.scaled, 1)
        dve.wait_ge(self.scaled, 2 * NT)

    def scale_and_shift(self, nc, dve, step, x, scale, shift):
        self.statistics(nc, dve, step, x)
        dve.wait_ge(self.rooted, 1)
        step(nc.vector.reciprocal(scale[:, :], self.var[:, :]))
        nc.vector.scalar_tensor_tensor(shift[:, :], self.mean[:, :], -1.0, scale[:, :], ALU.mult, ALU.mult)

    def act(self, nc, act):
        act.wait_ge(self.varied, 1)
        nc.scalar.activation(self.var[:, :], self.var[:, :], ACT.Sqrt).then_inc(self.rooted, 1)


def node_rows(dram, width=C):
    return dram.rearrange("(t p) c -> p t c", p=P)


def attend_update(nc, k, tag, acc, heads, x, guard, residual=None, pieces=()):
    with Phase(nc, tag) as ph:
        norm = Norm(ph)
        hp = ph.sb("hp", [P, NT, C])
        res = ph.sb("res", [P, NT, C]) if residual is not None else None
        pad = ph.sb("pad", [P, 1])
        own, loaded, divided, raised = (ph.sem(n) for n in ("own", "loaded", "divided", "raised"))
        block = ph.block()
        if pieces:
            scatter_beside(nc, ph, block, *pieces)

        @block.sync
        def _(sp):
            if residual is not None:
                sp.dma_start(res[:, :, :], node_rows(residual)).then_inc(loaded, 16)

        @block.scalar
        def _(act):
            act.wait_ge(divided, 1)
            nc.scalar.activation(acc[:, :, 0:C], acc[:, :, 0:C], ACT.Exp).then_inc(raised, 1)
            norm.act(nc, act)

        @block.vector
        def _(dve):
            step = Chain(dve, own)
            z = acc[:, :, C:C + heads]
            if guard:
                step(nc.vector.tensor_scalar(z, z, guard, None, ALU.add))
            else:
                step(nc.vector.tensor_scalar(pad[:, :], k.row[:, :], float(NL), None, ALU.is_ge))
                step(nc.vector.tensor_scalar(acc[:, NT - 1, C:C + heads], acc[:, NT - 1, C:C + heads], pad[:, 0:1], None, ALU.add))
            step(nc.vector.reciprocal(z, z))
            step(nc.vector.tensor_tensor(hp[:, :, :].rearrange("p t (h d) -> p t h d", h=heads),
                                         acc[:, :, 0:C].rearrange("p t (h d) -> p t h d", h=heads),
                                         z.unsqueeze(3).to_broadcast([P, NT, heads, C // heads]), ALU.mult))
            nc.vector.tensor_scalar(acc[:, :, 0:C], hp[:, :, :], 0.0, None, ALU.min).then_inc(divided, 1)
            dve.wait_ge(raised, 1)
            step(nc.vector.scalar_tensor_tensor(hp[:, :, :], hp[:, :, :], 0.0, acc[:, :, 0:C], ALU.max, ALU.add))
            if residual is not None:
                dve.wait_ge(loaded, 16)
                step(nc.vector.scalar_tensor_tensor(hp[:, :, :], hp[:, :, :], -1.0, res[:, :, :], ALU.add, ALU.add))
                step(nc.vector.tensor_tensor(x[:, :, :], x[:, :, :], hp[:, :, :], ALU.add))
            else:
                step(nc.vector.scalar_tensor_tensor(x[:, :, :], hp[:, :, :], -1.0, x[:, :, :], ALU.add, ALU.add))
            norm.dve(nc, dve, step, x, x)


def norm_into(nc, tag, x, y, add=None, add_dram=None):
    with Phase(nc, tag) as ph:
        norm = Norm(ph)
        own, loaded = ph.sem("own"), ph.sem("loaded")
        block = ph.block()

        @block.sync
        def _(sp):
            sp.dma_start(add[:, :, :], node_rows(add_dram)).then_inc(loaded, 16)

        @block.scalar
        def _(act):
            norm.act(nc, act)

        @block.vector
        def _(dve):
            step = Chain(dve, own)
            dve.wait_ge(loaded, 16)
            step(nc.vector.tensor_tensor(y[:, :, :], x[:, :, :], add[:, :, :], ALU.add))
            norm.dve(nc, dve, step, y, y)


class Affine:

    def __init__(self, nc, hold, tag, x, gain, bias, loads=()):
        self.scale, self.shift = hold.sb("row_scale", [P, NT]), hold.sb("row_shift", [P, NT])
        self.gain, self.bias = hold.sb("gain", [P, 2]), hold.sb("bias", [P, 2])
        with Phase(nc, tag) as ph:
            norm = Norm(ph)
            own, loaded = ph.sem("own"), ph.sem("loaded")
            block = ph.block()

            @block.sync
            def _(sp):
                for dst, a in ((self.gain, gain), (self.bias, bias)):
                    sp.dma_start(dst[:, :], a.rearrange("(c p) -> p c", p=P), allow_slow_non_contiguous=True).then_inc(loaded, 16)
                for dst, a in loads:
                    sp.dma_start(dst, a, allow_slow_non_contiguous=True).then_inc(loaded, 16)
                sp.wait_ge(loaded, 32 + 16 * len(loads))

            @block.scalar
            def _(act):
                norm.act(nc, act)

            @block.vector
            def _(dve):
                norm.scale_and_shift(nc, dve, Chain(dve, own), x, self.scale, self.shift)

    def copy(self, nc, out, x, t):
        return nc.scalar.activation(out, flat_tile(x, t), ACT.Identity, bias=self.shift[:, bass.ds(t, 1)],
                                    scale=self.scale[:, bass.ds(t, 1)])


class Dense:

    def __init__(self, ph, w1, b1, w2, b2):
        FF = w1.shape[1]
        self.w1, self.w2 = ph.sb("w1", [P, 2, FF]), ph.sb("w2", [P, FF // P, C])
        self.b1, self.b2 = ph.sb("b1", [P, FF // P]), ph.sb("b2", [P, C])
        self.loads = [(self.w1[:, :, :], w1.rearrange("(c p) f -> p c f", p=P)),
                      (self.w2[:, :, :], w2.rearrange("(f p) c -> p f c", p=P)),
                      (self.b1[:, :], b1.rearrange("(f p) -> p f", p=P)), (self.b2[:, :], b2.partition_broadcast(P))]


def feed_forward(nc, k, tag, h, affine, dense):
    w1_s, w2_s, b1_s, b2_s = dense.w1, dense.w2, dense.b1, dense.b2
    FS = 4
    F = w2_s.shape[1]
    with Phase(nc, tag) as ph:
        copy = [ph.sb(f"copy{u}", [P, C]) for u in range(FS)]
        turned = [ph.sb(f"turned{u}", [P, 2, P]) for u in range(FS)]
        inner = [ph.sb(f"inner{u}", [P, F, P]) for u in range(FS)]
        turn_p = [ph.ps(f"turn_p{n}", [P, 512]) for n in range(2)]
        up = [ph.ps(f"up{n}", [P, F // 2, P]) for n in range(4)]
        down = [ph.ps(f"down{n}", [P, 512]) for n in range(2)]
        copied, turn, moved, raised, bent, lowered, added, biased = (
            ph.sem(n) for n in ("copied", "turn", "moved", "raised", "bent", "lowered", "added", "biased"))
        block = ph.block()

        def tiles(eng, step):
            def body(i):
                for u in range(FS):
                    step(i * FS + u, u)

            rounds(eng, NT // FS, body)
            for t in range(NT // FS * FS, NT):
                step(t, t % FS)

        def there(t):
            return not isinstance(t, int) or 0 <= t < NT

        @block.scalar
        def _(act):
            def bend(t, u):
                after(act, lowered, t - FS + 1)
                for f in range(F):
                    act.wait_ge(raised, (2 * t + f // (F // 2) + 1))
                    last = nc.scalar.activation(inner[u][:, f, :], up[2 * (u % 2) + f // (F // 2)][:, f % (F // 2), :],
                                                ACT.Gelu, bias=b1_s[:, f:f + 1])
                    if f % (F // 2) == F // 2 - 1:
                        last.then_inc(bent, 1)

            def fetch(t, u):
                after(act, turn, t - FS + 1)
                affine.copy(nc, copy[u][:, :], h, t).then_inc(copied, 1)

            def step(t, u):
                if there(t + 1):
                    fetch(t + 1, (u + 1) % FS)
                bend(t, u)

            fetch(0, 0)
            tiles(act, step)

        @block.tensor
        def _(pe):
            def lower(t, u):
                pe.wait_ge(bent, 2 * t + 2)
                after(pe, added, t - 1)
                for f in range(F):
                    last = nc.tensor.matmul(down[u % 2][:, 0:C], inner[u][:, f, :], w2_s[:, f, :], start=(f == 0), stop=(f == F - 1))
                last.then_inc(lowered, 1)

            def turn_tile(t, u):
                pe.wait_ge(copied, t + 1)
                after(pe, moved, t - 1)
                for c in range(2):
                    last = nc.tensor.transpose(turn_p[u % 2][:, c * P:(c + 1) * P], copy[u][:, c * P:(c + 1) * P], k.ident[:, :])
                last.then_inc(turn, 1)

            def step(t, u):
                if there(t + 1):
                    turn_tile(t + 1, (u + 1) % FS)
                pe.wait_ge(moved, t + 1)
                for half in range(2):
                    after(pe, bent, (t - 2) * 2 + half + 1)
                    for f in range(half * F // 2, (half + 1) * F // 2):
                        for c in range(2):
                            last = nc.tensor.matmul(up[2 * (u % 2) + half][:, f % (F // 2), :], w1_s[:, c, f * P:(f + 1) * P],
                                                    turned[u][:, c, :], start=(c == 0), stop=(c == 1))
                    last.then_inc(raised, 1)
                if there(t - 1):
                    lower(t - 1, (u - 1) % FS)

            turn_tile(0, 0)
            tiles(pe, step)
            lower(NT - 1, (NT - 1) % FS)

        @block.vector
        def _(dve):
            def move_tile(t, u):
                dve.wait_ge(turn, t + 1)
                after(dve, raised, (t - FS + 1) * 2)
                for c in range(2):
                    last = nc.vector.tensor_scalar(turned[u][:, c, :], turn_p[u % 2][:, c * P:(c + 1) * P], affine.gain[:, c:c + 1],
                                                   affine.bias[:, c:c + 1], ALU.mult, ALU.add)
                last.then_inc(moved, 1)

            def add(t, u):
                dve.wait_ge(lowered, t + 1)
                dve.wait_ge(biased, t + 1)
                nc.vector.tensor_tensor(flat_tile(h, t), flat_tile(h, t), down[u % 2][:, 0:C], ALU.add).then_inc(added, 1)

            def step(t, u):
                if there(t + 1):
                    move_tile(t + 1, (u + 1) % FS)
                dve.wait_ge(copied, t + 1)
                nc.vector.tensor_tensor(flat_tile(h, t), flat_tile(h, t), b2_s[:, :], ALU.add).then_inc(biased, 1)
                if there(t - 2):
                    add(t - 2, (u - 2) % FS)

            move_tile(0, 0)
            tiles(dve, step)
            add(NT - 2, (NT - 2) % FS)
            add(NT - 1, (NT - 1) % FS)


def self_attend(nc, tag, acc, v_dram):
    with Phase(nc, tag) as ph:
        v = ph.sb("v", [P, NT, C])
        own, loaded = ph.sem("own"), ph.sem("loaded")
        block = ph.block()

        @block.sync
        def _(sp):
            sp.dma_start(v[:, :, :], node_rows(v_dram)).then_inc(loaded, 16)

        @block.vector
        def _(dve):
            step = Chain(dve, own)
            heads = lambda a: a.rearrange("p t (h d) -> p t h d", h=8)
            z, w = acc[:, :, C:C + 8], acc[:, :, C + 8:C + 16]
            step(nc.vector.tensor_tensor(z, z, w, ALU.add))
            step(nc.vector.tensor_scalar(z, z, 0.5, None, ALU.max))
            step(nc.vector.reciprocal(z, z))
            dve.wait_ge(loaded, 16)
            step(nc.vector.tensor_tensor(heads(v[:, :, :]), heads(v[:, :, :]), w.unsqueeze(3).to_broadcast([P, NT, 8, C // 8]), ALU.mult))
            step(nc.vector.tensor_tensor(acc[:, :, 0:C], acc[:, :, 0:C], v[:, :, :], ALU.add))
            step(nc.vector.tensor_tensor(heads(acc[:, :, 0:C]), heads(acc[:, :, 0:C]), z.unsqueeze(3).to_broadcast([P, NT, 8, C // 8]), ALU.mult))


def move(nc, tag, pairs):
    with Phase(nc, tag) as ph:
        done = ph.sem("done")
        block = ph.block()

        @block.sync
        def _(sp):
            for dst, src in pairs:
                sp.dma_start(dst, src).then_inc(done, 16)
            sp.wait_ge(done, 16 * len(pairs))


def turn_weights(nc, k, w_dram, w):
    with Phase(nc, "w0") as ph:
        rows = ph.sb("rows", [P, 2, C])
        bank = ph.ps("bank", [P, 4, P])
        loaded, turn = ph.sem("loaded"), ph.sem("turn")
        block = ph.block()

        @block.sync
        def _(sp):
            sp.dma_start(rows[:, :, :], w_dram.rearrange("h d c -> d h c")).then_inc(loaded, 16)

        @block.tensor
        def _(pe):
            pe.wait_ge(loaded, 16)
            for c in range(2):
                for h in range(2):
                    last = nc.tensor.transpose(bank[:, 2 * c + h, :], rows[:, h, c * P:(c + 1) * P], k.ident[:, :])
            last.then_inc(turn, 1)

        @block.vector
        def _(dve):
            dve.wait_ge(turn, 1)
            nc.vector.tensor_copy(w[:, :, :].rearrange("p c m -> p (c m)"), bank[:, :, :].rearrange("p a b -> p (a b)"))


def batch_norm_out(nc, k, acc, x, gamma, beta, out):
    with Phase(nc, "bn") as ph:
        norm = Norm(ph)
        g, b = ph.sb("g", [P, C]), ph.sb("b", [P, C])
        mean, scale = ph.sb("node_mean", [P, C]), ph.sb("node_scale", [P, C])
        sq = ph.sb("sq", [P, NT, C])
        col, total = ph.sb("col", [P, C]), ph.ps("total", [P, 2, C])
        pad = ph.sb("pad", [P, 1])
        own, loaded, folded, summed, varied, rooted, ready, stored = (
            ph.sem(n) for n in ("own", "loaded", "folded", "summed", "varied", "rooted", "ready", "stored"))
        block = ph.block()

        @block.sync
        def _(sp):
            sp.dma_start(g[:, :], gamma.partition_broadcast(P)).then_inc(loaded, 16)
            sp.dma_start(b[:, :], beta.partition_broadcast(P)).then_inc(loaded, 16)
            sp.wait_ge(ready, 1)
            full = (NT - 1) * P
            sp.dma_start(out[0:full, :].rearrange("(t p) c -> p t c", p=P), x[:, 0:NT - 1, :]).then_inc(stored, 16)
            sp.dma_start(out[full:N, :], x[0:NL, NT - 1, :]).then_inc(stored, 16)
            sp.wait_ge(stored, 32)

        @block.tensor
        def _(pe):
            for n in range(2):
                pe.wait_ge(folded, n + 1)
                nc.tensor.matmul(total[:, n, :], k.ones[:, :], col[:, :], start=True, stop=True).then_inc(summed, 1)

        @block.scalar
        def _(act):
            act.wait_ge(varied, 1)
            nc.scalar.activation(scale[:, :], scale[:, :], ACT.Sqrt).then_inc(rooted, 1)
            norm.act(nc, act)

        @block.vector
        def _(dve):
            step = Chain(dve, own)
            wide = lambda a: a[:, :].unsqueeze(1).to_broadcast([P, NT, C])
            nc.vector.tensor_reduce(col[:, :], acc[:, :, :].rearrange("p t c -> p c t"), AX.X, ALU.add).then_inc(folded, 1)
            step(nc.vector.tensor_scalar(pad[:, :], k.row[:, :], float(NL), None, ALU.is_lt))
            dve.wait_ge(summed, 1)
            step(nc.vector.tensor_scalar(mean[:, :], total[:, 0, :], 1.0 / N, None, ALU.mult))
            step(nc.vector.tensor_tensor(acc[:, :, :], acc[:, :, :], wide(mean), ALU.subtract))
            step(nc.vector.tensor_scalar(acc[:, NT - 1, :], acc[:, NT - 1, :], pad[:, 0:1], None, ALU.mult))
            step(nc.vector.tensor_tensor(sq[:, :, :], acc[:, :, :], acc[:, :, :], ALU.mult))
            nc.vector.tensor_reduce(col[:, :], sq[:, :, :].rearrange("p t c -> p c t"), AX.X, ALU.add).then_inc(folded, 1)
            dve.wait_ge(summed, 2)
            nc.vector.tensor_scalar(scale[:, :], total[:, 1, :], 1.0 / N, EPS, ALU.mult, ALU.add).then_inc(varied, 1)
            dve.wait_ge(rooted, 1)
            step(nc.vector.reciprocal(scale[:, :], scale[:, :]))
            dve.wait_ge(loaded, 32)
            step(nc.vector.tensor_tensor(scale[:, :], scale[:, :], g[:, :], ALU.mult))
            step(nc.vector.tensor_tensor(acc[:, :, :], acc[:, :, :], wide(scale), ALU.mult))
            step(nc.vector.tensor_tensor(x[:, :, :], x[:, :, :], acc[:, :, :], ALU.add))
            step(nc.vector.tensor_tensor(x[:, :, :], x[:, :, :], wide(b), ALU.add))
            norm.dve(nc, dve, step, x, x)
            nc.vector.memset(pad[:, :], 0.0).then_inc(ready, 1)


def first_layer(nc, k, t, x, scratch, by_src, by_dst, tile_of, tile_row):
    with Phase(nc, "l0") as h:
        rows = scratch("rows0", (NP, C + 2))
        index, local = h.sb("index", [P, STP], i32), h.sb("local", [P, STP])
        s_src = h.sb("s_src", [P, NT, 2])
        acc = h.sb("acc", [P, NT, C + 2])
        with Phase(nc, "p0") as ph:
            w = ph.sb("w", [P, 2, C])
            turn_weights(nc, k, t["L0_gnn_W"], w)

            def extra(ph):
                e = Extra()
                e.a, e.tmp, e.tick = ph.sb("a", [P, 2, C]), ph.sb("tmp", [P, C]), ph.sb("tick", [P, 1])
                a = t["L0_gnn_a"]
                e.loads = [(e.a[:, s, :].rearrange("p (h d) -> p h d", h=2), a[:, s * P:(s + 1) * P].partition_broadcast(P))
                           for s in range(2)]
                return e

            def post(dve, step, tile, out, e):
                fold_heads(nc, step, s_src[:, bass.ds(tile, 1), :].rearrange("p t c -> p (t c)"), out[:, 0:C], e.a[:, 0, :], e.tmp[:, :], 2)
                fold_heads(nc, step, out[:, C:C + 2], out[:, 0:C], e.a[:, 1, :], e.tmp[:, :], 2)

            project(nc, k, "proj0", x, C, w, [(t["L0_gnn_b"].rearrange("h d -> (h d)"), 0, C)], [Sink(rows, 0, C + 2)], "v",
                    C + 2, post, 4, extra, [(by_src, by_src.ROUNDS), (by_dst, 1)])
        load_order(nc, k, "srcload", by_src.table, tile_of, [index], local)
        by_source_pass(nc, k, "edge0", (local, tile_row, index, rows), s_src, acc)
        attend_update(nc, k, "up0", acc, 2, x, 0, None, [(by_dst, 2)])


def build(nc, t, out, scratch):
    Phase.used = []
    with Phase(nc, "all") as hold:
        k = make_constants(nc, hold)
        x_dram = scratch("x_rows", (NP, C))
        tile_of, tile_row = hold.sb("tile_of", [P, STP]), hold.sb("tile_row", [1, STP // U], i32)
        index, rel_index = hold.sb("index", [P, STP], i32), hold.sb("rel_index", [P, STP], i32)
        local = hold.sb("local", [P, STP])
        x = hold.sb("x", [P, NT, C])
        marks = Marks(hold)
        xl, res, al = scratch("xl_rows", (NP, C)), scratch("res_rows", (NP, C)), scratch("al_rows", (NP, 8))
        with Phase(nc, "front") as front:
            src_tile_of, src_tile_row = front.sb("tile_of", [P, STP]), front.sb("tile_row", [1, STP // U], i32)
            by_dst = Scatter(front, "dst", scratch("table_dst", (P * ST, 4), i32))
            by_src = Scatter(front, "src", scratch("table_src", (P * ST, 4), i32))
            sort_edges(nc, k, "src", t["src"], t["dst"], None, None, by_src, src_tile_of, src_tile_row,
                       nodes=(x, t["x"]))
            sort_edges(nc, k, "dst", t["dst"], t["src"], t["edge_type_8"], t["edge_weight"], by_dst, tile_of, tile_row, by_src)
            first_layer(nc, k, t, x, scratch, by_src, by_dst, src_tile_of, src_tile_row)
            with Phase(nc, "l1s") as ph:
                right = ph.sb("right", [P, NT, 8])
                second_rows(nc, k, t, x, right, xl, res, al, by_dst)
                assert by_dst.next == by_src.next == Scatter.ROUNDS
                load_order(nc, k, "dstload", by_dst.table, tile_of, [index, rel_index], local, marks)
                coef = ph.sb("coef", [P, STP, 8])
                with Phase(nc, "l1a") as pa:
                    score = pa.sb("score", [P, ST, 8])
                    alpha_pass(nc, k, "edge1a", (local, tile_row, index, al), right, score)
                    segment_softmax(nc, k, "soft1", marks, score, coef)
                acc = ph.sb("acc", [P, NT, C + 8])
                sum_pass(nc, k, "edge1b", (local, tile_row, index, xl), acc, coef, 8)
                attend_update(nc, k, "up1", acc, 8, x, 1e-16, res)
        move(nc, "keep2", [(node_rows(x_dram), x[:, :, :])])
        third_layer(nc, k, t, x, x_dram, scratch, marks, index, local, tile_row)
        with Phase(nc, "last") as last:
            rel_rows = scratch("rel_rows", (NP * 8, C))
            wide = rel_rows.rearrange("(n r) c -> n (r c)", r=8)
            project(nc, k, "proj3", x, 8 * C, [(t["L3_gnn_weight"][r], r * C, C) for r in range(8)], None,
                    [Sink(wide, 0, 8 * C)], "avav")
            acc = last.sb("acc", [P, NT, C])
            sum_pass(nc, k, "edge3", (local, tile_row, rel_index, rel_rows), acc)
            batch_norm_out(nc, k, acc, x, t["L3_gnn_gamma"], t["L3_gnn_beta"], out)


def second_rows(nc, k, t, x, right, xl, res, al, by_dst):
    def extra(ph):
        e = Extra()
        e.att, e.tmp, e.tick = ph.sb("att", [P, 2, C]), ph.sb("tmp", [P, C]), ph.sb("tick", [P, 1])
        e.loads = [(e.att[:, n, :], t[a].rearrange("a h d -> (a h d)").partition_broadcast(P))
                   for n, a in enumerate(("L1_gnn_att_l", "L1_gnn_att_r"))]
        return e

    def post(dve, step, tile, out, e):
        fold_heads(nc, step, out[:, 2 * C:2 * C + 8], out[:, 0:C], e.att[:, 0, :], e.tmp[:, :], 8)
        fold_heads(nc, step, flat_tile(right, tile), out[:, 0:C], e.att[:, 1, :], e.tmp[:, :], 8)

    project(nc, k, "proj1", x, 2 * C, [(t["L1_gnn_W_lin"], 0, C), (t["L1_gnn_W_res"], C, C)], None,
            [Sink(xl, 0, C), Sink(res, C, C), Sink(al, 2 * C, 8)], "a", 2 * C + 8, post, 4, extra, [(by_dst, by_dst.ROUNDS)])


def third_layer(nc, k, t, h, x_dram, scratch, marks, index, local, tile_row):
    w = lambda name: t["L2_gnn_" + name]
    k_rows, v_rows = (scratch(n, (NP, C)) for n in ("k_rows", "v_rows"))

    def ticker(ph):
        e = Extra()
        e.tmp, e.tick, e.loads = ph.sb("tmp", [P, C]), ph.sb("tick", [P, 1]), []
        return e

    def replace(dve, step, tile, out, e):
        step(nc.vector.tensor_copy(flat_tile(h, tile), out[:, 0:C]))

    def add(dve, step, tile, out, e):
        step(nc.vector.tensor_tensor(flat_tile(h, tile), flat_tile(h, tile), out[:, 0:C], ALU.add))

    project(nc, k, "proj2in", h, C, [(w("w_in"), 0, C)], [(w("b_in"), 0, C)], [], "v", None, replace, 1, ticker)
    for l in range(2):
        with Phase(nc, f"l2_{l}") as layer:
            coef = layer.sb("coef", [P, STP, 16])
            with Phase(nc, f"l2a_{l}") as ph:
                score, self_score = ph.sb("score", [P, ST, 8]), ph.sb("self_score", [P, ST, 8])
                with Phase(nc, f"l2q_{l}") as pq:
                    q = pq.sb("q", [P, NT, C + 8])
                    affine = Affine(nc, pq, f"norm_a{l}", h, w("ln1_g")[l], w("ln1_b")[l])

                    def post(dve, step, tile, out, e):
                        own = flat_tile(q, tile)
                        step(nc.vector.tensor_scalar(own[:, 0:C], out[:, 0:C], 32 ** -0.5, None, ALU.mult))
                        fold_heads(nc, step, own[:, C:C + 8], own[:, 0:C], out[:, C:2 * C], e.tmp[:, :], 8)

                    project(nc, k, f"proj2_{l}", h, 3 * C, [(w(n)[l], c * C, C) for c, n in enumerate(("wq", "wk", "wv"))],
                            [(w(n)[l], c * C, C) for c, n in enumerate(("bq", "bk", "bv"))],
                            [Sink(k_rows, C, C), Sink(v_rows, 2 * C, C)], "vv", None, post, 3, ticker, affine=affine)
                    score_pass(nc, k, f"edge2a_{l}", (local, tile_row, index, k_rows), q, score, self_score)
                segment_softmax(nc, k, f"soft2_{l}", marks, score, coef, self_score)
            with Phase(nc, f"l2b_{l}") as ph:
                acc = ph.sb("acc", [P, NT, C + 16])
                sum_pass(nc, k, f"edge2b_{l}", (local, tile_row, index, v_rows), acc, coef, 8, 8)
                self_attend(nc, f"self_{l}", acc, v_rows)
                project(nc, k, f"proj2o_{l}", acc[:, :, 0:C], C, [(w("wo")[l], 0, C)], [(w("bo")[l], 0, C)],
                        [], "v", None, add, 1, ticker)
            with Phase(nc, f"l2f_{l}") as ph:
                dense = Dense(ph, w("w1")[l], w("b1")[l], w("w2")[l], w("b2")[l])
                affine = Affine(nc, ph, f"norm_b{l}", h, w("ln2_g")[l], w("ln2_b")[l], dense.loads)
                feed_forward(nc, k, f"ffn_{l}", h, affine, dense)
    with Phase(nc, "l2out") as ph:
        before = ph.sb("before", [P, NT, C])
        norm_into(nc, "norm3", h, h, add=before, add_dram=x_dram)


def kernel(**inputs):
    import numpy as _np
    import concourse.bacc as _bacc
    from concourse import mybir as _mybir
    from concourse.bass_utils import run_bass_kernel_spmd as _run

    nc = _bacc.Bacc("TRN2", target_bir_lowering=False, num_devices=1)
    arrays, aps = {}, {}
    for name, value in inputs.items():
        a = _np.ascontiguousarray(value)
        arrays[f"in_{name}"] = a
        aps[name] = nc.dram_tensor(f"in_{name}", a.shape, _mybir.dt.from_np(a.dtype), kind="ExternalInput").ap()
    out = nc.dram_tensor("out", (N, C), _mybir.dt.float32, kind="ExternalOutput").ap()

    def scratch(name, shape, dt=_mybir.dt.float32):
        return nc.dram_tensor(name, shape, dt, kind="Internal").ap()

    build(nc, aps, out, scratch)
    r = _run(nc, [arrays], core_ids=[0])
    return r.results[0]["out"]
```
